# Optimizing a Trainium2 kernel written in Bass

```python
import numpy as np
import jax
import jax.numpy as jnp

def _softmax(x, axis=-1):
    return jax.nn.softmax(x, axis=axis)

def _gelu(x):
    return jax.nn.gelu(x, approximate=True)

def _silu(x):
    return jax.nn.silu(x)

def _sigmoid(x):
    return jax.nn.sigmoid(x)

def _layernorm(x, axis=-1, eps=1e-05):
    m = jnp.mean(x, axis=axis, keepdims=True)
    v = jnp.var(x, axis=axis, keepdims=True)
    return (x - m) / jnp.sqrt(v + eps)

def _scatter_add(tgt, idx, src, axis=0):
    return tgt.at[idx].add(src)

def _segment_sum(src, seg, n):
    return jax.ops.segment_sum(src, seg, n)
kernel_name = 'mk_gnn_resnorm_d2_gnn_r8_85f5bb'

def setup_inputs(seed: int=0):
    np.random.seed(seed)
    _w = jnp.asarray

    def _rec_inputs():
        import jax
        import jax.numpy as jnp
        _gk = jax.random.key(seed)
        x = -0.0001006 + 1 * jax.random.normal(jax.random.fold_in(_gk, 1), (6250, 96), jnp.float32)
        _s = jax.random.randint(jax.random.fold_in(_gk, 2), (50000,), 0, 6250, jnp.int32)
        _d = jax.random.randint(jax.random.fold_in(_gk, 3), (50000,), 0, 6250, jnp.int32)
        _loop = jnp.arange(6250, dtype=jnp.int32)
        src = jnp.concatenate([_s, _d, _loop])
        dst = jnp.concatenate([_d, _s, _loop])
        _o = jnp.argsort(dst, stable=True)
        src = src[_o]
        dst = dst[_o]
        edge_attr_96 = 5.93493e-05 + 1.00006 * jax.random.normal(jax.random.fold_in(_gk, 11), (106250, 96), jnp.float32)
        return (x, src, dst, edge_attr_96)
    x, src, dst, edge_attr_96 = _rec_inputs()

    def _L0_gnn_setup():
        import jax, jax.numpy as jnp
        import numpy as np
        N = 6250
        E = 100000
        DIM = 96
        HEADS = 4
        HEAD_DIM = DIM // HEADS
        SLOPE = 0.2
        EPS = 1e-05

        def _gat_layer(x, edge_index, W, att_src, att_dst, gat_bias, proj_W, proj_b, ln_g, ln_b):
            loop = jnp.arange(N, dtype=edge_index.dtype)
            src = jnp.concatenate([edge_index[0], loop])
            dst = jnp.concatenate([edge_index[1], loop])
            h = (x @ W).reshape(N, HEADS, HEAD_DIM)
            a_src = jnp.einsum('nhd,hd->nh', h, att_src)
            a_dst = jnp.einsum('nhd,hd->nh', h, att_dst)
            e = jax.nn.leaky_relu(a_src[src] + a_dst[dst], SLOPE)
            m = jax.ops.segment_max(e, dst, num_segments=N)
            e = jnp.exp(e - m[dst])
            denom = jax.ops.segment_sum(e, dst, num_segments=N)
            alpha = e / denom[dst]
            out = jax.ops.segment_sum(alpha[:, :, None] * h[src], dst, num_segments=N)
            out = out.reshape(N, HEADS * HEAD_DIM) + gat_bias
            proj = out @ proj_W.T + proj_b
            z = x + proj
            mu = jnp.mean(z, axis=-1, keepdims=True)
            var = jnp.mean((z - mu) ** 2, axis=-1, keepdims=True)
            return ln_g * (z - mu) / jnp.sqrt(var + EPS) + ln_b
        key = jax.random.key(seed)
        ks = jax.random.split(key, 10)
        s = 0.1
        return {'x': jax.random.normal(ks[0], (N, DIM), jnp.float32), 'edge_index': jax.random.randint(ks[1], (2, E), 0, N, dtype=jnp.int64), 'W': jax.random.normal(ks[2], (DIM, HEADS * HEAD_DIM), jnp.float32) * s, 'att_src': jax.random.normal(ks[3], (HEADS, HEAD_DIM), jnp.float32) * s, 'att_dst': jax.random.normal(ks[4], (HEADS, HEAD_DIM), jnp.float32) * s, 'gat_bias': jnp.zeros((DIM,), jnp.float32), 'proj_W': jax.random.normal(ks[5], (DIM, DIM), jnp.float32) * s, 'proj_b': jnp.zeros((DIM,), jnp.float32), 'ln_g': jnp.ones((DIM,), jnp.float32), 'ln_b': jnp.zeros((DIM,), jnp.float32)}
    _L0_gnn_all = _L0_gnn_setup()
    _L0_gnn_in = {k: v for k, v in _L0_gnn_all.items() if k in ('W', 'att_src', 'att_dst', 'gat_bias', 'proj_W', 'proj_b', 'ln_g', 'ln_b')}
    del _L0_gnn_all

    def _L1_gnn_setup():
        import jax, jax.numpy as jnp
        import numpy as np
        N_NODES = 6250
        N_EDGES = 100000
        IN_DIM = 96
        NUM_HEADS = 8
        HEAD_DIM = IN_DIM // NUM_HEADS
        key = jax.random.key(seed)
        ks = jax.random.split(key, 11)
        s = 1.0 / np.sqrt(IN_DIM)
        return {'x': jax.random.normal(ks[0], (N_NODES, IN_DIM), dtype=jnp.float32), 'edge_index': jax.random.randint(ks[1], (2, N_EDGES), 0, N_NODES, dtype=jnp.int64), 'edge_attr': jax.random.normal(ks[2], (N_EDGES, IN_DIM), dtype=jnp.float32), 'Wq': jax.random.normal(ks[3], (IN_DIM, IN_DIM), dtype=jnp.float32) * s, 'bq': jax.random.normal(ks[4], (IN_DIM,), dtype=jnp.float32) * s, 'Wk': jax.random.normal(ks[5], (IN_DIM, IN_DIM), dtype=jnp.float32) * s, 'bk': jax.random.normal(ks[6], (IN_DIM,), dtype=jnp.float32) * s, 'We': jax.random.normal(ks[7], (IN_DIM, IN_DIM), dtype=jnp.float32) * s, 'be': jax.random.normal(ks[8], (IN_DIM,), dtype=jnp.float32) * s, 'Wv': jax.random.normal(ks[9], (IN_DIM, IN_DIM), dtype=jnp.float32) * s, 'bv': jax.random.normal(ks[10], (IN_DIM,), dtype=jnp.float32) * s}
    _L1_gnn_all = _L1_gnn_setup()
    _L1_gnn_in = {k: v for k, v in _L1_gnn_all.items() if k in ('Wq', 'bq', 'Wk', 'bk', 'We', 'be', 'Wv', 'bv')}
    del _L1_gnn_all
    return {'x': x, 'src': src, 'dst': dst, 'edge_attr_96': edge_attr_96, 'L0_gnn_W': _L0_gnn_in['W'], 'L0_gnn_att_src': _L0_gnn_in['att_src'], 'L0_gnn_att_dst': _L0_gnn_in['att_dst'], 'L0_gnn_gat_bias': _L0_gnn_in['gat_bias'], 'L0_gnn_proj_W': _L0_gnn_in['proj_W'], 'L0_gnn_proj_b': _L0_gnn_in['proj_b'], 'L0_gnn_ln_g': _L0_gnn_in['ln_g'], 'L0_gnn_ln_b': _L0_gnn_in['ln_b'], 'L1_gnn_Wq': _L1_gnn_in['Wq'], 'L1_gnn_bq': _L1_gnn_in['bq'], 'L1_gnn_Wk': _L1_gnn_in['Wk'], 'L1_gnn_bk': _L1_gnn_in['bk'], 'L1_gnn_We': _L1_gnn_in['We'], 'L1_gnn_be': _L1_gnn_in['be'], 'L1_gnn_Wv': _L1_gnn_in['Wv'], 'L1_gnn_bv': _L1_gnn_in['bv']}

def reference(x, src, dst, edge_attr_96, L0_gnn_W, L0_gnn_att_src, L0_gnn_att_dst, L0_gnn_gat_bias, L0_gnn_proj_W, L0_gnn_proj_b, L0_gnn_ln_g, L0_gnn_ln_b, L1_gnn_Wq, L1_gnn_bq, L1_gnn_Wk, L1_gnn_bk, L1_gnn_We, L1_gnn_be, L1_gnn_Wv, L1_gnn_bv):
    import jax
    import jax.numpy as jnp

    def _L0_gnn_ref(x, edge_index, W, att_src, att_dst, gat_bias, proj_W, proj_b, ln_g, ln_b):
        import jax, jax.numpy as jnp
        import numpy as np
        N = 6250
        E = 100000
        DIM = 96
        HEADS = 4
        HEAD_DIM = DIM // HEADS
        SLOPE = 0.2
        EPS = 1e-05

        def _gat_layer(x, edge_index, W, att_src, att_dst, gat_bias, proj_W, proj_b, ln_g, ln_b):
            loop = jnp.arange(N, dtype=edge_index.dtype)
            src = jnp.concatenate([edge_index[0], loop])
            dst = jnp.concatenate([edge_index[1], loop])
            h = (x @ W).reshape(N, HEADS, HEAD_DIM)
            a_src = jnp.einsum('nhd,hd->nh', h, att_src)
            a_dst = jnp.einsum('nhd,hd->nh', h, att_dst)
            e = jax.nn.leaky_relu(a_src[src] + a_dst[dst], SLOPE)
            m = jax.ops.segment_max(e, dst, num_segments=N)
            e = jnp.exp(e - m[dst])
            denom = jax.ops.segment_sum(e, dst, num_segments=N)
            alpha = e / denom[dst]
            out = jax.ops.segment_sum(alpha[:, :, None] * h[src], dst, num_segments=N)
            out = out.reshape(N, HEADS * HEAD_DIM) + gat_bias
            proj = out @ proj_W.T + proj_b
            z = x + proj
            mu = jnp.mean(z, axis=-1, keepdims=True)
            var = jnp.mean((z - mu) ** 2, axis=-1, keepdims=True)
            return ln_g * (z - mu) / jnp.sqrt(var + EPS) + ln_b
        return _gat_layer(x, edge_index, W, att_src, att_dst, gat_bias, proj_W, proj_b, ln_g, ln_b)

    def _L1_gnn_ref(x, edge_index, edge_attr, Wq, bq, Wk, bk, We, be, Wv, bv):
        import jax, jax.numpy as jnp
        import numpy as np
        N_NODES = 6250
        N_EDGES = 100000
        IN_DIM = 96
        NUM_HEADS = 8
        HEAD_DIM = IN_DIM // NUM_HEADS
        N = x.shape[0]
        H, D = (NUM_HEADS, HEAD_DIM)
        Q_h = (x @ Wq + bq).reshape(N, H, D)
        K_h = (x @ Wk + bk).reshape(N, H, D)
        V_h = (x @ Wv + bv).reshape(N, H, D)
        E = (edge_attr @ We + be).reshape(-1, H, D)
        src_idx = edge_index[0]
        dst_idx = edge_index[1]
        src = K_h[src_idx]
        dest = Q_h[dst_idx]
        score = src * dest / jnp.sqrt(jnp.asarray(D, x.dtype))
        score = score * E
        score = jnp.exp(jnp.clip(score.sum(-1, keepdims=True), -5.0, 5.0))
        msg = V_h[src_idx] * score
        wV = jax.ops.segment_sum(msg, dst_idx, num_segments=N)
        Z = jax.ops.segment_sum(score, dst_idx, num_segments=N)
        h_out = wV / (Z + 1e-06)
        return h_out.reshape(N, H * D)
    edge_index = jnp.stack([src, dst])
    x = _layernorm(x + _L0_gnn_ref(x, edge_index, L0_gnn_W, L0_gnn_att_src, L0_gnn_att_dst, L0_gnn_gat_bias, L0_gnn_proj_W, L0_gnn_proj_b, L0_gnn_ln_g, L0_gnn_ln_b), axis=-1)
    x = _layernorm(x + _L1_gnn_ref(x, edge_index, edge_attr_96, L1_gnn_Wq, L1_gnn_bq, L1_gnn_Wk, L1_gnn_bk, L1_gnn_We, L1_gnn_be, L1_gnn_Wv, L1_gnn_bv), axis=-1)
    return x

_drawn_inputs = setup_inputs


def setup_inputs(seed=0):
    import zlib

    import numpy as np

    out = dict(_drawn_inputs(seed))
    spreads = {'L0_gnn_gat_bias': (0.0, 0.1),
     'L0_gnn_proj_b': (0.0, 0.1),
     'L0_gnn_ln_g': (1.0, 0.2),
     'L0_gnn_ln_b': (0.0, 0.1)}
    factors = {}
    for name, (base, spread) in spreads.items():
        noise = np.random.default_rng([zlib.crc32(name.encode()), seed]).standard_normal(out[name].shape)
        drawn = base * np.exp(spread * noise) if base else spread * noise
        out[name] = jnp.asarray(drawn.astype(out[name].dtype))
    for name, factor in factors.items():
        out[name] = (out[name] * factor).astype(out[name].dtype)
    return out
```

```python
from contextlib import ExitStack

import concourse.bass as bass
import numpy as np
from concourse import mybir


class Bag:
    pass


F32 = mybir.dt.float32
BF16 = mybir.dt.bfloat16
I32 = mybir.dt.int32
ALU = mybir.AluOpType
ACT = mybir.ActivationFunctionType
AX_X = mybir.AxisListType.X
RMAX = bass.bass_isa.ReduceOp.max

P = 128
D = 96
H0, D0 = 4, 24
H1, D1 = 8, 12
SLOPE, EPS = 0.2, 1e-5
ROW0 = D + 2 * H0
GAT0 = D + H0
ACC0 = D + H0
ACC1 = D + H1
QUAD = 4
RING = 4
PAR = 2
GRP = 7
SHIFT = 8192.0
BIG = 3e38
SPREAD_MAX = 60.0
LAST_DST = 1 << 20


def sizes(n_nodes, n_edges):
    z = Bag()
    z.N, z.E = n_nodes, n_edges
    z.NB = -(-n_nodes // (P * GRP)) * GRP
    z.FULL = n_nodes // P
    z.REST = n_nodes - z.FULL * P
    z.NG = z.NB // GRP
    z.T = -(-n_edges // P)
    z.TAIL = n_edges - (z.T - 1) * P
    z.KC = -(-z.T // P)
    body = QUAD * RING
    z.NIT = -(-(z.T + z.NB - 1) // body)
    z.NQ = z.NIT * RING
    z.STEPS = z.NIT * body
    z.BROWS = z.STEPS - z.T + 2
    assert z.BROWS >= z.NB and z.NIT >= 3
    return z


def constants(z):
    part = np.arange(P, dtype=np.float32)[:, None]
    tile = part + P * np.arange(z.KC, dtype=np.float32)[None, :]
    heads = (np.arange(P)[:, None] // D0 == np.arange(H0)[None, :]).astype(np.float32)
    cols = [
        np.eye(P, dtype=np.float32),
        np.tile(np.arange(P, dtype=np.float32)[None, :], (P, 1)),
        tile,
        (tile > 0).astype(np.float32),
        heads,
        part + P * np.arange(z.NB, dtype=np.float32)[None, :],
    ]
    at, where = 0, []
    for c in cols:
        where.append((at, at + c.shape[1]))
        at += c.shape[1]
    steps = np.tile(np.arange(z.STEPS, dtype=np.float32)[None, :], (P, 1))
    tail = np.full((1, P + 1), -1, np.int32)
    tail[0, P] = LAST_DST
    return np.ascontiguousarray(np.concatenate(cols, 1)), where, steps, tail


def over(ap, n):
    return ap.unsqueeze(len(ap.shape)).to_broadcast([*ap.shape, n])


def across(ap, n):
    return ap.unsqueeze(1).to_broadcast([ap.shape[0], n, ap.shape[1]])


def load_phase(nc, z, d, s, where):
    with ExitStack() as ctx:
        sb = lambda n, sh, dt=F32: ctx.enter_context(nc.sbuf_tensor(n, sh, dt))
        sem = lambda n: ctx.enter_context(nc.semaphore(n))
        w_raw = sb("w_raw", [D, D])
        pw_raw = sb("pw_raw", [D, D])
        att = sb("att", [D, 2])
        attm = sb("attm", [D, 2, H0])
        gbias = sb("gbias", [D, 1])
        pbias = sb("pbias", [1, D])
        bias2 = sb("bias2", [1, D])
        w_t = sb("w_t", [D, D])
        dst_i = sb("dst_i", [P, z.KC, P + 1], I32)
        src_i = sb("src_i", [P, z.KC, P], I32)
        first_i = sb("first_i", [P, z.KC], I32)
        later_i = sb("later_i", [P, z.KC], I32)
        down = sb("down", [P, z.KC, P])
        down_max = sb("down_max", [P, 1])
        ps_w = ctx.enter_context(nc.psum_tensor("ps_w", [P, 512], F32))
        ps_p = ctx.enter_context(nc.psum_tensor("ps_p", [P, 512], F32))
        ps_a = ctx.enter_context(nc.psum_tensor("ps_a", [P, 512], F32))
        ps_b = ctx.enter_context(nc.psum_tensor("ps_b", [P, 512], F32))

        cleared = sem("cleared")
        x_loaded, x_cleared = sem("x_loaded"), sem("x_cleared")
        par_loaded = sem("par_loaded")
        par_more = sem("par_more")
        edges_loaded = sem("edges_loaded")
        tail_loaded = sem("tail_loaded")
        w_turned, w_copied = sem("w_turned"), sem("w_copied")
        p_turned, p_copied = sem("p_turned"), sem("p_copied")
        att_made, comp_done = sem("att_made"), sem("comp_done")
        bias_done, bias_made, bias_put = sem("bias_done"), sem("bias_made"), sem("bias_put")
        dve_step = sem("dve_step")
        viol_in, viol_out = sem("viol_in"), sem("viol_out")

        ra = z.T - 1
        lp, lk = ra % P, ra // P
        N_PAR, N_MORE, N_EDGE = 8, 11, 0

        with nc.Block(no_gpsimd_drain=True) as block:

            @block.gpsimd
            def _(pool):
                pool.memset(s.x_sb[:, z.FULL:z.NB, :], 0.0).then_inc(x_cleared, 1)
                pool.memset(dst_i[:, :, :], 0).then_inc(cleared, 1)
                pool.memset(src_i[:, :, :], 0).then_inc(cleared, 1)
                pool.memset(first_i[:, :], 0).then_inc(cleared, 1)
                pool.wait_ge(viol_in, 1)
                pool.partition_all_reduce(s.viol[:, :], down_max[:, :], P, RMAX).then_inc(viol_out, 1)

            @block.sync
            def _(sp):
                sp.dma_start(w_raw[:, :], d.W).then_inc(par_loaded, 16)
                sp.dma_start(s.cst[:, :], d.cst).then_inc(par_loaded, 16)
                sp.dma_start(att[:, 0:1], d.att_src.rearrange("h (e o) -> (h e) o", o=1)).then_inc(par_loaded, 16)
                sp.dma_start(att[:, 1:2], d.att_dst.rearrange("h (e o) -> (h e) o", o=1)).then_inc(par_loaded, 16)
                sp.dma_start(pw_raw[:, :], d.proj_W).then_inc(par_loaded, 16)
                sp.dma_start(gbias[:, :], d.gat_bias.rearrange("(e o) -> e o", o=1)).then_inc(par_loaded, 16)
                sp.dma_start(pbias[:, :], d.proj_b.rearrange("(o e) -> o e", o=1)).then_inc(par_loaded, 16)
                sp.dma_start(s.steps[:, :], d.steps).then_inc(par_loaded, 16)
                sp.wait_ge(x_cleared, 1)
                sp.dma_start(s.x_sb[:, 0:z.FULL, :],
                             d.x[0:z.FULL * P, :].rearrange("(b p) e -> p b e", p=P)).then_inc(x_loaded, 16)
                if z.REST:
                    sp.dma_start(s.x_sb[0:z.REST, z.FULL, :], d.x[z.FULL * P:z.N, :]).then_inc(x_loaded, 16)
                row = lambda v: v.rearrange("(o e) -> o e", o=1)
                for n, (w, b) in enumerate(((d.Wk, d.bk), (d.Wv, d.bv), (d.Wq, d.bq))):
                    sp.dma_start(s.w_kvq[0:D, n * D:(n + 1) * D], w).then_inc(par_more, 16)
                    sp.dma_start(s.w_kvq[D:D + 1, n * D:(n + 1) * D], row(b)).then_inc(par_more, 16)
                sp.dma_start(s.w_e[0:D, :], d.We).then_inc(par_more, 16)
                sp.dma_start(s.w_e[D:D + 1, :], row(d.be)).then_inc(par_more, 16)
                sp.dma_start(s.ln_g[:, :], row(d.ln_g).to_broadcast([P, D])).then_inc(par_more, 16)
                sp.dma_start(s.ln_b[:, :], row(d.ln_b).to_broadcast([P, D])).then_inc(par_more, 16)
                sp.wait_ge(bias_made, 1)
                sp.dma_start(s.w_proj[D:D + 1, :], bias2[:, :]).then_inc(par_more, 16)
                sp.wait_ge(x_loaded, 16 * (1 + bool(z.REST)))
                sp.wait_ge(par_more, 16 * N_MORE)

            @block.scalar
            def _(act):
                act.wait_ge(cleared, 3)
                n_loads = 0
                for k in range(z.KC):
                    n = min(P, ra - k * P)
                    if n <= 0:
                        break
                    at = k * P * P
                    act.dma_start(dst_i[0:n, k, 0:P], d.dst[at:at + n * P].rearrange("(t e) -> t e", e=P)).then_inc(edges_loaded, 16)
                    act.dma_start(dst_i[0:n, k, P:P + 1],
                                  d.dst[at + P:at + n * P + 1:P].rearrange("(t e) -> t e", e=1),
                                  allow_slow_non_contiguous=True).then_inc(edges_loaded, 16)
                    act.dma_start(src_i[0:n, k, :], d.src[at:at + n * P].rearrange("(t e) -> t e", e=P)).then_inc(edges_loaded, 16)
                    act.dma_start(first_i[0:n, k:k + 1],
                                  d.dst[at:at + (n - 1) * P + 1:P].rearrange("(t e) -> t e", e=1),
                                  allow_slow_non_contiguous=True).then_inc(edges_loaded, 16)
                    n_loads += 4
                act.dma_start(dst_i[lp:lp + 1, lk, :], d.tail).then_inc(tail_loaded, 16)
                act.wait_ge(tail_loaded, 16)
                act.dma_start(dst_i[lp:lp + 1, lk, P - z.TAIL:P],
                              d.dst[z.E - z.TAIL:z.E].rearrange("(o e) -> o e", o=1)).then_inc(edges_loaded, 16)
                act.dma_start(src_i[lp:lp + 1, lk, :],
                              d.src[z.E - P:z.E].rearrange("(o e) -> o e", o=1)).then_inc(edges_loaded, 16)
                act.dma_start(first_i[lp:lp + 1, lk:lk + 1],
                              d.dst[z.E - z.TAIL:z.E - z.TAIL + 1].rearrange("(o e) -> o e", o=1)).then_inc(edges_loaded, 16)
                act.wait_ge(edges_loaded, 16 * (n_loads + 3))
                act.wait_ge(w_turned, 1)
                act.activation(w_t[:, :], ps_w[0:D, 0:D], ACT.Copy).then_inc(w_copied, 1)
                act.wait_ge(p_turned, 1)
                act.activation(s.w_proj[0:D, :], ps_p[0:D, 0:D], ACT.Copy).then_inc(p_copied, 1)

            @block.tensor
            def _(pe):
                pe.wait_ge(par_loaded, 16 * N_PAR)
                pe.transpose(ps_w[0:D, 0:D], w_raw[:, :], s.ident[0:D, 0:D]).then_inc(w_turned, 1)
                pe.transpose(ps_p[0:D, 0:D], pw_raw[:, :], s.ident[0:D, 0:D]).then_inc(p_turned, 1)
                pe.wait_ge(w_copied, 1)
                pe.wait_ge(att_made, 2)
                pe.matmul(ps_a[0:D, 0:2 * H0], w_t[:, :], attm[:, :, :].rearrange("p a h -> p (a h)"),
                          start=True, stop=True).then_inc(comp_done, 1)
                pe.wait_ge(p_copied, 1)
                pe.matmul(ps_b[0:1, 0:D], gbias[:, :], s.w_proj[0:D, :], start=True, stop=True).then_inc(bias_done, 1)

            @block.vector
            def _(dve):
                dve.memset(s.x_t1[:, :, :], 1.0).then_inc(dve_step, 1)
                dve.memset(s.attr_t1[:, :, :], 1.0).then_inc(dve_step, 1)
                dve.wait_ge(par_loaded, 16 * N_PAR)
                dve.tensor_copy(s.w_x[:, 0:D], w_raw[:, :]).then_inc(dve_step, 1)
                for a in range(2):
                    dve.tensor_scalar(attm[:, a, :], s.heads[0:D, :], att[:, a:a + 1], None, ALU.mult).then_inc(att_made, 1)
                dve.wait_ge(edges_loaded, 16 * (4 * (-(-ra // P)) + 3))
                dve.tensor_tensor(down[:, :, :], dst_i[:, :, 0:P], dst_i[:, :, 1:P + 1], ALU.is_gt).then_inc(dve_step, 1)
                dve.wait_ge(dve_step, 4)
                dve.tensor_reduce(down_max[:, :], down[:, :, :].rearrange("p k e -> p (k e)"), AX_X, ALU.max).then_inc(viol_in, 1)
                dve.tensor_scalar(s.dst_f[:, :, :], dst_i[:, :, 0:P], SHIFT, None, ALU.add).then_inc(dve_step, 1)
                dve.tensor_copy(s.src_f[:, :, :], src_i[:, :, :]).then_inc(dve_step, 1)
                dve.tensor_copy(later_i[:, :], dst_i[:, :, P]).then_inc(dve_step, 1)
                dve.wait_ge(dve_step, 7)
                dve.tensor_scalar(first_i[:, :], first_i[:, :], 7, None, ALU.arith_shift_right).then_inc(dve_step, 1)
                dve.tensor_scalar(later_i[:, :], later_i[:, :], 7, None, ALU.arith_shift_right).then_inc(dve_step, 1)
                dve.wait_ge(dve_step, 9)
                dve.tensor_copy(s.lo[:, :], first_i[:, :]).then_inc(dve_step, 1)
                dve.tensor_copy(s.hi[:, :], later_i[:, :]).then_inc(dve_step, 1)
                dve.wait_ge(comp_done, 1)
                dve.tensor_copy(s.w_x[:, D:ROW0], ps_a[0:D, 0:2 * H0]).then_inc(dve_step, 1)
                dve.wait_ge(bias_done, 1)
                dve.tensor_tensor(bias2[:, :], ps_b[0:1, 0:D], pbias[:, :], ALU.add).then_inc(bias_made, 1)
                dve.wait_ge(viol_out, 1)
                dve.tensor_scalar(s.is_sorted[:, :], s.viol[:, :], -1.0, 1.0, ALU.mult, ALU.add).then_inc(dve_step, 1)
                dve.tensor_scalar(s.passes[:, :], s.viol[:, :], float(z.NB - 1), 1.0, ALU.mult, ALU.add).then_inc(dve_step, 1)
                dve.wait_ge(dve_step, 14)
                dve.tensor_scalar(s.lo[:, :], s.lo[:, :], s.is_sorted[:, 0:1], None, ALU.mult).then_inc(dve_step, 1)
                dve.tensor_scalar(s.hi[:, :], s.hi[:, :], s.is_sorted[:, 0:1], 1.0, ALU.mult, ALU.add).then_inc(dve_step, 1)
                dve.wait_ge(dve_step, 16)
                dve.tensor_tensor(s.lo[:, :], s.lo[:, :], s.tile_no[:, :], ALU.add).then_inc(dve_step, 1)
                dve.tensor_tensor(s.hi[:, :], s.hi[:, :], s.tile_no[:, :], ALU.add).then_inc(dve_step, 1)
                dve.wait_ge(dve_step, 18)
                dve.tensor_tensor(s.lo[:, :], s.lo[:, :], s.not_first[:, :], ALU.mult).then_inc(dve_step, 1)
                dve.wait_ge(dve_step, 19)


def table_phase(nc, z, d, s):
    with ExitStack() as ctx:
        sb = lambda n, sh, dt=F32: ctx.enter_context(nc.sbuf_tensor(n, sh, dt))
        ps = lambda n: ctx.enter_context(nc.psum_tensor(n, [P, 1024], F32))
        sem = lambda n: ctx.enter_context(nc.semaphore(n))
        x_g = sb("x_g", [P, GRP, D])
        pick = sb("pick", [P, z.KC, z.STEPS])
        row_t = sb("row_t", [1, z.STEPS])
        row_b = s.block_f
        row_e = sb("row_e", [1, z.STEPS])
        neg_p = sb("neg_p", [1, P])
        ext = sb("ext", [P, 2 * H0])
        ext_all = sb("ext_all", [P, 2 * H0])
        spread = sb("spread", [P, H0])
        wide = sb("wide", [P, 2])
        ps_x, ps_h, ps_s, ps_r = ps("ps_x"), ps("ps_h"), ps("ps_s"), ps("ps_r")
        HALF = -(-z.STEPS // 2)
        halves = [(0, HALF), (HALF, z.STEPS - HALF)]
        KL = z.T - (z.KC - 1) * P

        x_copied, x_turned, xt_copied = sem("x_copied"), sem("x_turned"), sem("xt_copied")
        h_done, h_copied, t0_stored = sem("h_done"), sem("h_copied"), sem("t0_stored")
        pick_step, pick_done = sem("pick_step"), sem("pick_done")
        row_done, row_copied, row_step, rel_done, src_done = sem("row_done"), sem("row_copied"), sem("row_step"), sem("rel_done"), sem("src_done")
        srcs_copied, rels_copied = sem("srcs_copied"), sem("rels_copied")
        neg_set, ext_step, ext_in, ext_out = sem("neg_set"), sem("ext_step"), sem("ext_in"), sem("ext_out")
        t0_rows = d.T0.rearrange("(b p) c -> p b c", p=P)

        with nc.Block(no_gpsimd_drain=True) as block:

            @block.sync
            def _(sp):
                with sp.Fori(0, z.NG) as g:
                    sp.wait_ge(h_copied, g + 2)
                    sp.dma_start(t0_rows[:, bass.ds(g * GRP, GRP), :],
                                 s.tab0[:, bass.ds(g * GRP, GRP), 0:GAT0]).then_inc(t0_stored, 16)
                sp.wait_ge(t0_stored, 16 * z.NG)

            @block.scalar
            def _(act):
                act.sem_inc(xt_copied, 1)
                with act.Fori(0, z.NG) as g:
                    act.wait_ge(x_turned, g + 2)
                    act.wait_ge(h_done, g + 1)
                    act.activation(s.x_t[0:D, 0:4 * P], ps_x[0:D, 0:4 * P], ACT.Copy)
                    act.activation(s.x_t[0:D, 4 * P:GRP * P], ps_x[0:D, 4 * P:GRP * P], ACT.Copy).then_inc(xt_copied, 1)
                for n, (at, w) in enumerate(halves):
                    act.wait_ge(src_done, n + 1)
                    act.activation(s.src_idx[:, at:at + w], ps_s[:, 512 * n:512 * n + w], ACT.Copy).then_inc(srcs_copied, 1)
                act.wait_ge(srcs_copied, 2)

            @block.tensor
            def _(pe):
                pe.sem_inc(x_turned, 1)
                pe.sem_inc(h_done, 1)
                with pe.Fori(0, z.NG) as g:
                    pe.wait_ge(x_copied, g + 1)
                    pe.wait_ge(xt_copied, g + 1)
                    for j in range(GRP):
                        last = pe.transpose(ps_x[0:D, j * P:(j + 1) * P], x_g[:, j, :], s.ident[:, :])
                    last.then_inc(x_turned, 1)
                    pe.wait_ge(xt_copied, g + 2)
                    pe.wait_ge(h_copied, g + 1)
                    for j in range(GRP):
                        last = pe.matmul(ps_h[:, j * P:j * P + ROW0], s.x_t[0:D, j * P:(j + 1) * P], s.w_x[:, :],
                                         start=True, stop=True)
                    last.then_inc(h_done, 1)
                rows = [P] * (z.KC - 1) + [KL]
                for n, (at, w) in enumerate(halves):
                    for k in range(z.KC):
                        pe.wait_ge(pick_done, k + 1)
                        last = pe.matmul(ps_r[0:1, 512 * n:512 * n + w], s.tile_no[0:rows[k], k:k + 1],
                                         pick[0:rows[k], k, at:at + w], start=(k == 0), stop=(k == z.KC - 1))
                    last.then_inc(row_done, 1)
                for n, (at, w) in enumerate(halves):
                    for k in range(z.KC):
                        last = pe.matmul(ps_s[:, 512 * n:512 * n + w], s.src_f[0:rows[k], k, :],
                                         pick[0:rows[k], k, at:at + w], start=(k == 0), stop=(k == z.KC - 1))
                    last.then_inc(src_done, 1)
                pe.wait_ge(h_copied, z.NG + 1)
                pe.wait_ge(row_step, 2)
                pe.wait_ge(neg_set, 1)
                for n, (at, w) in enumerate(halves):
                    for k in range(z.KC):
                        pe.matmul(ps_h[:, 512 * n:512 * n + w], s.dst_f[0:rows[k], k, :],
                                  pick[0:rows[k], k, at:at + w], start=(k == 0), stop=False)
                    pe.matmul(ps_h[:, 512 * n:512 * n + w], neg_p[:, :], row_b[:, at:at + w],
                              start=False, stop=True).then_inc(rel_done, 1)

            @block.gpsimd
            def _(pool):
                pool.wait_ge(ext_in, 1)
                pool.partition_all_reduce(ext_all[:, :], ext[:, :], P, RMAX).then_inc(ext_out, 1)

            @block.vector
            def _(dve):
                dve.memset(neg_p[:, :], -float(P)).then_inc(neg_set, 1)
                dve.memset(s.acc[:, :, :], 0.0).then_inc(ext_step, 1)
                dve.memset(s.q_tab[:, :, :, :], 0.0).then_inc(ext_step, 1)
                dve.memset(s.d_tab[:, :, :, :], 0.0).then_inc(ext_step, 1)
                dve.sem_inc(h_copied, 1)
                with dve.Fori(0, z.NG) as g:
                    dve.wait_ge(x_turned, g + 1)
                    dve.tensor_scalar(x_g[:, :, :], s.x_sb[:, bass.ds(g * GRP, GRP), :], 1.0, None, ALU.mult).then_inc(x_copied, 1)
                    dve.wait_ge(h_done, g + 2)
                    hb = ps_h[:, :].rearrange("p (j c) -> p j c", c=P)
                    dve.tensor_scalar(s.tab0[:, bass.ds(g * GRP, 4), :], hb[:, 0:4, 0:ROW0], 1.0, None, ALU.mult)
                    dve.tensor_scalar(s.tab0[:, bass.ds(g * GRP + 4, GRP - 4), :], hb[:, 4:GRP, 0:ROW0], 1.0, None,
                                      ALU.mult).then_inc(h_copied, 1)
                for k in range(z.KC):
                    dve.tensor_scalar(pick[:, k, :], s.steps[:, :], s.hi[:, k:k + 1], None, ALU.is_lt).then_inc(pick_step, 1)
                    dve.wait_ge(pick_step, k + 1)
                    dve.scalar_tensor_tensor(out=pick[:, k, :], in0=s.steps[:, :], scalar=s.lo[:, k:k + 1],
                                             in1=pick[:, k, :], op0=ALU.is_ge, op1=ALU.mult).then_inc(pick_done, 1)
                dve.wait_ge(h_copied, z.NG + 1)
                a_src = s.tab0[:, :, D:D + H0].rearrange("p b h -> p h b")
                dve.tensor_reduce(ext[:, 0:H0], a_src, AX_X, ALU.max).then_inc(ext_step, 1)
                dve.tensor_reduce(spread[:, :], a_src, AX_X, ALU.min).then_inc(ext_step, 1)
                dve.wait_ge(ext_step, 5)
                dve.tensor_scalar(ext[:, H0:2 * H0], spread[:, :], -1.0, None, ALU.mult).then_inc(ext_in, 1)
                dve.wait_ge(ext_in, 1)
                for n, (at, w) in enumerate(halves):
                    dve.wait_ge(row_done, n + 1)
                    dve.tensor_copy(row_t[:, at:at + w], ps_r[0:1, 512 * n:512 * n + w]).then_inc(row_copied, 1)
                dve.wait_ge(row_copied, 2)
                dve.tensor_tensor(row_b[:, :], s.steps[0:1, :], row_t[:, :], ALU.subtract).then_inc(row_step, 1)
                dve.wait_ge(row_step, 1)
                dve.tensor_scalar(row_b[:, :], row_b[:, :], s.is_sorted[0:1, 0:1], None, ALU.mult).then_inc(row_step, 1)
                dve.tensor_scalar(row_e[:, :], row_t[:, :], float(P), float(z.E - P), ALU.mult, ALU.min).then_inc(row_step, 1)
                dve.wait_ge(row_step, 3)
                dve.tensor_copy(s.edge_row[:, :], row_e[:, :]).then_inc(row_step, 1)
                dve.tensor_copy(s.block_row0[:, :], row_b[:, :]).then_inc(row_step, 1)
                dve.wait_ge(row_step, 5)
                dve.tensor_copy(s.block_row[:, :], s.block_row0[:, :]).then_inc(row_step, 1)
                dve.wait_ge(ext_out, 1)
                dve.tensor_tensor(spread[:, :], ext_all[:, 0:H0], ext_all[:, H0:2 * H0], ALU.add).then_inc(row_step, 1)
                dve.tensor_scalar(s.bound[:, :, :], across(ext_all[:, 0:H0], z.NB), 1.0, None, ALU.mult).then_inc(row_step, 1)
                dve.wait_ge(row_step, 8)
                dve.tensor_reduce(wide[:, 0:1], spread[:, :], AX_X, ALU.max).then_inc(row_step, 1)
                dve.wait_ge(row_step, 9)
                dve.tensor_scalar(wide[:, 1:2], wide[:, 0:1], SPREAD_MAX, None, ALU.is_le).then_inc(row_step, 1)
                dve.wait_ge(row_step, 10)
                dve.tensor_scalar(s.is_wide[:, :], wide[:, 1:2], -1.0, 1.0, ALU.mult, ALU.add).then_inc(row_step, 1)
                for n, (at, w) in enumerate(halves):
                    dve.wait_ge(rel_done, n + 1)
                    dve.tensor_scalar(s.rel0[:, at:at + w], ps_h[:, 512 * n:512 * n + w], -SHIFT, None,
                                      ALU.add).then_inc(rels_copied, 1)
                dve.wait_ge(rels_copied, 2)
                dve.tensor_copy(s.rel[:, :], s.rel0[:, :]).then_inc(rels_copied, 1)
                dve.wait_ge(rels_copied, 3)


def shift_phase(nc, z, d, s):
    with ExitStack() as ctx:
        sb = lambda n, sh, dt=F32: ctx.enter_context(nc.sbuf_tensor(n, sh, dt))
        sem = lambda n: ctx.enter_context(nc.semaphore(n))
        ad_c = sb("ad_c", [P, z.NB, 2 * H0])
        rest = sb("rest", [P, z.NB, 2 * H0])
        part = sb("part", [P, z.NB, 2 * H0])
        own = sb("own", [P, z.NB, H0])
        sum_b = sb("sum_b", [P, z.NB, H0])
        sc, own_exp = sem("shift_step"), sem("own_exp")
        a_src, a_dst = s.tab0[:, :, D:D + H0], s.tab0[:, :, D + H0:ROW0]
        with nc.Block(no_gpsimd_drain=True) as block:

            @block.scalar
            def _(act):
                act.wait_ge(sc, 7)
                act.activation(s.acc[:, 0:z.NB, D:D + H0], own[:, :, :], ACT.Exp).then_inc(own_exp, 1)

            @block.vector
            def _(dve):
                dve.tensor_copy(ad_c[:, :, 0:H0], a_dst).then_inc(sc, 1)
                dve.tensor_tensor(sum_b[:, :, :], s.bound[:, :, :], a_dst, ALU.add).then_inc(sc, 1)
                dve.tensor_tensor(own[:, :, :], a_src, a_dst, ALU.add).then_inc(sc, 1)
                dve.wait_ge(sc, 2)
                dve.scalar_tensor_tensor(out=ad_c[:, :, H0:2 * H0], in0=sum_b[:, :, :], scalar=SLOPE,
                                         in1=sum_b[:, :, :], op0=ALU.mult, op1=ALU.max).then_inc(sc, 1)
                dve.wait_ge(sc, 3)
                dve.scalar_tensor_tensor(out=part[:, :, 0:H0], in0=own[:, :, :], scalar=SLOPE,
                                         in1=own[:, :, :], op0=ALU.mult, op1=ALU.max).then_inc(sc, 1)
                dve.wait_ge(sc, 5)
                dve.tensor_tensor(own[:, :, :], part[:, :, 0:H0], ad_c[:, :, H0:2 * H0], ALU.subtract).then_inc(sc, 1)
                dve.tensor_copy(s.d_tab[:, 0:z.NB, 0, :], ad_c[:, :, :]).then_inc(sc, 1)
                dve.wait_ge(sc, 7)
                dve.tensor_tensor(rest[:, :, :], ad_c[:, :, :], s.d_tab[:, 0:z.NB, 0, :], ALU.subtract).then_inc(sc, 1)
                dve.wait_ge(sc, 8)
                dve.tensor_copy(s.d_tab[:, 0:z.NB, 1, :], rest[:, :, :]).then_inc(sc, 1)
                dve.wait_ge(sc, 9)
                dve.tensor_tensor(part[:, :, :], rest[:, :, :], s.d_tab[:, 0:z.NB, 1, :], ALU.subtract).then_inc(sc, 1)
                dve.wait_ge(sc, 10)
                dve.tensor_copy(s.d_tab[:, 0:z.NB, 2, :], part[:, :, :]).then_inc(sc, 1)
                dve.wait_ge(own_exp, 1)
                for h in range(H0):
                    dve.tensor_tensor(s.acc[:, 0:z.NB, h * D0:(h + 1) * D0], s.tab0[:, :, h * D0:(h + 1) * D0],
                                      s.acc[:, 0:z.NB, D + h:D + h + 1].to_broadcast([P, z.NB, D0]),
                                      ALU.mult).then_inc(sc, 1)
                dve.wait_ge(sc, 11 + H0)


def exact_max_phase(nc, z, d, s):
    with ExitStack() as ctx:
        sb = lambda n, sh, dt=F32: ctx.enter_context(nc.sbuf_tensor(n, sh, dt))
        sem = lambda n: ctx.enter_context(nc.semaphore(n))
        idx = sb("mx_idx", [P, 1], I32)
        dst_col = sb("mx_dst", [P, 1])
        rows = sb("mx_rows", [P, GAT0])
        wide_s = sb("mx_wide_s", [P, H0 + 1, P])
        cand = sb("mx_cand", [P, H0, P])
        limit = sb("mx_limit", [P, P])
        a_all = sb("mx_a_all", [P, H0, P])
        dst_all = sb("mx_dst_all", [P, P])
        best = sb("mx_best", [P, H0])
        nb_col = sb("mx_nb", [P, 1])
        dst_abs = sb("mx_dst_abs", [P, z.STEPS])
        pos_p = sb("mx_pos_p", [1, P])
        ps_a = ctx.enter_context(nc.psum_tensor("mx_ps_a", [P, 512], F32))
        ps_d = ctx.enter_context(nc.psum_tensor("mx_ps_d", [P, 512], F32))
        idx_set, landed, spread_set, turned = sem("mx_idx_set"), sem("mx_landed"), sem("mx_spread"), sem("mx_turned")
        step, tile_in = sem("mx_step"), sem("mx_tile_in")
        pos_set, block_out, abs_done = sem("mx_pos_set"), sem("mx_block_out"), sem("mx_abs_done")
        HALF = -(-z.STEPS // 2)
        halves = [(0, HALF), (HALF, z.STEPS - HALF)]
        with nc.Block(no_gpsimd_drain=True) as block:

            @block.gpsimd
            def _(pool):
                wide = pool.value_load(s.is_wide[0:1, 0:1], min_val=0, max_val=1)
                with pool.If(wide != 0):
                    with pool.Fori(0, z.STEPS) as t:
                        pool.wait_ge(idx_set, t + 1)
                        pool.sem_inc(tile_in, 1)
                        pool.indirect_dma_start(rows[:, :], None, d.T0,
                                                bass.IndirectOffsetOnAxis(ap=idx[:, 0:1], axis=0)).then_inc(landed, 16)
                with pool.Else():
                    pool.sem_inc(tile_in, 1)

            @block.tensor
            def _(pe):
                wide = pe.value_load(s.is_wide[0:1, 0:1], min_val=0, max_val=1)
                with pe.If(wide != 0):
                    pe.wait_ge(pos_set, 1)
                    pe.matmul(ps_a[:, 0:HALF], pos_p[:, :], s.block_f[:, 0:HALF], start=True, stop=True)
                    pe.matmul(ps_d[:, 0:z.STEPS - HALF], pos_p[:, :], s.block_f[:, HALF:z.STEPS],
                              start=True, stop=True).then_inc(block_out, 1)
                    with pe.Fori(0, z.STEPS) as t:
                        pe.wait_ge(spread_set, t + 1)
                        for h in range(H0):
                            pe.matmul(ps_a[:, h * P:(h + 1) * P], wide_s[:, h, :], s.ident[:, :], start=True, stop=True)
                        pe.matmul(ps_d[:, 0:P], wide_s[:, H0, :], s.ident[:, :], start=True, stop=True).then_inc(turned, 1)
                with pe.Else():
                    pe.sem_inc(turned, 1)

            @block.vector
            def _(dve):
                wide = dve.value_load(s.is_wide[0:1, 0:1], min_val=0, max_val=1)
                with dve.If(wide != 0):
                    dve.memset(pos_p[:, :], float(P)).then_inc(pos_set, 1)
                    dve.wait_ge(block_out, 1)
                    for (at, w), ps in zip(halves, (ps_a, ps_d)):
                        dve.tensor_tensor(dst_abs[:, at:at + w], s.rel0[:, at:at + w], ps[:, 0:w], ALU.add).then_inc(abs_done, 1)
                    dve.wait_ge(abs_done, 2)
                    dve.tensor_copy(s.bound[:, :, :], s.tab0[:, :, D:D + H0]).then_inc(step, 1)
                    dve.wait_ge(step, 1)
                    PER = 6 + 5 * z.NB
                    with dve.Fori(0, z.STEPS) as t:
                        base = dve.snap(t * PER + 1)
                        dve.tensor_copy(dst_col[:, :], dst_abs[:, bass.ds(t, 1)]).then_inc(step, 1)
                        dve.tensor_copy(idx[:, :], s.src_idx[:, bass.ds(t, 1)]).then_inc(idx_set, 1)
                        dve.wait_ge(landed, t * 16 + 16)
                        for h in range(H0):
                            dve.tensor_scalar(wide_s[:, h, :], rows[:, D + h:D + h + 1].to_broadcast([P, P]), 1.0, None,
                                              ALU.mult).then_inc(step, 1)
                        dve.wait_ge(step, base + 5)
                        dve.tensor_scalar(wide_s[:, H0, :], dst_col[:, 0:1].to_broadcast([P, P]), 1.0, None,
                                          ALU.mult).then_inc(spread_set, 1)
                        dve.wait_ge(turned, t + 1)
                        dve.tensor_copy(a_all[:, :, :].rearrange("p h e -> p (h e)"), ps_a[:, :])
                        dve.tensor_copy(dst_all[:, :], ps_d[:, 0:P]).then_inc(step, 1)
                        with dve.Fori(0, z.NB) as b:
                            at = dve.snap(base + 6 + b * 5)
                            dve.wait_ge(step, at)
                            dve.tensor_copy(nb_col[:, :], s.node_no[:, bass.ds(b, 1)]).then_inc(step, 1)
                            dve.wait_ge(step, at + 1)
                            dve.tensor_scalar(limit[:, :], dst_all[:, :], nb_col[:, 0:1], BIG,
                                              ALU.is_equal, ALU.mult).then_inc(step, 1)
                            dve.wait_ge(step, at + 2)
                            dve.scalar_tensor_tensor(out=cand[:, :, :], in0=across(limit[:, :], H0), scalar=BIG / 2,
                                                     in1=a_all[:, :, :], op0=ALU.subtract, op1=ALU.min).then_inc(step, 1)
                            dve.wait_ge(step, at + 3)
                            dve.tensor_reduce(best[:, :], cand[:, :, :], AX_X, ALU.max).then_inc(step, 1)
                            dve.wait_ge(step, at + 4)
                            dve.tensor_tensor(s.bound[:, bass.ds(b, 1), :].rearrange("p o h -> p (o h)"),
                                              s.bound[:, bass.ds(b, 1), :].rearrange("p o h -> p (o h)"),
                                              best[:, :], ALU.max).then_inc(step, 1)
                        dve.wait_ge(step, base + PER)
                with dve.Else():
                    dve.sem_inc(step, 1)


def edge_phase(nc, z, d, s, layer):
    second = layer == 1
    heads, hd, wide = (H1, D1, ACC1) if second else (H0, D0, ACC0)
    row_w = 2 * D if second else GAT0
    dst_w = D if second else 2 * H0
    table, dst_tab = (d.T1, s.q_tab) if second else (d.T0, s.d_tab)
    acc = s.acc
    with ExitStack() as ctx:
        sb = lambda n, sh, dt=F32: ctx.enter_context(nc.sbuf_tensor(f"{n}{layer}", sh, dt))
        ps = lambda n, sh: ctx.enter_context(nc.psum_tensor(f"{n}{layer}", sh, F32))
        sem = lambda n: ctx.enter_context(nc.semaphore(f"{n}{layer}"))
        idx = sb("idx", [P, RING, QUAD], I32)
        got = sb("got", [P, RING, QUAD, row_w])
        hot = sb("hot", [P, RING, QUAD, P])
        hot_t = sb("hot_t", [P, PAR, QUAD, P], BF16)
        msg = sb("msg", [P, PAR, QUAD, wide])
        sc_a = sb("sc_a", [P, PAR, QUAD, heads])
        sc_b = sb("sc_b", [P, PAR, QUAD, heads])
        sc_c = sb("sc_c", [P, PAR, QUAD, heads])
        sc_d = sb("sc_d", [P, PAR, QUAD, heads])
        ps_hot = ps("ps_hot", [P, PAR, QUAD, P])
        ps_acc = ps("ps_acc", [P, PAR, 512])
        if second:
            prod = sb("prod", [P, PAR, QUAD, D])
            prod_e = sb("prod_e", [P, PAR, QUAD, D])
            attr = sb("attr", [P, RING, QUAD, D])
            attr_t = s.attr_t1[:, :, :].rearrange("p a (j e) -> p a j e", e=P)
            ps_attr = ps("ps_attr", [P, PAR, QUAD, P])
            ps_e = ps("ps_e", [P, 512])
            ps_dst = ps("ps_dst", [P, 1, 512])
        else:
            ps_dst = ps("ps_dst", [P, PAR, 512])
        DST_PAR = 1 if second else PAR
        SCORE0 = 0 if second else PAR

        rows_ready = sem("rows_ready")
        idx_ready = sem("idx_ready")
        gathered = [sem(f"gathered{k}") for k in range(RING)]
        hot_done = sem("hot_done")
        hot_turned = sem("hot_turned")
        hot_t_done = sem("hot_t_done")
        dst_done = sem("dst_done")
        score_done = sem("score_done")
        dst_used = sem("dst_used") if second else score_done
        exp_done = sem("exp_done")
        msg_done = sem("msg_done")
        sum_done = sem("sum_done")
        acc_done = sem("acc_done")
        mid_a, mid_b, mid_c = sem("mid_a"), sem("mid_b"), sem("mid_c")
        pool_go, pass_begun = sem("pool_go"), sem("pass_begun")
        if second:
            attr_in = [sem(f"attr_in{k}") for k in range(RING)]
            attr_turned = sem("attr_turned")
            attr_t_done = sem("attr_t_done")
            e_done = sem("e_done")
            e_used = sem("e_used")

        def in_slots(eng, first, last, slot):
            n_pass = eng.value_load(s.passes[0:1, 0:1], min_val=1, max_val=z.NB)
            with eng.Fori(0, n_pass) as p:
                eng.wait_ge(rows_ready, p * 2 + 2)
                eng.sem_inc(pass_begun, 1)
                base = eng.snap(p * z.NQ)
                rounds = eng.snap(p * z.NIT)
                for q in range(first, RING):
                    slot(q, base, 0, rounds, lambda c, q=q: 0 <= q + c < z.NQ)
                with eng.Fori(1, z.NIT - 1) as it:
                    at = eng.snap(base + it * RING)
                    rd = eng.snap(rounds + it)
                    for k in range(RING):
                        slot(k, at, it, rd, lambda c: True)
                end = z.NIT - 1
                at = eng.snap(base + end * RING)
                rd = eng.snap(rounds + end)
                for k in range(RING + last):
                    slot(k, at, end, rd, lambda c, k=k: 0 <= end * RING + k + c < z.NQ)
                if eng is nc.vector:
                    dve = eng
                    dve.wait_ge(acc_done, (base + z.NQ + PAR) * QUAD)
                    dve.tensor_scalar(s.rel[:, :], s.rel[:, :], -float(P), None, ALU.add).then_inc(rows_ready, 1)
                    dve.tensor_scalar(s.block_row[:, :], s.block_row[:, :], 1, None, ALU.add).then_inc(rows_ready, 1)

        def steps_of(it, n):
            return bass.ds(it * (RING * QUAD) + n * QUAD, QUAD)

        with nc.Block(no_gpsimd_drain=True) as block:

            @block.gpsimd
            def _(pool):
                def slot(k, base, it, rounds, has):
                    pool.wait_ge(idx_ready, base + (k + 1))
                    pool.wait_ge(msg_done, base + (k + 1))
                    pool.sem_inc(pool_go, 1)
                    for j in range(QUAD):
                        pool.indirect_dma_start(got[:, k % RING, j, :], None, table,
                                                bass.IndirectOffsetOnAxis(ap=idx[:, k % RING, j:j + 1], axis=0)
                                                ).then_inc(gathered[k % RING], 16)
                in_slots(pool, 0, 0, slot)

            @block.sync
            def _(sp):
                if not second:
                    return
                regs = [sp.alloc_register(f"edge_at{j}") for j in range(QUAD)]

                def slot(k, base, it, rounds, has):
                    sp.reg_load(regs, s.edge_row[0:1, steps_of(it, k)])
                    sp.wait_ge(attr_turned, base + (k + 1))
                    for j in range(QUAD):
                        at = sp.snap(regs[j], min_val=0, max_val=z.E - P)
                        sp.dma_start(attr[:, k % RING, j, :], d.attr[bass.ds(at, P), :]).then_inc(attr_in[k % RING], 16)
                in_slots(sp, 0, 0, slot)

            @block.scalar
            def _(act):
                act.sem_inc(hot_t_done, PAR)
                if second:
                    act.sem_inc(attr_t_done, PAR)

                def slot(k, base, it, rounds, has):
                    if has(0):
                        n = k
                        act.wait_ge(score_done, base + (n + 1 + SCORE0))
                        act.wait_ge(sum_done, base + (n - PAR + RING + 1))
                        act.activation(msg[:, n % PAR, :, D:wide], sc_c[:, n % PAR, :, :], ACT.Exp).then_inc(exp_done, 1)
                    if has(2):
                        n = k + 2
                        act.wait_ge(hot_turned, base + (n + 1))
                        act.wait_ge(dst_done, base + (n + 1))
                        act.activation(hot_t[:, n % PAR, :, :], ps_hot[:, n % PAR, :, :], ACT.Copy).then_inc(hot_t_done, 1)
                        if second:
                            act.wait_ge(attr_turned, base + (n + RING + 1))
                            act.wait_ge(e_done, base + (n + 1))
                            act.activation(attr_t[0:D, n % PAR, :, :], ps_attr[0:D, n % PAR, :, :],
                                           ACT.Copy).then_inc(attr_t_done, 1)
                in_slots(act, -2, 0, slot)

            @block.tensor
            def _(pe):
                pe.sem_inc(dst_done, PAR)
                pe.sem_inc(sum_done, RING)
                if second:
                    pe.sem_inc(attr_turned, RING)
                    pe.sem_inc(e_done, PAR)
                regs = [pe.alloc_register(f"block_at{layer}_{j}") for j in range(QUAD)]

                def slot(k, base, it, rounds, has):
                    if has(-1):
                        n = k - 1
                        pe.wait_ge(msg_done, base + (n + RING + 1))
                        pe.wait_ge(acc_done, (base + (n + 1)) * QUAD)
                        for j in range(QUAD):
                            last = pe.matmul(ps_acc[:, n % PAR, j * wide:(j + 1) * wide], hot[:, n % RING, j, :],
                                             msg[:, n % PAR, j, :], start=True, stop=True)
                        last.then_inc(sum_done, 1)
                    if has(1):
                        n = k + 1
                        pe.reg_load(regs, s.block_row[0:1, steps_of(it, n)])
                        pe.wait_ge(hot_t_done, base + (n + PAR + 1))
                        pe.wait_ge(dst_used, base + (n + 1))
                        for j in range(QUAD):
                            b = pe.snap(regs[j], min_val=0, max_val=z.BROWS - 1)
                            for c in range(3):
                                last = pe.matmul(ps_dst[:, n % DST_PAR, j * dst_w:(j + 1) * dst_w],
                                                 hot_t[:, n % PAR, j, :],
                                                 dst_tab[:, bass.ds(b, 1), c, :].rearrange("p o e -> p (o e)"),
                                                 start=(c == 0), stop=(c == 2))
                        last.then_inc(dst_done, 1)
                        if second:
                            pe.wait_ge(attr_t_done, base + (n + PAR + 1))
                            pe.wait_ge(e_used, base + (n + 1))
                            for j in range(QUAD):
                                last = pe.matmul(ps_e[:, j * D:(j + 1) * D], attr_t[:, n % PAR, j, :], s.w_e[:, :],
                                                 start=True, stop=True)
                            last.then_inc(e_done, 1)
                    if has(2):
                        n = k + 2
                        pe.wait_ge(hot_done, base + (n + 1))
                        pe.wait_ge(hot_t_done, base + (n + 1))
                        for j in range(QUAD):
                            last = pe.transpose(ps_hot[:, n % PAR, j, :], hot[:, n % RING, j, :], s.ident[:, :])
                        last.then_inc(hot_turned, 1)
                        if second:
                            pe.wait_ge(attr_in[n % RING], (rounds + (n // RING + 1)) * (16 * QUAD))
                            pe.wait_ge(attr_t_done, base + (n + 1))
                            for j in range(QUAD):
                                last = pe.transpose(ps_attr[0:D, n % PAR, j, :], attr[:, n % RING, j, :], s.ident[:, :])
                            last.then_inc(attr_turned, 1)
                in_slots(pe, -2, 1, slot)

            @block.vector
            def _(dve):
                dve.sem_inc(rows_ready, 2)
                dve.sem_inc(msg_done, RING)
                dve.sem_inc(dst_used, DST_PAR)
                dve.sem_inc(acc_done, QUAD * PAR)
                if second:
                    dve.sem_inc(e_used, 1)
                regs = [dve.alloc_register(f"sum_at{layer}_{j}") for j in range(QUAD)]

                def slot(k, base, it, rounds, has):
                    def add(j):
                        if not has(-2):
                            return
                        n = k - 2
                        if j == 0:
                            dve.reg_load(regs, s.block_row[0:1, steps_of(it, n)])
                            dve.wait_ge(sum_done, base + (n + RING + 1))
                        b = dve.snap(regs[j], min_val=0, max_val=z.BROWS - 1)
                        to = acc[:, bass.ds(b, 1), 0:wide].rearrange("p o e -> p (o e)")
                        dve.wait_ge(acc_done, (base + (n + PAR)) * QUAD + j)
                        dve.tensor_tensor(to, to, ps_acc[:, n % PAR, j * wide:(j + 1) * wide], ALU.add).then_inc(acc_done, 1)

                    add(0)
                    add(1)
                    if has(-1):
                        n = k - 1
                        dve.wait_ge(exp_done, base + (n + 1))
                        val = got[:, n % RING, :, D:2 * D] if second else got[:, n % RING, :, 0:D]
                        dve.tensor_tensor(msg[:, n % PAR, :, 0:D].rearrange("p j (h e) -> p j h e", e=hd),
                                          val.rearrange("p j (h e) -> p j h e", e=hd),
                                          over(msg[:, n % PAR, :, D:wide], hd), ALU.mult).then_inc(msg_done, 1)
                    if has(3):
                        n = k + 3
                        dve.tensor_copy(idx[:, n % RING, :], s.src_idx[:, steps_of(it, n)]).then_inc(idx_ready, 1)
                    if has(0):
                        dve.wait_ge(gathered[k % RING], (rounds + (k // RING + 1)) * (16 * QUAD))
                        dve.wait_ge(dst_done, base + (k + PAR + 1))
                        at = ps_dst[:, k % DST_PAR, 0:QUAD * dst_w].rearrange("p (j e) -> p j e", j=QUAD)
                        rows = got[:, k % RING, :, :]
                        par = k % PAR
                        if second:
                            dve.tensor_tensor(prod[:, par, :, :], rows[:, :, 0:D], at, ALU.mult).then_inc(dst_used, 1)
                        else:
                            dve.tensor_tensor(sc_a[:, par, :, :], rows[:, :, D:D + H0], at[:, :, 0:H0], ALU.add).then_inc(mid_a, 1)
                    add(2)
                    if has(0):
                        if second:
                            dve.wait_ge(e_done, base + (k + PAR + 1))
                            dve.wait_ge(dst_used, base + (k + 2))
                            dve.tensor_tensor(prod_e[:, par, :, :], prod[:, par, :, :],
                                              ps_e[:, 0:QUAD * D].rearrange("p (j e) -> p j e", j=QUAD),
                                              ALU.mult).then_inc(e_used, 1)
                        else:
                            dve.wait_ge(mid_a, base + (k + 1))
                            dve.scalar_tensor_tensor(out=sc_b[:, par, :, :], in0=sc_a[:, par, :, :], scalar=SLOPE,
                                                     in1=sc_a[:, par, :, :], op0=ALU.mult, op1=ALU.max).then_inc(mid_b, 1)
                    if has(2):
                        n = k + 2
                        dve.wait_ge(sum_done, base + (n + 1))
                        dve.tensor_tensor(hot[:, n % RING, :, :], across(s.iota[:, :], QUAD),
                                          over(s.rel[:, steps_of(it, n)], P), ALU.is_equal).then_inc(hot_done, 1)
                    if has(0):
                        if second:
                            dve.wait_ge(e_used, base + (k + 2))
                            dve.tensor_reduce(sc_a[:, par, :, :].rearrange("p j h -> p (j h)"),
                                              prod_e[:, par, :, :].rearrange("p j (h e) -> p (j h) e", e=D1),
                                              AX_X, ALU.add).then_inc(mid_a, 1)
                        else:
                            dve.wait_ge(mid_b, base + (k + 1))
                            dve.tensor_tensor(sc_d[:, par, :, :], sc_b[:, par, :, :], at[:, :, H0:2 * H0],
                                              ALU.subtract).then_inc(mid_c, 1)
                    add(3)
                    if has(0):
                        if second:
                            dve.wait_ge(mid_a, base + (k + 1))
                            dve.tensor_scalar(sc_c[:, par, :, :], sc_a[:, par, :, :], 5.0, -5.0,
                                              ALU.min, ALU.max).then_inc(score_done, 1)
                        else:
                            dve.wait_ge(mid_c, base + (k + 1))
                            dve.tensor_scalar(sc_c[:, par, :, :], sc_d[:, par, :, :], 0.0, None,
                                              ALU.min).then_inc(score_done, 1)
                in_slots(dve, -3, 2, slot)


def linker(eng, sem, base):
    count = [0]

    def link(ins):
        count[0] += 1
        ins.then_inc(sem, 1)
        eng.wait_ge(sem, base + count[0])
    link.count = count
    return link


def center(dve, link, out, v, total):
    link(dve.tensor_reduce(total[:, :], v, AX_X, ALU.add))
    link(dve.tensor_scalar(total[:, :], total[:, :], -1.0 / D, None, ALU.mult))
    link(dve.tensor_tensor(out, v, over(total[:, :], D), ALU.add))


def inverse_deviation(dve, link, v, square, total, asked, root, at):
    link(dve.tensor_tensor(square, v, v, ALU.mult))
    link(dve.tensor_reduce(total[:, :], square, AX_X, ALU.add))
    dve.tensor_scalar(total[:, :], total[:, :], 1.0 / D, EPS, ALU.mult, ALU.add).then_inc(asked, 1)
    dve.wait_ge(root, at)
    link(dve.reciprocal(total[:, :], total[:, :]))


def middle_phase(nc, z, d, s):
    with ExitStack() as ctx:
        sb = lambda n, sh, dt=F32: ctx.enter_context(nc.sbuf_tensor(f"mid_{n}", sh, dt))
        sem = lambda n: ctx.enter_context(nc.semaphore(f"mid_{n}"))
        inv = sb("inv", [P, GRP, H0])
        agg = sb("agg", [P, GRP, D])
        agg_t = sb("agg_t", [D + 1, GRP * P])
        v = sb("v", [P, GRP, D])
        vc = sb("vc", [P, GRP, D])
        sq = sb("sq", [P, GRP, D])
        x1g = sb("x1g", [P, GRP, D])
        tot = sb("tot", [P, GRP])
        tot2 = sb("tot2", [P, GRP])
        zeros = sb("zeros", [P, GRP])
        kv = sb("kv", [P, GRP, 2 * D])
        q = sb("q", [P, GRP, D])
        q_hi = sb("q_hi", [P, GRP, D], BF16)
        q_r = sb("q_r", [P, GRP, D])
        q_s = sb("q_s", [P, GRP, D])
        ps_t = ctx.enter_context(nc.psum_tensor("mid_ps_t", [P, 1024], F32))
        ps_z = ctx.enter_context(nc.psum_tensor("mid_ps_z", [P, 1024], F32))
        ps_k = ctx.enter_context(nc.psum_tensor("mid_ps_k", [P, 4, 512], F32))
        dv, ones_set = sem("dv"), sem("ones_set")
        agg_done, agg_turned, agg_copied, z_done = sem("agg_done"), sem("agg_turned"), sem("agg_copied"), sem("z_done")
        asked, root = sem("asked"), sem("root")
        x1_done, x1_turned, x1_copied = sem("x1_done"), sem("x1_turned"), sem("x1_copied")
        k_done, kv_copied, q_copied, t1_stored = sem("k_done"), sem("kv_copied"), sem("q_copied"), sem("t1_stored")
        split_step, split_done, split_go = sem("split_step"), sem("split_done"), sem("split_go")
        t1_rows = d.T1.rearrange("(b p) c -> p b c", p=P)
        parts = [(0, 4), (4, GRP)]
        with nc.Block(no_gpsimd_drain=True) as block:

            @block.sync
            def _(sp):
                with sp.Fori(0, z.NG) as g:
                    sp.wait_ge(kv_copied, g * 2 + 2)
                    sp.dma_start(t1_rows[:, bass.ds(g * GRP, GRP), :], kv[:, :, :]).then_inc(t1_stored, 16)
                sp.wait_ge(t1_stored, 16 * (z.NG + 1))

            @block.scalar
            def _(act):
                act.sem_inc(t1_stored, 16)
                with act.Fori(0, z.NG) as g:
                    act.wait_ge(agg_turned, g + 1)
                    act.activation(agg_t[0:D, 0:4 * P], ps_t[0:D, 0:4 * P], ACT.Copy)
                    act.activation(agg_t[0:D, 4 * P:GRP * P], ps_t[0:D, 4 * P:GRP * P], ACT.Copy).then_inc(agg_copied, 1)
                    for n in range(2):
                        t = (tot, tot2)[n]
                        act.wait_ge(asked, g * 2 + (n + 1))
                        act.activation(t[:, :], t[:, :], ACT.Sqrt).then_inc(root, 1)
                    act.wait_ge(x1_turned, g + 1)
                    act.activation(s.x_t1[0:D, 0, 0:4 * P], ps_t[0:D, 0:4 * P], ACT.Copy)
                    act.activation(s.x_t1[0:D, 0, 4 * P:GRP * P], ps_t[0:D, 4 * P:GRP * P], ACT.Copy).then_inc(x1_copied, 1)
                    act.wait_ge(t1_stored, g * 16 + 16)
                    for n, (a, b) in enumerate(parts):
                        act.wait_ge(k_done, g * 2 + (n + 1))
                        act.activation(kv[:, a:b, :], ps_k[:, 0:b - a, 0:2 * D], ACT.Copy).then_inc(kv_copied, 1)

            @block.tensor
            def _(pe):
                pe.wait_ge(ones_set, 1)
                with pe.Fori(0, z.NG) as g:
                    pe.wait_ge(agg_done, g + 1)
                    for j in range(GRP):
                        last = pe.transpose(ps_t[0:D, j * P:(j + 1) * P], agg[:, j, :], s.ident[:, :])
                    last.then_inc(agg_turned, 1)
                    pe.wait_ge(agg_copied, g + 1)
                    for j in range(GRP):
                        last = pe.matmul(ps_z[:, j * P:j * P + D], agg_t[:, j * P:(j + 1) * P], s.w_proj[:, :],
                                         start=True, stop=True)
                    last.then_inc(z_done, 1)
                    pe.wait_ge(x1_done, g + 1)
                    for j in range(GRP):
                        last = pe.transpose(ps_t[0:D, j * P:(j + 1) * P], x1g[:, j, :], s.ident[:, :])
                    last.then_inc(x1_turned, 1)
                    pe.wait_ge(x1_copied, g + 1)
                    for n, (a, b) in enumerate(parts):
                        if n:
                            pe.wait_ge(q_copied, g * 2 + n)
                        for j in range(a, b):
                            last = pe.matmul(ps_k[:, j - a, 0:3 * D], s.x_t1[:, 0, j * P:(j + 1) * P], s.w_kvq[:, :],
                                             start=True, stop=True)
                        last.then_inc(k_done, 1)

            @block.gpsimd
            def _(pool):
                pool.sem_inc(split_done, 1)
                with pool.Fori(0, z.NG) as g:
                    pool.wait_ge(q_copied, g * 2 + 2)
                    pool.sem_inc(split_step, 1)
                    to = s.q_tab[:, bass.ds(g * GRP, GRP), :, :]
                    n = g * 6
                    pool.tensor_copy(to[:, :, 0, :], q[:, :, :]).then_inc(split_step, 1)
                    pool.wait_ge(split_step, n + 2)
                    pool.sem_inc(split_go, 1)
                    pool.tensor_tensor(q_r[:, :, :], q[:, :, :], to[:, :, 0, :], ALU.subtract).then_inc(split_step, 1)
                    pool.wait_ge(split_step, n + 3)
                    pool.sem_inc(split_step, 1)
                    pool.tensor_copy(to[:, :, 1, :], q_r[:, :, :]).then_inc(split_step, 1)
                    pool.wait_ge(split_step, n + 5)
                    pool.sem_inc(split_go, 1)
                    pool.tensor_tensor(q_s[:, :, :], q_r[:, :, :], to[:, :, 1, :], ALU.subtract).then_inc(split_step, 1)
                    pool.wait_ge(split_step, n + 6)
                    pool.sem_inc(split_go, 1)
                    pool.tensor_copy(to[:, :, 2, :], q_s[:, :, :]).then_inc(split_done, 1)
                pool.wait_ge(split_done, z.NG + 1)

            @block.vector
            def _(dve):
                dve.memset(agg_t[:, :], 1.0).then_inc(ones_set, 1)
                dve.memset(zeros[:, :], 0.0).then_inc(ones_set, 1)
                dve.wait_ge(ones_set, 2)
                dve.tensor_copy(s.rel[:, :], s.rel0[:, :]).then_inc(ones_set, 1)
                dve.tensor_copy(s.block_row[:, :], s.block_row0[:, :]).then_inc(ones_set, 1)
                with dve.Fori(0, z.NG) as g:
                    link = linker(dve, dv, dve.snap(g * LINKS))
                    blocks = bass.ds(g * GRP, GRP)
                    link(dve.reciprocal(inv[:, :, :], s.acc[:, blocks, D:ACC0]))
                    dve.tensor_tensor(agg[:, :, :].rearrange("p j (h e) -> p j h e", e=D0),
                                      s.acc[:, blocks, 0:D].rearrange("p j (h e) -> p j h e", e=D0),
                                      over(inv[:, :, :], D0), ALU.mult).then_inc(agg_done, 1)
                    dve.wait_ge(z_done, g + 1)
                    for a, b in parts:
                        link(dve.tensor_tensor(v[:, a:b, :], s.x_sb[:, bass.ds(g * GRP + a, b - a), :],
                                               ps_z[:, :].rearrange("p (j c) -> p j c", c=P)[:, a:b, 0:D], ALU.add))
                    center(dve, link, vc[:, :, :], v[:, :, :], tot)
                    inverse_deviation(dve, link, vc[:, :, :], sq[:, :, :], tot, asked, root, g * 2 + 1)
                    link(dve.tensor_tensor(vc[:, :, :], vc[:, :, :], over(tot[:, :], D), ALU.mult))
                    link(dve.tensor_tensor(vc[:, :, :], vc[:, :, :], across(s.ln_g[:, :], GRP), ALU.mult))
                    link(dve.tensor_tensor(vc[:, :, :], vc[:, :, :], across(s.ln_b[:, :], GRP), ALU.add))
                    link(dve.tensor_tensor(v[:, :, :], s.x_sb[:, blocks, :], vc[:, :, :], ALU.add))
                    center(dve, link, vc[:, :, :], v[:, :, :], tot2)
                    inverse_deviation(dve, link, vc[:, :, :], sq[:, :, :], tot2, asked, root, g * 2 + 2)
                    dve.tensor_tensor(x1g[:, :, :], vc[:, :, :], over(tot2[:, :], D), ALU.mult).then_inc(x1_done, 1)
                    dve.wait_ge(x1_done, g + 1)
                    link(dve.tensor_scalar(s.x1[:, blocks, :], x1g[:, :, :], 1.0, None, ALU.mult))
                    link(dve.tensor_scalar(s.acc[:, blocks, :], over(zeros[:, :], ACC1), 1.0, None, ALU.mult))
                    dve.wait_ge(split_done, g + 1)
                    for n, (a, b) in enumerate(parts):
                        dve.wait_ge(kv_copied, g * 2 + (n + 1))
                        dve.tensor_scalar(q[:, a:b, :], ps_k[:, 0:b - a, 2 * D:3 * D], 1.0 / float(np.sqrt(D1)), None,
                                          ALU.mult).then_inc(q_copied, 1)
                    assert link.count[0] == LINKS, link.count


LINKS = 21


def last_phase(nc, z, d, s):
    with ExitStack() as ctx:
        sb = lambda n, sh, dt=F32: ctx.enter_context(nc.sbuf_tensor(f"end_{n}", sh, dt))
        sem = lambda n: ctx.enter_context(nc.semaphore(f"end_{n}"))
        inv = sb("inv", [P, GRP, H1])
        v = sb("v", [P, GRP, D])
        vc = sb("vc", [P, GRP, D])
        sq = sb("sq", [P, GRP, D])
        tot = sb("tot", [P, GRP])
        dv, asked, root, y_done, stored = sem("dv"), sem("asked"), sem("root"), sem("y_done"), sem("stored")
        with nc.Block(no_gpsimd_drain=True) as block:

            @block.scalar
            def _(act):
                with act.Fori(0, z.NG) as g:
                    act.wait_ge(asked, g + 1)
                    act.activation(tot[:, :], tot[:, :], ACT.Sqrt).then_inc(root, 1)

            @block.vector
            def _(dve):
                with dve.Fori(0, z.NG) as g:
                    link = linker(dve, dv, dve.snap(g * 10))
                    blocks = bass.ds(g * GRP, GRP)
                    link(dve.tensor_scalar(inv[:, :, :], s.acc[:, blocks, D:ACC1], 1e-6, None, ALU.add))
                    link(dve.reciprocal(inv[:, :, :], inv[:, :, :]))
                    link(dve.tensor_tensor(v[:, :, :].rearrange("p j (h e) -> p j h e", e=D1),
                                           s.acc[:, blocks, 0:D].rearrange("p j (h e) -> p j h e", e=D1),
                                           over(inv[:, :, :], D1), ALU.mult))
                    link(dve.tensor_tensor(v[:, :, :], s.x1[:, blocks, :], v[:, :, :], ALU.add))
                    center(dve, link, vc[:, :, :], v[:, :, :], tot)
                    inverse_deviation(dve, link, vc[:, :, :], sq[:, :, :], tot, asked, root, g + 1)
                    dve.tensor_tensor(s.x_sb[:, blocks, :], vc[:, :, :], over(tot[:, :], D), ALU.mult).then_inc(y_done, 1)
                    assert link.count[0] == 10, link.count

            @block.sync
            def _(sp):
                n_stores = 0
                for g in range(z.NG):
                    a, b = g * GRP, min((g + 1) * GRP, z.FULL)
                    sp.wait_ge(y_done, g + 1)
                    if b > a:
                        sp.dma_start(d.out[a * P:b * P, :].rearrange("(b p) e -> p b e", p=P),
                                     s.x_sb[:, a:b, :]).then_inc(stored, 16)
                        n_stores += 1
                    if z.REST and g * GRP <= z.FULL < (g + 1) * GRP:
                        sp.dma_start(d.out[z.FULL * P:z.N, :], s.x_sb[0:z.REST, z.FULL, :]).then_inc(stored, 16)
                        n_stores += 1
                sp.wait_ge(stored, 16 * n_stores)


def build(nc, z, d, where):
    d.T0 = nc.dram_tensor("T0", [z.NB * P, GAT0], F32).ap()
    d.T1 = nc.dram_tensor("T1", [z.NB * P, 2 * D], F32).ap()
    with ExitStack() as ctx:
        def sb(name, shape, dt=F32):
            return ctx.enter_context(nc.sbuf_tensor(name, shape, dt))

        s = Bag()
        s.cst = sb("cst", [P, where[-1][1]])
        s.ident, s.iota, s.tile_no, s.not_first, s.heads, s.node_no = (s.cst[:, a:b] for a, b in where)
        s.x_sb = sb("x_sb", [P, z.NB, D])
        s.acc = sb("acc", [P, z.BROWS, ACC1])
        s.q_tab = sb("q_tab", [P, z.BROWS, 3, D], BF16)
        s.d_tab = sb("d_tab", [P, z.BROWS, 3, 2 * H0], BF16)
        s.w_kvq = sb("w_kvq", [D + 1, 3 * D])
        s.w_e = sb("w_e", [D + 1, D])
        s.w_proj = sb("w_proj", [D + 1, D])
        s.ln_g = sb("ln_g", [P, D])
        s.ln_b = sb("ln_b", [P, D])
        s.x_t1 = sb("x_t1", [D + 1, 1, GRP * P])
        s.attr_t1 = sb("attr_t1", [D + 1, PAR, QUAD * P])
        s.x_t = s.x_t1[:, 0, :]
        s.src_idx = sb("src_idx", [P, z.STEPS], I32)
        s.rel0 = sb("rel0", [P, z.STEPS])
        s.rel = sb("rel", [P, z.STEPS])
        s.block_f = sb("block_f", [1, z.STEPS])
        s.block_row0 = sb("block_row0", [1, z.STEPS], I32)
        s.block_row = sb("block_row", [1, z.STEPS], I32)
        s.edge_row = sb("edge_row", [1, z.STEPS], I32)
        s.viol = sb("viol", [P, 1])
        s.is_sorted = sb("is_sorted", [P, 1])
        s.passes = sb("passes", [P, 1], I32)
        s.is_wide = sb("is_wide", [P, 1], I32)
        with nc.sbuf_tensor("tab0", [P, z.NB, ROW0], F32) as s.tab0, nc.sbuf_tensor("bound", [P, z.NB, H0], F32) as s.bound:
            with ExitStack() as early:
                eb = lambda n, sh: early.enter_context(nc.sbuf_tensor(n, sh, F32))
                s.steps = eb("steps", [P, z.STEPS])
                s.w_x = eb("w_x", [D, ROW0])
                s.dst_f = eb("dst_f", [P, z.KC, P])
                s.src_f = eb("src_f", [P, z.KC, P])
                s.lo = eb("lo", [P, z.KC])
                s.hi = eb("hi", [P, z.KC])
                load_phase(nc, z, d, s, where)
                table_phase(nc, z, d, s)
            exact_max_phase(nc, z, d, s)
            shift_phase(nc, z, d, s)
        edge_phase(nc, z, d, s, 0)
        s.x1 = sb("x1", [P, z.NB, D])
        middle_phase(nc, z, d, s)
        edge_phase(nc, z, d, s, 1)
        last_phase(nc, z, d, s)


_INS = ['x', 'src', 'dst', 'edge_attr_96', 'L0_gnn_W', 'L0_gnn_att_src', 'L0_gnn_att_dst', 'L0_gnn_gat_bias',
        'L0_gnn_proj_W', 'L0_gnn_proj_b', 'L0_gnn_ln_g', 'L0_gnn_ln_b', 'L1_gnn_Wq', 'L1_gnn_bq', 'L1_gnn_Wk',
        'L1_gnn_bk', 'L1_gnn_We', 'L1_gnn_be', 'L1_gnn_Wv', 'L1_gnn_bv']


def program(nc, inputs):
    z = sizes(inputs['x'].shape[0], inputs['src'].shape[0])
    table, where, steps, tail = constants(z)
    arrays = {name: np.ascontiguousarray(inputs[name]) for name in _INS}
    arrays |= {'cst': table, 'steps': steps, 'tail': tail}

    def given(name):
        a = arrays[name]
        return nc.dram_tensor(f"in_{name}_dram", a.shape, mybir.dt.from_np(a.dtype), kind="ExternalInput").ap()

    d = Bag()
    d.x, d.src, d.dst, d.attr = (given(n) for n in _INS[:4])
    d.W, d.att_src, d.att_dst, d.gat_bias, d.proj_W, d.proj_b, d.ln_g, d.ln_b = (given(n) for n in _INS[4:12])
    d.Wq, d.bq, d.Wk, d.bk, d.We, d.be, d.Wv, d.bv = (given(n) for n in _INS[12:])
    d.cst, d.steps, d.tail = given('cst'), given('steps'), given('tail')
    d.out = nc.dram_tensor("out_0_dram", (z.N, D), F32, kind="ExternalOutput").ap()
    build(nc, z, d, where)
    return {f"in_{name}_dram": a for name, a in arrays.items()}


def kernel(**inputs):
    import concourse.bacc as _bacc
    from concourse.bass_utils import run_bass_kernel_spmd as _run

    nc = _bacc.Bacc("TRN2", target_bir_lowering=False, num_devices=1)
    arrays = program(nc, inputs)
    r = _run(nc, [arrays], core_ids=[0])
    return r.results[0]["out_0_dram"]
```

```python
from contextlib import ExitStack

import concourse.bass as bass
import numpy as np
from concourse import mybir


class Bag:
    pass


F32 = mybir.dt.float32
BF16 = mybir.dt.bfloat16
I32 = mybir.dt.int32
ALU = mybir.AluOpType
ACT = mybir.ActivationFunctionType
AX_X = mybir.AxisListType.X
RMAX = bass.bass_isa.ReduceOp.max

P = 128
D = 96
H0, D0 = 4, 24
H1, D1 = 8, 12
SLOPE, EPS = 0.2, 1e-5
ROW0 = D + 2 * H0
GAT0 = D + H0
ACC0 = D + H0
ACC1 = D + H1
QUAD = 4
RING = 4
PAR = 2
GRP = 7
SHIFT = 8192.0
BIG = 3e38
SPREAD_MAX = 60.0
LAST_DST = 1 << 20


def sizes(n_nodes, n_edges):
    z = Bag()
    z.N, z.E = n_nodes, n_edges
    z.NB = -(-n_nodes // (P * GRP)) * GRP
    z.FULL = n_nodes // P
    z.REST = n_nodes - z.FULL * P
    z.NG = z.NB // GRP
    z.T = -(-n_edges // P)
    z.TAIL = n_edges - (z.T - 1) * P
    z.KC = -(-z.T // P)
    body = QUAD * RING
    z.NIT = -(-(z.T + z.NB - 1) // body)
    z.NQ = z.NIT * RING
    z.STEPS = z.NIT * body
    z.BROWS = z.STEPS - z.T + 2
    assert z.BROWS >= z.NB and z.NIT >= 3
    return z


def constants(z):
    part = np.arange(P, dtype=np.float32)[:, None]
    tile = part + P * np.arange(z.KC, dtype=np.float32)[None, :]
    heads = (np.arange(P)[:, None] // D0 == np.arange(H0)[None, :]).astype(np.float32)
    cols = [
        np.eye(P, dtype=np.float32),
        np.tile(np.arange(P, dtype=np.float32)[None, :], (P, 1)),
        tile,
        (tile > 0).astype(np.float32),
        heads,
        part + P * np.arange(z.NB, dtype=np.float32)[None, :],
    ]
    at, where = 0, []
    for c in cols:
        where.append((at, at + c.shape[1]))
        at += c.shape[1]
    steps = np.tile(np.arange(z.STEPS, dtype=np.float32)[None, :], (P, 1))
    tail = np.full((1, P + 1), -1, np.int32)
    tail[0, P] = LAST_DST
    return np.ascontiguousarray(np.concatenate(cols, 1)), where, steps, tail


def over(ap, n):
    return ap.unsqueeze(len(ap.shape)).to_broadcast([*ap.shape, n])


def across(ap, n):
    return ap.unsqueeze(1).to_broadcast([ap.shape[0], n, ap.shape[1]])


def load_phase(nc, z, d, s, where):
    with ExitStack() as ctx:
        sb = lambda n, sh, dt=F32: ctx.enter_context(nc.sbuf_tensor(n, sh, dt))
        sem = lambda n: ctx.enter_context(nc.semaphore(n))
        w_raw = sb("w_raw", [D, D])
        pw_raw = sb("pw_raw", [D, D])
        att = sb("att", [D, 2])
        attm = sb("attm", [D, 2, H0])
        gbias = sb("gbias", [D, 1])
        pbias = sb("pbias", [1, D])
        bias2 = sb("bias2", [1, D])
        w_t = sb("w_t", [D, D])
        dst_i = sb("dst_i", [P, z.KC, P + 1], I32)
        src_i = sb("src_i", [P, z.KC, P], I32)
        first_i = sb("first_i", [P, z.KC], I32)
        later_i = sb("later_i", [P, z.KC], I32)
        down = sb("down", [P, z.KC, P])
        down_max = sb("down_max", [P, 1])
        ps_w = ctx.enter_context(nc.psum_tensor("ps_w", [P, 512], F32))
        ps_p = ctx.enter_context(nc.psum_tensor("ps_p", [P, 512], F32))
        ps_a = ctx.enter_context(nc.psum_tensor("ps_a", [P, 512], F32))
        ps_b = ctx.enter_context(nc.psum_tensor("ps_b", [P, 512], F32))

        cleared = sem("cleared")
        x_loaded, x_cleared = sem("x_loaded"), sem("x_cleared")
        par_loaded = sem("par_loaded")
        par_more = sem("par_more")
        edges_loaded = sem("edges_loaded")
        tail_loaded = sem("tail_loaded")
        w_turned, w_copied = sem("w_turned"), sem("w_copied")
        p_turned, p_copied = sem("p_turned"), sem("p_copied")
        att_made, comp_done = sem("att_made"), sem("comp_done")
        bias_done, bias_made, bias_put = sem("bias_done"), sem("bias_made"), sem("bias_put")
        dve_step = sem("dve_step")
        viol_in, viol_out = sem("viol_in"), sem("viol_out")

        ra = z.T - 1
        lp, lk = ra % P, ra // P
        N_PAR, N_MORE, N_EDGE = 8, 11, 0

        with nc.Block(no_gpsimd_drain=True) as block:

            @block.gpsimd
            def _(pool):
                pool.memset(s.x_sb[:, z.FULL:z.NB, :], 0.0).then_inc(x_cleared, 1)
                pool.memset(dst_i[:, :, :], 0).then_inc(cleared, 1)
                pool.memset(src_i[:, :, :], 0).then_inc(cleared, 1)
                pool.memset(first_i[:, :], 0).then_inc(cleared, 1)
                pool.wait_ge(viol_in, 1)
                pool.partition_all_reduce(s.viol[:, :], down_max[:, :], P, RMAX).then_inc(viol_out, 1)

            @block.sync
            def _(sp):
                sp.dma_start(w_raw[:, :], d.W).then_inc(par_loaded, 16)
                sp.dma_start(s.cst[:, :], d.cst).then_inc(par_loaded, 16)
                sp.dma_start(att[:, 0:1], d.att_src.rearrange("h (e o) -> (h e) o", o=1)).then_inc(par_loaded, 16)
                sp.dma_start(att[:, 1:2], d.att_dst.rearrange("h (e o) -> (h e) o", o=1)).then_inc(par_loaded, 16)
                sp.dma_start(pw_raw[:, :], d.proj_W).then_inc(par_loaded, 16)
                sp.dma_start(gbias[:, :], d.gat_bias.rearrange("(e o) -> e o", o=1)).then_inc(par_loaded, 16)
                sp.dma_start(pbias[:, :], d.proj_b.rearrange("(o e) -> o e", o=1)).then_inc(par_loaded, 16)
                sp.dma_start(s.steps[:, :], d.steps).then_inc(par_loaded, 16)
                sp.wait_ge(x_cleared, 1)
                sp.dma_start(s.x_sb[:, 0:z.FULL, :],
                             d.x[0:z.FULL * P, :].rearrange("(b p) e -> p b e", p=P)).then_inc(x_loaded, 16)
                if z.REST:
                    sp.dma_start(s.x_sb[0:z.REST, z.FULL, :], d.x[z.FULL * P:z.N, :]).then_inc(x_loaded, 16)
                row = lambda v: v.rearrange("(o e) -> o e", o=1)
                for n, (w, b) in enumerate(((d.Wk, d.bk), (d.Wv, d.bv), (d.Wq, d.bq))):
                    sp.dma_start(s.w_kvq[0:D, n * D:(n + 1) * D], w).then_inc(par_more, 16)
                    sp.dma_start(s.w_kvq[D:D + 1, n * D:(n + 1) * D], row(b)).then_inc(par_more, 16)
                sp.dma_start(s.w_e[0:D, :], d.We).then_inc(par_more, 16)
                sp.dma_start(s.w_e[D:D + 1, :], row(d.be)).then_inc(par_more, 16)
                sp.dma_start(s.ln_g[:, :], row(d.ln_g).to_broadcast([P, D])).then_inc(par_more, 16)
                sp.dma_start(s.ln_b[:, :], row(d.ln_b).to_broadcast([P, D])).then_inc(par_more, 16)
                sp.wait_ge(bias_made, 1)
                sp.dma_start(s.w_proj[D:D + 1, :], bias2[:, :]).then_inc(par_more, 16)
                sp.wait_ge(x_loaded, 16 * (1 + bool(z.REST)))
                sp.wait_ge(par_more, 16 * N_MORE)

            @block.scalar
            def _(act):
                act.wait_ge(cleared, 3)
                n_loads = 0
                for k in range(z.KC):
                    n = min(P, ra - k * P)
                    if n <= 0:
                        break
                    at = k * P * P
                    act.dma_start(dst_i[0:n, k, 0:P], d.dst[at:at + n * P].rearrange("(t e) -> t e", e=P)).then_inc(edges_loaded, 16)
                    act.dma_start(dst_i[0:n, k, P:P + 1],
                                  d.dst[at + P:at + n * P + 1:P].rearrange("(t e) -> t e", e=1),
                                  allow_slow_non_contiguous=True).then_inc(edges_loaded, 16)
                    act.dma_start(src_i[0:n, k, :], d.src[at:at + n * P].rearrange("(t e) -> t e", e=P)).then_inc(edges_loaded, 16)
                    act.dma_start(first_i[0:n, k:k + 1],
                                  d.dst[at:at + (n - 1) * P + 1:P].rearrange("(t e) -> t e", e=1),
                                  allow_slow_non_contiguous=True).then_inc(edges_loaded, 16)
                    n_loads += 4
                act.dma_start(dst_i[lp:lp + 1, lk, :], d.tail).then_inc(tail_loaded, 16)
                act.wait_ge(tail_loaded, 16)
                act.dma_start(dst_i[lp:lp + 1, lk, P - z.TAIL:P],
                              d.dst[z.E - z.TAIL:z.E].rearrange("(o e) -> o e", o=1)).then_inc(edges_loaded, 16)
                act.dma_start(src_i[lp:lp + 1, lk, :],
                              d.src[z.E - P:z.E].rearrange("(o e) -> o e", o=1)).then_inc(edges_loaded, 16)
                act.dma_start(first_i[lp:lp + 1, lk:lk + 1],
                              d.dst[z.E - z.TAIL:z.E - z.TAIL + 1].rearrange("(o e) -> o e", o=1)).then_inc(edges_loaded, 16)
                act.wait_ge(edges_loaded, 16 * (n_loads + 3))
                act.wait_ge(w_turned, 1)
                act.activation(w_t[:, :], ps_w[0:D, 0:D], ACT.Copy).then_inc(w_copied, 1)
                act.wait_ge(p_turned, 1)
                act.activation(s.w_proj[0:D, :], ps_p[0:D, 0:D], ACT.Copy).then_inc(p_copied, 1)

            @block.tensor
            def _(pe):
                pe.wait_ge(par_loaded, 16 * N_PAR)
                pe.transpose(ps_w[0:D, 0:D], w_raw[:, :], s.ident[0:D, 0:D]).then_inc(w_turned, 1)
                pe.transpose(ps_p[0:D, 0:D], pw_raw[:, :], s.ident[0:D, 0:D]).then_inc(p_turned, 1)
                pe.wait_ge(w_copied, 1)
                pe.wait_ge(att_made, 2)
                pe.matmul(ps_a[0:D, 0:2 * H0], w_t[:, :], attm[:, :, :].rearrange("p a h -> p (a h)"),
                          start=True, stop=True).then_inc(comp_done, 1)
                pe.wait_ge(p_copied, 1)
                pe.matmul(ps_b[0:1, 0:D], gbias[:, :], s.w_proj[0:D, :], start=True, stop=True).then_inc(bias_done, 1)

            @block.vector
            def _(dve):
                dve.memset(s.x_t1[:, :, :], 1.0).then_inc(dve_step, 1)
                dve.memset(s.attr_t1[:, :, :], 1.0).then_inc(dve_step, 1)
                dve.wait_ge(par_loaded, 16 * N_PAR)
                dve.tensor_copy(s.w_x[:, 0:D], w_raw[:, :]).then_inc(dve_step, 1)
                for a in range(2):
                    dve.tensor_scalar(attm[:, a, :], s.heads[0:D, :], att[:, a:a + 1], None, ALU.mult).then_inc(att_made, 1)
                dve.wait_ge(edges_loaded, 16 * (4 * (-(-ra // P)) + 3))
                dve.tensor_tensor(down[:, :, :], dst_i[:, :, 0:P], dst_i[:, :, 1:P + 1], ALU.is_gt).then_inc(dve_step, 1)
                dve.wait_ge(dve_step, 4)
                dve.tensor_reduce(down_max[:, :], down[:, :, :].rearrange("p k e -> p (k e)"), AX_X, ALU.max).then_inc(viol_in, 1)
                dve.tensor_scalar(s.dst_f[:, :, :], dst_i[:, :, 0:P], SHIFT, None, ALU.add).then_inc(dve_step, 1)
                dve.tensor_copy(s.src_f[:, :, :], src_i[:, :, :]).then_inc(dve_step, 1)
                dve.tensor_copy(later_i[:, :], dst_i[:, :, P]).then_inc(dve_step, 1)
                dve.wait_ge(dve_step, 7)
                dve.tensor_scalar(first_i[:, :], first_i[:, :], 7, None, ALU.arith_shift_right).then_inc(dve_step, 1)
                dve.tensor_scalar(later_i[:, :], later_i[:, :], 7, None, ALU.arith_shift_right).then_inc(dve_step, 1)
                dve.wait_ge(dve_step, 9)
                dve.tensor_copy(s.lo[:, :], first_i[:, :]).then_inc(dve_step, 1)
                dve.tensor_copy(s.hi[:, :], later_i[:, :]).then_inc(dve_step, 1)
                dve.wait_ge(comp_done, 1)
                dve.tensor_copy(s.w_x[:, D:ROW0], ps_a[0:D, 0:2 * H0]).then_inc(dve_step, 1)
                dve.wait_ge(bias_done, 1)
                dve.tensor_tensor(bias2[:, :], ps_b[0:1, 0:D], pbias[:, :], ALU.add).then_inc(bias_made, 1)
                dve.wait_ge(viol_out, 1)
                dve.tensor_scalar(s.is_sorted[:, :], s.viol[:, :], -1.0, 1.0, ALU.mult, ALU.add).then_inc(dve_step, 1)
                dve.tensor_scalar(s.passes[:, :], s.viol[:, :], float(z.NB - 1), 1.0, ALU.mult, ALU.add).then_inc(dve_step, 1)
                dve.wait_ge(dve_step, 14)
                dve.tensor_scalar(s.lo[:, :], s.lo[:, :], s.is_sorted[:, 0:1], None, ALU.mult).then_inc(dve_step, 1)
                dve.tensor_scalar(s.hi[:, :], s.hi[:, :], s.is_sorted[:, 0:1], 1.0, ALU.mult, ALU.add).then_inc(dve_step, 1)
                dve.wait_ge(dve_step, 16)
                dve.tensor_tensor(s.lo[:, :], s.lo[:, :], s.tile_no[:, :], ALU.add).then_inc(dve_step, 1)
                dve.tensor_tensor(s.hi[:, :], s.hi[:, :], s.tile_no[:, :], ALU.add).then_inc(dve_step, 1)
                dve.wait_ge(dve_step, 18)
                dve.tensor_tensor(s.lo[:, :], s.lo[:, :], s.not_first[:, :], ALU.mult).then_inc(dve_step, 1)
                dve.wait_ge(dve_step, 19)


def table_phase(nc, z, d, s):
    with ExitStack() as ctx:
        sb = lambda n, sh, dt=F32: ctx.enter_context(nc.sbuf_tensor(n, sh, dt))
        ps = lambda n: ctx.enter_context(nc.psum_tensor(n, [P, 1024], F32))
        sem = lambda n: ctx.enter_context(nc.semaphore(n))
        x_g = sb("x_g", [P, GRP, D])
        pick = sb("pick", [P, z.KC, z.STEPS])
        row_t = sb("row_t", [1, z.STEPS])
        row_b = s.block_f
        row_e = sb("row_e", [1, z.STEPS])
        neg_p = sb("neg_p", [1, P])
        ext = sb("ext", [P, 2 * H0])
        ext_all = sb("ext_all", [P, 2 * H0])
        spread = sb("spread", [P, H0])
        wide = sb("wide", [P, 2])
        ps_x, ps_h, ps_s, ps_r = ps("ps_x"), ps("ps_h"), ps("ps_s"), ps("ps_r")
        HALF = -(-z.STEPS // 2)
        halves = [(0, HALF), (HALF, z.STEPS - HALF)]
        KL = z.T - (z.KC - 1) * P

        x_copied, x_turned, xt_copied = sem("x_copied"), sem("x_turned"), sem("xt_copied")
        h_done, h_copied, t0_stored = sem("h_done"), sem("h_copied"), sem("t0_stored")
        pick_step, pick_done = sem("pick_step"), sem("pick_done")
        row_done, row_copied, row_step, rel_done, src_done = sem("row_done"), sem("row_copied"), sem("row_step"), sem("rel_done"), sem("src_done")
        srcs_copied, rels_copied = sem("srcs_copied"), sem("rels_copied")
        neg_set, ext_step, ext_in, ext_out = sem("neg_set"), sem("ext_step"), sem("ext_in"), sem("ext_out")
        t0_rows = d.T0.rearrange("(b p) c -> p b c", p=P)

        with nc.Block(no_gpsimd_drain=True) as block:

            @block.sync
            def _(sp):
                with sp.Fori(0, z.NG) as g:
                    sp.wait_ge(h_copied, g + 2)
                    sp.dma_start(t0_rows[:, bass.ds(g * GRP, GRP), :],
                                 s.tab0[:, bass.ds(g * GRP, GRP), 0:GAT0]).then_inc(t0_stored, 16)
                sp.wait_ge(t0_stored, 16 * z.NG)

            @block.scalar
            def _(act):
                act.sem_inc(xt_copied, 1)
                with act.Fori(0, z.NG) as g:
                    act.wait_ge(x_turned, g + 2)
                    act.wait_ge(h_done, g + 1)
                    act.activation(s.x_t[0:D, 0:4 * P], ps_x[0:D, 0:4 * P], ACT.Copy)
                    act.activation(s.x_t[0:D, 4 * P:GRP * P], ps_x[0:D, 4 * P:GRP * P], ACT.Copy).then_inc(xt_copied, 1)
                for n, (at, w) in enumerate(halves):
                    act.wait_ge(src_done, n + 1)
                    act.activation(s.src_idx[:, at:at + w], ps_s[:, 512 * n:512 * n + w], ACT.Copy).then_inc(srcs_copied, 1)
                act.wait_ge(srcs_copied, 2)

            @block.tensor
            def _(pe):
                pe.sem_inc(x_turned, 1)
                pe.sem_inc(h_done, 1)
                with pe.Fori(0, z.NG) as g:
                    pe.wait_ge(x_copied, g + 1)
                    pe.wait_ge(xt_copied, g + 1)
                    for j in range(GRP):
                        last = pe.transpose(ps_x[0:D, j * P:(j + 1) * P], x_g[:, j, :], s.ident[:, :])
                    last.then_inc(x_turned, 1)
                    pe.wait_ge(xt_copied, g + 2)
                    pe.wait_ge(h_copied, g + 1)
                    for j in range(GRP):
                        last = pe.matmul(ps_h[:, j * P:j * P + ROW0], s.x_t[0:D, j * P:(j + 1) * P], s.w_x[:, :],
                                         start=True, stop=True)
                    last.then_inc(h_done, 1)
                rows = [P] * (z.KC - 1) + [KL]
                for n, (at, w) in enumerate(halves):
                    for k in range(z.KC):
                        pe.wait_ge(pick_done, k + 1)
                        last = pe.matmul(ps_r[0:1, 512 * n:512 * n + w], s.tile_no[0:rows[k], k:k + 1],
                                         pick[0:rows[k], k, at:at + w], start=(k == 0), stop=(k == z.KC - 1))
                    last.then_inc(row_done, 1)
                for n, (at, w) in enumerate(halves):
                    for k in range(z.KC):
                        last = pe.matmul(ps_s[:, 512 * n:512 * n + w], s.src_f[0:rows[k], k, :],
                                         pick[0:rows[k], k, at:at + w], start=(k == 0), stop=(k == z.KC - 1))
                    last.then_inc(src_done, 1)
                pe.wait_ge(h_copied, z.NG + 1)
                pe.wait_ge(row_step, 2)
                pe.wait_ge(neg_set, 1)
                for n, (at, w) in enumerate(halves):
                    for k in range(z.KC):
                        pe.matmul(ps_h[:, 512 * n:512 * n + w], s.dst_f[0:rows[k], k, :],
                                  pick[0:rows[k], k, at:at + w], start=(k == 0), stop=False)
                    pe.matmul(ps_h[:, 512 * n:512 * n + w], neg_p[:, :], row_b[:, at:at + w],
                              start=False, stop=True).then_inc(rel_done, 1)

            @block.gpsimd
            def _(pool):
                pool.wait_ge(ext_in, 1)
                pool.partition_all_reduce(ext_all[:, :], ext[:, :], P, RMAX).then_inc(ext_out, 1)

            @block.vector
            def _(dve):
                dve.memset(neg_p[:, :], -float(P)).then_inc(neg_set, 1)
                dve.memset(s.acc[:, :, :], 0.0).then_inc(ext_step, 1)
                dve.memset(s.q_tab[:, :, :, :], 0.0).then_inc(ext_step, 1)
                dve.memset(s.d_tab[:, :, :, :], 0.0).then_inc(ext_step, 1)
                dve.sem_inc(h_copied, 1)
                with dve.Fori(0, z.NG) as g:
                    dve.wait_ge(x_turned, g + 1)
                    dve.tensor_scalar(x_g[:, :, :], s.x_sb[:, bass.ds(g * GRP, GRP), :], 1.0, None, ALU.mult).then_inc(x_copied, 1)
                    dve.wait_ge(h_done, g + 2)
                    hb = ps_h[:, :].rearrange("p (j c) -> p j c", c=P)
                    dve.tensor_scalar(s.tab0[:, bass.ds(g * GRP, 4), :], hb[:, 0:4, 0:ROW0], 1.0, None, ALU.mult)
                    dve.tensor_scalar(s.tab0[:, bass.ds(g * GRP + 4, GRP - 4), :], hb[:, 4:GRP, 0:ROW0], 1.0, None,
                                      ALU.mult).then_inc(h_copied, 1)
                for k in range(z.KC):
                    dve.tensor_scalar(pick[:, k, :], s.steps[:, :], s.hi[:, k:k + 1], None, ALU.is_lt).then_inc(pick_step, 1)
                    dve.wait_ge(pick_step, k + 1)
                    dve.scalar_tensor_tensor(out=pick[:, k, :], in0=s.steps[:, :], scalar=s.lo[:, k:k + 1],
                                             in1=pick[:, k, :], op0=ALU.is_ge, op1=ALU.mult).then_inc(pick_done, 1)
                dve.wait_ge(h_copied, z.NG + 1)
                a_src = s.tab0[:, :, D:D + H0].rearrange("p b h -> p h b")
                dve.tensor_reduce(ext[:, 0:H0], a_src, AX_X, ALU.max).then_inc(ext_step, 1)
                dve.tensor_reduce(spread[:, :], a_src, AX_X, ALU.min).then_inc(ext_step, 1)
                dve.wait_ge(ext_step, 5)
                dve.tensor_scalar(ext[:, H0:2 * H0], spread[:, :], -1.0, None, ALU.mult).then_inc(ext_in, 1)
                dve.wait_ge(ext_in, 1)
                for n, (at, w) in enumerate(halves):
                    dve.wait_ge(row_done, n + 1)
                    dve.tensor_copy(row_t[:, at:at + w], ps_r[0:1, 512 * n:512 * n + w]).then_inc(row_copied, 1)
                dve.wait_ge(row_copied, 2)
                dve.tensor_tensor(row_b[:, :], s.steps[0:1, :], row_t[:, :], ALU.subtract).then_inc(row_step, 1)
                dve.wait_ge(row_step, 1)
                dve.tensor_scalar(row_b[:, :], row_b[:, :], s.is_sorted[0:1, 0:1], None, ALU.mult).then_inc(row_step, 1)
                dve.tensor_scalar(row_e[:, :], row_t[:, :], float(P), float(z.E - P), ALU.mult, ALU.min).then_inc(row_step, 1)
                dve.wait_ge(row_step, 3)
                dve.tensor_copy(s.edge_row[:, :], row_e[:, :]).then_inc(row_step, 1)
                dve.tensor_copy(s.block_row0[:, :], row_b[:, :]).then_inc(row_step, 1)
                dve.wait_ge(row_step, 5)
                dve.tensor_copy(s.block_row[:, :], s.block_row0[:, :]).then_inc(row_step, 1)
                dve.wait_ge(ext_out, 1)
                dve.tensor_tensor(spread[:, :], ext_all[:, 0:H0], ext_all[:, H0:2 * H0], ALU.add).then_inc(row_step, 1)
                dve.tensor_scalar(s.bound[:, :, :], across(ext_all[:, 0:H0], z.NB), 1.0, None, ALU.mult).then_inc(row_step, 1)
                dve.wait_ge(row_step, 8)
                dve.tensor_reduce(wide[:, 0:1], spread[:, :], AX_X, ALU.max).then_inc(row_step, 1)
                dve.wait_ge(row_step, 9)
                dve.tensor_scalar(wide[:, 1:2], wide[:, 0:1], SPREAD_MAX, None, ALU.is_le).then_inc(row_step, 1)
                dve.wait_ge(row_step, 10)
                dve.tensor_scalar(s.is_wide[:, :], wide[:, 1:2], -1.0, 1.0, ALU.mult, ALU.add).then_inc(row_step, 1)
                for n, (at, w) in enumerate(halves):
                    dve.wait_ge(rel_done, n + 1)
                    dve.tensor_scalar(s.rel0[:, at:at + w], ps_h[:, 512 * n:512 * n + w], -SHIFT, None,
                                      ALU.add).then_inc(rels_copied, 1)
                dve.wait_ge(rels_copied, 2)
                dve.tensor_copy(s.rel[:, :], s.rel0[:, :]).then_inc(rels_copied, 1)
                dve.wait_ge(rels_copied, 3)


def shift_phase(nc, z, d, s):
    with ExitStack() as ctx:
        sb = lambda n, sh, dt=F32: ctx.enter_context(nc.sbuf_tensor(n, sh, dt))
        sem = lambda n: ctx.enter_context(nc.semaphore(n))
        ad_c = sb("ad_c", [P, z.NB, 2 * H0])
        rest = sb("rest", [P, z.NB, 2 * H0])
        part = sb("part", [P, z.NB, 2 * H0])
        own = sb("own", [P, z.NB, H0])
        sum_b = sb("sum_b", [P, z.NB, H0])
        sc, own_exp = sem("shift_step"), sem("own_exp")
        a_src, a_dst = s.tab0[:, :, D:D + H0], s.tab0[:, :, D + H0:ROW0]
        with nc.Block(no_gpsimd_drain=True) as block:

            @block.scalar
            def _(act):
                act.wait_ge(sc, 7)
                act.activation(s.acc[:, 0:z.NB, D:D + H0], own[:, :, :], ACT.Exp).then_inc(own_exp, 1)

            @block.vector
            def _(dve):
                dve.tensor_copy(ad_c[:, :, 0:H0], a_dst).then_inc(sc, 1)
                dve.tensor_tensor(sum_b[:, :, :], s.bound[:, :, :], a_dst, ALU.add).then_inc(sc, 1)
                dve.tensor_tensor(own[:, :, :], a_src, a_dst, ALU.add).then_inc(sc, 1)
                dve.wait_ge(sc, 2)
                dve.scalar_tensor_tensor(out=ad_c[:, :, H0:2 * H0], in0=sum_b[:, :, :], scalar=SLOPE,
                                         in1=sum_b[:, :, :], op0=ALU.mult, op1=ALU.max).then_inc(sc, 1)
                dve.wait_ge(sc, 3)
                dve.scalar_tensor_tensor(out=part[:, :, 0:H0], in0=own[:, :, :], scalar=SLOPE,
                                         in1=own[:, :, :], op0=ALU.mult, op1=ALU.max).then_inc(sc, 1)
                dve.wait_ge(sc, 5)
                dve.tensor_tensor(own[:, :, :], part[:, :, 0:H0], ad_c[:, :, H0:2 * H0], ALU.subtract).then_inc(sc, 1)
                dve.tensor_copy(s.d_tab[:, 0:z.NB, 0, :], ad_c[:, :, :]).then_inc(sc, 1)
                dve.wait_ge(sc, 7)
                dve.tensor_tensor(rest[:, :, :], ad_c[:, :, :], s.d_tab[:, 0:z.NB, 0, :], ALU.subtract).then_inc(sc, 1)
                dve.wait_ge(sc, 8)
                dve.tensor_copy(s.d_tab[:, 0:z.NB, 1, :], rest[:, :, :]).then_inc(sc, 1)
                dve.wait_ge(sc, 9)
                dve.tensor_tensor(part[:, :, :], rest[:, :, :], s.d_tab[:, 0:z.NB, 1, :], ALU.subtract).then_inc(sc, 1)
                dve.wait_ge(sc, 10)
                dve.tensor_copy(s.d_tab[:, 0:z.NB, 2, :], part[:, :, :]).then_inc(sc, 1)
                dve.wait_ge(own_exp, 1)
                for h in range(H0):
                    dve.tensor_tensor(s.acc[:, 0:z.NB, h * D0:(h + 1) * D0], s.tab0[:, :, h * D0:(h + 1) * D0],
                                      s.acc[:, 0:z.NB, D + h:D + h + 1].to_broadcast([P, z.NB, D0]),
                                      ALU.mult).then_inc(sc, 1)
                dve.wait_ge(sc, 11 + H0)


def exact_max_phase(nc, z, d, s):
    with ExitStack() as ctx:
        sb = lambda n, sh, dt=F32: ctx.enter_context(nc.sbuf_tensor(n, sh, dt))
        sem = lambda n: ctx.enter_context(nc.semaphore(n))
        idx = sb("mx_idx", [P, 1], I32)
        dst_col = sb("mx_dst", [P, 1])
        rows = sb("mx_rows", [P, GAT0])
        wide_s = sb("mx_wide_s", [P, H0 + 1, P])
        cand = sb("mx_cand", [P, H0, P])
        limit = sb("mx_limit", [P, P])
        a_all = sb("mx_a_all", [P, H0, P])
        dst_all = sb("mx_dst_all", [P, P])
        best = sb("mx_best", [P, H0])
        nb_col = sb("mx_nb", [P, 1])
        dst_abs = sb("mx_dst_abs", [P, z.STEPS])
        pos_p = sb("mx_pos_p", [1, P])
        ps_a = ctx.enter_context(nc.psum_tensor("mx_ps_a", [P, 512], F32))
        ps_d = ctx.enter_context(nc.psum_tensor("mx_ps_d", [P, 512], F32))
        idx_set, landed, spread_set, turned = sem("mx_idx_set"), sem("mx_landed"), sem("mx_spread"), sem("mx_turned")
        step, tile_in = sem("mx_step"), sem("mx_tile_in")
        pos_set, block_out, abs_done = sem("mx_pos_set"), sem("mx_block_out"), sem("mx_abs_done")
        HALF = -(-z.STEPS // 2)
        halves = [(0, HALF), (HALF, z.STEPS - HALF)]
        with nc.Block(no_gpsimd_drain=True) as block:

            @block.gpsimd
            def _(pool):
                wide = pool.value_load(s.is_wide[0:1, 0:1], min_val=0, max_val=1)
                with pool.If(wide != 0):
                    with pool.Fori(0, z.STEPS) as t:
                        pool.wait_ge(idx_set, t + 1)
                        pool.sem_inc(tile_in, 1)
                        pool.indirect_dma_start(rows[:, :], None, d.T0,
                                                bass.IndirectOffsetOnAxis(ap=idx[:, 0:1], axis=0)).then_inc(landed, 16)
                with pool.Else():
                    pool.sem_inc(tile_in, 1)

            @block.tensor
            def _(pe):
                wide = pe.value_load(s.is_wide[0:1, 0:1], min_val=0, max_val=1)
                with pe.If(wide != 0):
                    pe.wait_ge(pos_set, 1)
                    pe.matmul(ps_a[:, 0:HALF], pos_p[:, :], s.block_f[:, 0:HALF], start=True, stop=True)
                    pe.matmul(ps_d[:, 0:z.STEPS - HALF], pos_p[:, :], s.block_f[:, HALF:z.STEPS],
                              start=True, stop=True).then_inc(block_out, 1)
                    with pe.Fori(0, z.STEPS) as t:
                        pe.wait_ge(spread_set, t + 1)
                        for h in range(H0):
                            pe.matmul(ps_a[:, h * P:(h + 1) * P], wide_s[:, h, :], s.ident[:, :], start=True, stop=True)
                        pe.matmul(ps_d[:, 0:P], wide_s[:, H0, :], s.ident[:, :], start=True, stop=True).then_inc(turned, 1)
                with pe.Else():
                    pe.sem_inc(turned, 1)

            @block.vector
            def _(dve):
                wide = dve.value_load(s.is_wide[0:1, 0:1], min_val=0, max_val=1)
                with dve.If(wide != 0):
                    dve.memset(pos_p[:, :], float(P)).then_inc(pos_set, 1)
                    dve.wait_ge(block_out, 1)
                    for (at, w), ps in zip(halves, (ps_a, ps_d)):
                        dve.tensor_tensor(dst_abs[:, at:at + w], s.rel0[:, at:at + w], ps[:, 0:w], ALU.add).then_inc(abs_done, 1)
                    dve.wait_ge(abs_done, 2)
                    dve.tensor_copy(s.bound[:, :, :], s.tab0[:, :, D:D + H0]).then_inc(step, 1)
                    dve.wait_ge(step, 1)
                    PER = 6 + 5 * z.NB
                    with dve.Fori(0, z.STEPS) as t:
                        base = dve.snap(t * PER + 1)
                        dve.tensor_copy(dst_col[:, :], dst_abs[:, bass.ds(t, 1)]).then_inc(step, 1)
                        dve.tensor_copy(idx[:, :], s.src_idx[:, bass.ds(t, 1)]).then_inc(idx_set, 1)
                        dve.wait_ge(landed, t * 16 + 16)
                        for h in range(H0):
                            dve.tensor_scalar(wide_s[:, h, :], rows[:, D + h:D + h + 1].to_broadcast([P, P]), 1.0, None,
                                              ALU.mult).then_inc(step, 1)
                        dve.wait_ge(step, base + 5)
                        dve.tensor_scalar(wide_s[:, H0, :], dst_col[:, 0:1].to_broadcast([P, P]), 1.0, None,
                                          ALU.mult).then_inc(spread_set, 1)
                        dve.wait_ge(turned, t + 1)
                        dve.tensor_copy(a_all[:, :, :].rearrange("p h e -> p (h e)"), ps_a[:, :])
                        dve.tensor_copy(dst_all[:, :], ps_d[:, 0:P]).then_inc(step, 1)
                        with dve.Fori(0, z.NB) as b:
                            at = dve.snap(base + 6 + b * 5)
                            dve.wait_ge(step, at)
                            dve.tensor_copy(nb_col[:, :], s.node_no[:, bass.ds(b, 1)]).then_inc(step, 1)
                            dve.wait_ge(step, at + 1)
                            dve.tensor_scalar(limit[:, :], dst_all[:, :], nb_col[:, 0:1], BIG,
                                              ALU.is_equal, ALU.mult).then_inc(step, 1)
                            dve.wait_ge(step, at + 2)
                            dve.scalar_tensor_tensor(out=cand[:, :, :], in0=across(limit[:, :], H0), scalar=BIG / 2,
                                                     in1=a_all[:, :, :], op0=ALU.subtract, op1=ALU.min).then_inc(step, 1)
                            dve.wait_ge(step, at + 3)
                            dve.tensor_reduce(best[:, :], cand[:, :, :], AX_X, ALU.max).then_inc(step, 1)
                            dve.wait_ge(step, at + 4)
                            dve.tensor_tensor(s.bound[:, bass.ds(b, 1), :].rearrange("p o h -> p (o h)"),
                                              s.bound[:, bass.ds(b, 1), :].rearrange("p o h -> p (o h)"),
                                              best[:, :], ALU.max).then_inc(step, 1)
                        dve.wait_ge(step, base + PER)
                with dve.Else():
                    dve.sem_inc(step, 1)


def edge_phase(nc, z, d, s, layer):
    second = layer == 1
    heads, hd, wide = (H1, D1, ACC1) if second else (H0, D0, ACC0)
    row_w = 2 * D if second else GAT0
    dst_w = D if second else 2 * H0
    table, dst_tab = (d.T1, s.q_tab) if second else (d.T0, s.d_tab)
    acc = s.acc
    with ExitStack() as ctx:
        sb = lambda n, sh, dt=F32: ctx.enter_context(nc.sbuf_tensor(f"{n}{layer}", sh, dt))
        ps = lambda n, sh: ctx.enter_context(nc.psum_tensor(f"{n}{layer}", sh, F32))
        sem = lambda n: ctx.enter_context(nc.semaphore(f"{n}{layer}"))
        idx = sb("idx", [P, RING, QUAD], I32)
        got = sb("got", [P, RING, QUAD, row_w])
        hot = sb("hot", [P, RING, QUAD, P])
        hot_t = sb("hot_t", [P, PAR, QUAD, P], BF16)
        msg = sb("msg", [P, PAR, QUAD, wide])
        sc_a = sb("sc_a", [P, PAR, QUAD, heads])
        sc_b = sb("sc_b", [P, PAR, QUAD, heads])
        sc_c = sb("sc_c", [P, PAR, QUAD, heads])
        sc_d = sb("sc_d", [P, PAR, QUAD, heads])
        ps_hot = ps("ps_hot", [P, PAR, QUAD, P])
        ps_acc = ps("ps_acc", [P, PAR, 512])
        if second:
            prod = sb("prod", [P, PAR, QUAD, D])
            prod_e = sb("prod_e", [P, PAR, QUAD, D])
            attr = sb("attr", [P, RING, QUAD, D])
            attr_t = s.attr_t1[:, :, :].rearrange("p a (j e) -> p a j e", e=P)
            ps_attr = ps("ps_attr", [P, PAR, QUAD, P])
            ps_e = ps("ps_e", [P, 512])
            ps_dst = ps("ps_dst", [P, 1, 512])
        else:
            ps_dst = ps("ps_dst", [P, PAR, 512])
        DST_PAR = 1 if second else PAR
        SCORE0 = 0 if second else PAR

        rows_ready = sem("rows_ready")
        idx_ready = sem("idx_ready")
        gathered = [sem(f"gathered{k}") for k in range(RING)]
        hot_done = sem("hot_done")
        hot_turned = sem("hot_turned")
        hot_t_done = sem("hot_t_done")
        dst_done = sem("dst_done")
        score_done = sem("score_done")
        dst_used = sem("dst_used") if second else score_done
        exp_done = sem("exp_done")
        msg_done = sem("msg_done")
        sum_done = sem("sum_done")
        acc_done = sem("acc_done")
        mid_a, mid_b, mid_c = sem("mid_a"), sem("mid_b"), sem("mid_c")
        pool_go, pass_begun = sem("pool_go"), sem("pass_begun")
        if second:
            attr_in = [sem(f"attr_in{k}") for k in range(RING)]
            attr_turned = sem("attr_turned")
            attr_t_done = sem("attr_t_done")
            e_done = sem("e_done")
            e_used = sem("e_used")

        def in_slots(eng, first, last, slot):
            n_pass = eng.value_load(s.passes[0:1, 0:1], min_val=1, max_val=z.NB)
            with eng.Fori(0, n_pass) as p:
                eng.wait_ge(rows_ready, p * 2 + 2)
                eng.sem_inc(pass_begun, 1)
                base = eng.snap(p * z.NQ)
                rounds = eng.snap(p * z.NIT)
                for q in range(first, RING):
                    slot(q, base, 0, rounds, lambda c, q=q: 0 <= q + c < z.NQ)
                with eng.Fori(1, z.NIT - 1) as it:
                    at = eng.snap(base + it * RING)
                    rd = eng.snap(rounds + it)
                    for k in range(RING):
                        slot(k, at, it, rd, lambda c: True)
                end = z.NIT - 1
                at = eng.snap(base + end * RING)
                rd = eng.snap(rounds + end)
                for k in range(RING + last):
                    slot(k, at, end, rd, lambda c, k=k: 0 <= end * RING + k + c < z.NQ)
                if eng is nc.vector:
                    dve = eng
                    dve.wait_ge(acc_done, (base + z.NQ + PAR) * QUAD)
                    dve.tensor_scalar(s.rel[:, :], s.rel[:, :], -float(P), None, ALU.add).then_inc(rows_ready, 1)
                    dve.tensor_scalar(s.block_row[:, :], s.block_row[:, :], 1, None, ALU.add).then_inc(rows_ready, 1)

        def steps_of(it, n):
            return bass.ds(it * (RING * QUAD) + n * QUAD, QUAD)

        with nc.Block(no_gpsimd_drain=True) as block:

            @block.gpsimd
            def _(pool):
                def slot(k, base, it, rounds, has):
                    pool.wait_ge(idx_ready, base + (k + 1))
                    pool.wait_ge(msg_done, base + (k + 1))
                    pool.sem_inc(pool_go, 1)
                    for j in range(QUAD):
                        pool.indirect_dma_start(got[:, k % RING, j, :], None, table,
                                                bass.IndirectOffsetOnAxis(ap=idx[:, k % RING, j:j + 1], axis=0)
                                                ).then_inc(gathered[k % RING], 16)
                in_slots(pool, 0, 0, slot)

            @block.sync
            def _(sp):
                if not second:
                    return
                regs = [sp.alloc_register(f"edge_at{j}") for j in range(QUAD)]

                def slot(k, base, it, rounds, has):
                    sp.reg_load(regs, s.edge_row[0:1, steps_of(it, k)])
                    sp.wait_ge(attr_turned, base + (k + 1))
                    for j in range(QUAD):
                        at = sp.snap(regs[j], min_val=0, max_val=z.E - P)
                        sp.dma_start(attr[:, k % RING, j, :], d.attr[bass.ds(at, P), :]).then_inc(attr_in[k % RING], 16)
                in_slots(sp, 0, 0, slot)

            @block.scalar
            def _(act):
                act.sem_inc(hot_t_done, PAR)
                if second:
                    act.sem_inc(attr_t_done, PAR)

                def slot(k, base, it, rounds, has):
                    if has(0):
                        n = k
                        act.wait_ge(score_done, base + (n + 1 + SCORE0))
                        act.wait_ge(sum_done, base + (n - PAR + RING + 1))
                        act.activation(msg[:, n % PAR, :, D:wide], sc_c[:, n % PAR, :, :], ACT.Exp).then_inc(exp_done, 1)
                    if has(2):
                        n = k + 2
                        act.wait_ge(hot_turned, base + (n + 1))
                        act.wait_ge(dst_done, base + (n + 1))
                        act.activation(hot_t[:, n % PAR, :, :], ps_hot[:, n % PAR, :, :], ACT.Copy).then_inc(hot_t_done, 1)
                        if second:
                            act.wait_ge(attr_turned, base + (n + RING + 1))
                            act.wait_ge(e_done, base + (n + 1))
                            act.activation(attr_t[0:D, n % PAR, :, :], ps_attr[0:D, n % PAR, :, :],
                                           ACT.Copy).then_inc(attr_t_done, 1)
                in_slots(act, -2, 0, slot)

            @block.tensor
            def _(pe):
                pe.sem_inc(dst_done, PAR)
                pe.sem_inc(sum_done, RING)
                if second:
                    pe.sem_inc(attr_turned, RING)
                    pe.sem_inc(e_done, PAR)
                regs = [pe.alloc_register(f"block_at{layer}_{j}") for j in range(QUAD)]

                def slot(k, base, it, rounds, has):
                    if has(-1):
                        n = k - 1
                        pe.wait_ge(msg_done, base + (n + RING + 1))
                        pe.wait_ge(acc_done, (base + (n + 1)) * QUAD)
                        for j in range(QUAD):
                            last = pe.matmul(ps_acc[:, n % PAR, j * wide:(j + 1) * wide], hot[:, n % RING, j, :],
                                             msg[:, n % PAR, j, :], start=True, stop=True)
                        last.then_inc(sum_done, 1)
                    if has(1):
                        n = k + 1
                        pe.reg_load(regs, s.block_row[0:1, steps_of(it, n)])
                        pe.wait_ge(hot_t_done, base + (n + PAR + 1))
                        pe.wait_ge(dst_used, base + (n + 1))
                        for j in range(QUAD):
                            b = pe.snap(regs[j], min_val=0, max_val=z.BROWS - 1)
                            for c in range(3):
                                last = pe.matmul(ps_dst[:, n % DST_PAR, j * dst_w:(j + 1) * dst_w],
                                                 hot_t[:, n % PAR, j, :],
                                                 dst_tab[:, bass.ds(b, 1), c, :].rearrange("p o e -> p (o e)"),
                                                 start=(c == 0), stop=(c == 2))
                        last.then_inc(dst_done, 1)
                        if second:
                            pe.wait_ge(attr_t_done, base + (n + PAR + 1))
                            pe.wait_ge(e_used, base + (n + 1))
                            for j in range(QUAD):
                                last = pe.matmul(ps_e[:, j * D:(j + 1) * D], attr_t[:, n % PAR, j, :], s.w_e[:, :],
                                                 start=True, stop=True)
                            last.then_inc(e_done, 1)
                    if has(2):
                        n = k + 2
                        pe.wait_ge(hot_done, base + (n + 1))
                        pe.wait_ge(hot_t_done, base + (n + 1))
                        for j in range(QUAD):
                            last = pe.transpose(ps_hot[:, n % PAR, j, :], hot[:, n % RING, j, :], s.ident[:, :])
                        last.then_inc(hot_turned, 1)
                        if second:
                            pe.wait_ge(attr_in[n % RING], (rounds + (n // RING + 1)) * (16 * QUAD))
                            pe.wait_ge(attr_t_done, base + (n + 1))
                            for j in range(QUAD):
                                last = pe.transpose(ps_attr[0:D, n % PAR, j, :], attr[:, n % RING, j, :], s.ident[:, :])
                            last.then_inc(attr_turned, 1)
                in_slots(pe, -2, 1, slot)

            @block.vector
            def _(dve):
                dve.sem_inc(rows_ready, 2)
                dve.sem_inc(msg_done, RING)
                dve.sem_inc(dst_used, DST_PAR)
                dve.sem_inc(acc_done, QUAD * PAR)
                if second:
                    dve.sem_inc(e_used, 1)
                regs = [dve.alloc_register(f"sum_at{layer}_{j}") for j in range(QUAD)]

                def slot(k, base, it, rounds, has):
                    def add(j):
                        if not has(-2):
                            return
                        n = k - 2
                        if j == 0:
                            dve.reg_load(regs, s.block_row[0:1, steps_of(it, n)])
                            dve.wait_ge(sum_done, base + (n + RING + 1))
                        b = dve.snap(regs[j], min_val=0, max_val=z.BROWS - 1)
                        to = acc[:, bass.ds(b, 1), 0:wide].rearrange("p o e -> p (o e)")
                        dve.wait_ge(acc_done, (base + (n + PAR)) * QUAD + j)
                        dve.tensor_tensor(to, to, ps_acc[:, n % PAR, j * wide:(j + 1) * wide], ALU.add).then_inc(acc_done, 1)

                    add(0)
                    add(1)
                    if has(-1):
                        n = k - 1
                        dve.wait_ge(exp_done, base + (n + 1))
                        val = got[:, n % RING, :, D:2 * D] if second else got[:, n % RING, :, 0:D]
                        dve.tensor_tensor(msg[:, n % PAR, :, 0:D].rearrange("p j (h e) -> p j h e", e=hd),
                                          val.rearrange("p j (h e) -> p j h e", e=hd),
                                          over(msg[:, n % PAR, :, D:wide], hd), ALU.mult).then_inc(msg_done, 1)
                    if has(3):
                        n = k + 3
                        dve.tensor_copy(idx[:, n % RING, :], s.src_idx[:, steps_of(it, n)]).then_inc(idx_ready, 1)
                    if has(0):
                        dve.wait_ge(gathered[k % RING], (rounds + (k // RING + 1)) * (16 * QUAD))
                        dve.wait_ge(dst_done, base + (k + PAR + 1))
                        at = ps_dst[:, k % DST_PAR, 0:QUAD * dst_w].rearrange("p (j e) -> p j e", j=QUAD)
                        rows = got[:, k % RING, :, :]
                        par = k % PAR
                        if second:
                            dve.tensor_tensor(prod[:, par, :, :], rows[:, :, 0:D], at, ALU.mult).then_inc(dst_used, 1)
                        else:
                            dve.tensor_tensor(sc_a[:, par, :, :], rows[:, :, D:D + H0], at[:, :, 0:H0], ALU.add).then_inc(mid_a, 1)
                    add(2)
                    if has(0):
                        if second:
                            dve.wait_ge(e_done, base + (k + PAR + 1))
                            dve.wait_ge(dst_used, base + (k + 2))
                            dve.tensor_tensor(prod_e[:, par, :, :], prod[:, par, :, :],
                                              ps_e[:, 0:QUAD * D].rearrange("p (j e) -> p j e", j=QUAD),
                                              ALU.mult).then_inc(e_used, 1)
                        else:
                            dve.wait_ge(mid_a, base + (k + 1))
                            dve.scalar_tensor_tensor(out=sc_b[:, par, :, :], in0=sc_a[:, par, :, :], scalar=SLOPE,
                                                     in1=sc_a[:, par, :, :], op0=ALU.mult, op1=ALU.max).then_inc(mid_b, 1)
                    if has(2):
                        n = k + 2
                        dve.wait_ge(sum_done, base + (n + 1))
                        dve.tensor_tensor(hot[:, n % RING, :, :], across(s.iota[:, :], QUAD),
                                          over(s.rel[:, steps_of(it, n)], P), ALU.is_equal).then_inc(hot_done, 1)
                    if has(0):
                        if second:
                            dve.wait_ge(e_used, base + (k + 2))
                            dve.tensor_reduce(sc_a[:, par, :, :].rearrange("p j h -> p (j h)"),
                                              prod_e[:, par, :, :].rearrange("p j (h e) -> p (j h) e", e=D1),
                                              AX_X, ALU.add).then_inc(mid_a, 1)
                        else:
                            dve.wait_ge(mid_b, base + (k + 1))
                            dve.tensor_tensor(sc_d[:, par, :, :], sc_b[:, par, :, :], at[:, :, H0:2 * H0],
                                              ALU.subtract).then_inc(mid_c, 1)
                    add(3)
                    if has(0):
                        if second:
                            dve.wait_ge(mid_a, base + (k + 1))
                            dve.tensor_scalar(sc_c[:, par, :, :], sc_a[:, par, :, :], 5.0, -5.0,
                                              ALU.min, ALU.max).then_inc(score_done, 1)
                        else:
                            dve.wait_ge(mid_c, base + (k + 1))
                            dve.tensor_scalar(sc_c[:, par, :, :], sc_d[:, par, :, :], 0.0, None,
                                              ALU.min).then_inc(score_done, 1)
                in_slots(dve, -3, 2, slot)


def held(eng, nobody):
    eng.sem_inc(nobody, 1)


def group_slots(eng, n, first, last, slot):
    for g in range(first, 1):
        slot(g, lambda c, g=g: 0 <= g + c < n)
    with eng.Fori(1, n + first) as g:
        slot(g, lambda c: True)
    for g in range(n + first, n + last):
        slot(g, lambda c, g=g: 0 <= g + c < n)


def statistics(dve, v, stats, mean_var, stats_done, nobody, at, var_out, asked):
    for j in range(GRP):
        ins = dve.bn_stats(stats[:, j, :], v[:, j, :])
    ins.then_inc(stats_done, 1)
    dve.wait_ge(stats_done, at * 2 + 1)
    held(dve, nobody)
    for j in range(GRP):
        ins = dve.bn_aggr(mean_var[:, j, :], stats[:, j, :])
    ins.then_inc(stats_done, 1)
    dve.wait_ge(stats_done, at * 2 + 2)
    dve.tensor_scalar(var_out, mean_var[:, :, 1], EPS, None, ALU.add).then_inc(asked, 1)


def scale_and_bias(dve, mean_var, dev, inv, bias, root, inv_done, scaled, at):
    dve.wait_ge(root, at + 1)
    dve.reciprocal(inv, dev).then_inc(inv_done, 1)
    dve.wait_ge(inv_done, at + 1)
    dve.scalar_tensor_tensor(out=bias, in0=mean_var[:, :, 0], scalar=-1.0, in1=inv,
                             op0=ALU.mult, op1=ALU.mult).then_inc(scaled, 1)


def normalize(act, out, v, inv, bias, done):
    for j in range(GRP):
        ins = act.activation(out[:, j, :], v[:, j, :], ACT.Identity, scale=inv[:, j:j + 1], bias=bias[:, j:j + 1])
    ins.then_inc(done, 1)


def middle_phase(nc, z, d, s):
    with ExitStack() as ctx:
        sb = lambda n, sh, dt=F32: ctx.enter_context(nc.sbuf_tensor(f"mid_{n}", sh, dt))
        sem = lambda n: ctx.enter_context(nc.semaphore(f"mid_{n}"))
        inv = sb("inv", [P, GRP, H0])
        agg = sb("agg", [P, GRP, D])
        agg_t = sb("agg_t", [D + 1, GRP * P])
        v1 = sb("v1", [P, GRP, D])
        n1 = sb("n1", [P, GRP, D])
        n1g = sb("n1g", [P, GRP, D])
        xb = sb("xb", [P, GRP, D])
        v2 = sb("v2", [P, GRP, D])
        x1g = sb("x1g", [P, GRP, D])
        stats = [sb(f"stats{n}", [P, GRP, 6]) for n in range(2)]
        mean_var = [sb(f"mean_var{n}", [P, GRP, 2]) for n in range(2)]
        dev = [sb(f"dev{n}", [P, GRP]) for n in range(2)]
        inv_dev = [sb(f"inv_dev{n}", [P, GRP]) for n in range(2)]
        bias = [sb(f"bias{n}", [P, GRP]) for n in range(2)]
        zeros = sb("zeros", [P, GRP])
        kv = sb("kv", [P, GRP, 2 * D])
        q = sb("q", [P, GRP, D])
        q_hi = sb("q_hi", [P, GRP, D], BF16)
        q_r = sb("q_r", [P, GRP, D])
        ps_t = ctx.enter_context(nc.psum_tensor("mid_ps_t", [P, 1024], F32))
        ps_z = ctx.enter_context(nc.psum_tensor("mid_ps_z", [P, 1024], F32))
        ps_k = ctx.enter_context(nc.psum_tensor("mid_ps_k", [P, 4, 512], F32))
        ones_set, nobody = sem("ones_set"), sem("nobody")
        inv_set = sem("inv_set")
        agg_done = sem("agg_done")
        agg_turned, agg_copied = sem("agg_turned"), sem("agg_copied")
        z_done, z_read = sem("z_done"), sem("z_read")
        stats_done = [sem(f"stats_done{n}") for n in range(2)]
        asked = [sem(f"asked{n}") for n in range(2)]
        root = [sem(f"root{n}") for n in range(2)]
        inv_done = [sem(f"inv_done{n}") for n in range(2)]
        scaled = [sem(f"scaled{n}") for n in range(2)]
        normed = [sem(f"normed{n}") for n in range(2)]
        xb_done, g_done, v2_done = sem("xb_done"), sem("g_done"), sem("v2_done")
        x1_turned, x1_copied, x1_kept = sem("x1_turned"), sem("x1_copied"), sem("x1_kept")
        k_done, kv_copied, q_copied, t1_stored = sem("k_done"), sem("kv_copied"), sem("q_copied"), sem("t1_stored")
        split_step, split_done, cleared, q_put = sem("split_step"), sem("split_done"), sem("cleared"), sem("q_put")
        t1_rows = d.T1.rearrange("(b p) c -> p b c", p=P)
        parts = [(0, 4), (4, GRP)]
        NG = z.NG

        def blocks(g, a=0, b=GRP):
            return bass.ds(g * GRP + a, b - a)

        with nc.Block(no_gpsimd_drain=True) as block:

            @block.sync
            def _(sp):
                with sp.Fori(0, NG) as g:
                    sp.wait_ge(kv_copied, g * 2 + 2)
                    sp.dma_start(t1_rows[:, blocks(g), :], kv[:, :, :]).then_inc(t1_stored, 16)
                sp.wait_ge(t1_stored, 16 * (NG + 1))

            @block.scalar
            def _(act):
                act.sem_inc(t1_stored, 16)

                def slot(g, has):
                    if has(2):
                        act.wait_ge(agg_turned, g + 4)
                        act.activation(agg_t[0:D, 0:4 * P], ps_t[0:D, 0:4 * P], ACT.Copy)
                        act.activation(agg_t[0:D, 4 * P:GRP * P], ps_t[0:D, 4 * P:GRP * P], ACT.Copy).then_inc(agg_copied, 1)
                    if has(0):
                        act.wait_ge(asked[1], g + 1)
                        act.activation(dev[1][:, :], dev[1][:, :], ACT.Sqrt).then_inc(root[1], 1)
                    if has(1):
                        act.wait_ge(asked[0], g + 2)
                        act.activation(dev[0][:, :], dev[0][:, :], ACT.Sqrt).then_inc(root[0], 1)
                    if has(0):
                        act.wait_ge(scaled[1], g + 1)
                        act.wait_ge(x1_kept, g + 1)
                        held(act, nobody)
                        normalize(act, x1g, v2, inv_dev[1], bias[1], normed[1])
                    if has(1):
                        act.wait_ge(scaled[0], g + 2)
                        act.wait_ge(g_done, g + 2)
                        held(act, nobody)
                        normalize(act, n1, v1, inv_dev[0], bias[0], normed[0])
                    if has(0):
                        act.wait_ge(x1_turned, g + 1)
                        act.activation(s.x_t1[0:D, 0, 0:4 * P], ps_t[0:D, 0:4 * P], ACT.Copy)
                        act.activation(s.x_t1[0:D, 0, 4 * P:GRP * P], ps_t[0:D, 4 * P:GRP * P], ACT.Copy).then_inc(x1_copied, 1)
                    for n, (a, b) in enumerate(parts):
                        if has(0):
                            act.wait_ge(k_done, g * 2 + (n + 1))
                            if n == 0:
                                act.wait_ge(t1_stored, g * 16 + 16)
                                act.wait_ge(split_done, g + 1)
                            held(act, nobody)
                            act.activation(kv[:, a:b, :], ps_k[:, 0:b - a, 0:2 * D], ACT.Copy).then_inc(kv_copied, 1)
                            for to in (q_hi, q):
                                ins = act.activation(to[:, a:b, :], ps_k[:, 0:b - a, 2 * D:3 * D], ACT.Copy,
                                                     scale=1.0 / float(np.sqrt(D1)))
                            ins.then_inc(q_copied, 1)
                group_slots(act, NG, -3, 0, slot)

            @block.tensor
            def _(pe):
                pe.wait_ge(ones_set, 2)
                pe.sem_inc(agg_turned, 1)

                def slot(g, has):
                    if has(2):
                        pe.wait_ge(agg_done, g + 3)
                        for j in range(GRP):
                            ins = pe.transpose(ps_t[0:D, j * P:(j + 1) * P], agg[:, j, :], s.ident[:, :])
                        ins.then_inc(agg_turned, 1)
                        pe.wait_ge(agg_copied, g + 3)
                        pe.wait_ge(z_read, g + 3)
                        for j in range(GRP):
                            ins = pe.matmul(ps_z[:, j * P:j * P + D], agg_t[:, j * P:(j + 1) * P], s.w_proj[:, :],
                                            start=True, stop=True)
                        ins.then_inc(z_done, 1)
                    if has(0):
                        pe.wait_ge(normed[1], g + 1)
                        for j in range(GRP):
                            ins = pe.transpose(ps_t[0:D, j * P:(j + 1) * P], x1g[:, j, :], s.ident[:, :])
                        ins.then_inc(x1_turned, 1)
                        pe.wait_ge(x1_copied, g + 1)
                        for n, (a, b) in enumerate(parts):
                            if n:
                                pe.wait_ge(q_copied, g * 2 + n)
                            for j in range(a, b):
                                ins = pe.matmul(ps_k[:, j - a, 0:3 * D], s.x_t1[:, 0, j * P:(j + 1) * P],
                                                s.w_kvq[:, :], start=True, stop=True)
                            ins.then_inc(k_done, 1)
                group_slots(pe, NG, -3, 0, slot)

            @block.gpsimd
            def _(pool):
                pool.sem_inc(split_done, 1)
                pool.sem_inc(x1_kept, 1)

                def slot(g, has):
                    if has(1):
                        pool.wait_ge(v2_done, g + 2)
                        held(pool, nobody)
                        pool.tensor_tensor(xb[:, :, :], s.x_sb[:, blocks(g + 1), :], across(s.ln_b[:, :], GRP),
                                           ALU.add).then_inc(xb_done, 1)
                    if has(0):
                        pool.wait_ge(x1_turned, g + 1)
                        held(pool, nobody)
                        pool.tensor_copy(s.x1[:, blocks(g), :], x1g[:, :, :]).then_inc(x1_kept, 1)
                        pool.wait_ge(q_copied, g * 2 + 2)
                        pool.wait_ge(q_put, g + 1)
                        held(pool, nobody)
                        to = s.q_tab[:, blocks(g), :, :]
                        pool.tensor_tensor(to[:, :, 1, :], q[:, :, :], q_hi[:, :, :], ALU.subtract)
                        pool.tensor_tensor(q_r[:, :, :], q[:, :, :], q_hi[:, :, :], ALU.subtract).then_inc(split_step, 1)
                        pool.wait_ge(split_step, g + 1)
                        held(pool, nobody)
                        pool.tensor_tensor(to[:, :, 2, :], q_r[:, :, :], to[:, :, 1, :], ALU.subtract).then_inc(split_done, 1)
                group_slots(pool, NG, -3, 0, slot)
                pool.wait_ge(split_done, NG + 1)
                pool.wait_ge(x1_kept, NG + 1)

            @block.vector
            def _(dve):
                dve.memset(agg_t[:, :], 1.0).then_inc(ones_set, 1)
                dve.memset(zeros[:, :], 0.0).then_inc(ones_set, 1)
                dve.tensor_copy(s.rel[:, :], s.rel0[:, :]).then_inc(ones_set, 1)
                dve.tensor_copy(s.block_row[:, :], s.block_row0[:, :]).then_inc(ones_set, 1)
                dve.sem_inc(g_done, 1)
                dve.sem_inc(v2_done, 1)
                dve.sem_inc(z_read, 1)
                dve.wait_ge(ones_set, 2)

                def slot(g, has):
                    if has(0):
                        dve.wait_ge(normed[0], g + 1)
                        dve.tensor_tensor(n1g[:, :, :], n1[:, :, :], across(s.ln_g[:, :], GRP), ALU.mult).then_inc(g_done, 1)
                        dve.wait_ge(g_done, g + 2)
                        dve.wait_ge(xb_done, g + 1)
                        dve.tensor_tensor(v2[:, :, :], n1g[:, :, :], xb[:, :, :], ALU.add).then_inc(v2_done, 1)
                        dve.wait_ge(v2_done, g + 2)
                        statistics(dve, v2, stats[1], mean_var[1], stats_done[1], nobody, g, dev[1][:, :], asked[1])
                    if has(1):
                        dve.wait_ge(z_done, g + 2)
                        for a, b in parts:
                            ins = dve.tensor_tensor(v1[:, a:b, :], s.x_sb[:, blocks(g + 1, a, b), :],
                                                    ps_z[:, :].rearrange("p (j c) -> p j c", c=P)[:, a:b, 0:D], ALU.add)
                        ins.then_inc(z_read, 1)
                        dve.wait_ge(z_read, g + 3)
                        statistics(dve, v1, stats[0], mean_var[0], stats_done[0], nobody, g + 1, dev[0][:, :], asked[0])
                    if has(-1):
                        dve.wait_ge(q_copied, g * 2)
                        dve.tensor_scalar(s.q_tab[:, blocks(g - 1), 0, :], q_hi[:, :, :], 1.0, None, ALU.mult).then_inc(q_put, 1)
                    if has(0):
                        scale_and_bias(dve, mean_var[1], dev[1][:, :], inv_dev[1][:, :], bias[1][:, :], root[1],
                                       inv_done[1], scaled[1], g)
                    if has(1):
                        scale_and_bias(dve, mean_var[0], dev[0][:, :], inv_dev[0][:, :], bias[0][:, :], root[0],
                                       inv_done[0], scaled[0], g + 1)
                    if has(3):
                        dve.reciprocal(inv[:, :, :], s.acc[:, blocks(g + 3), D:ACC0]).then_inc(inv_set, 1)
                        dve.wait_ge(inv_set, g + 4)
                        dve.wait_ge(agg_turned, g + 4)
                        dve.tensor_tensor(agg[:, :, :].rearrange("p j (h e) -> p j h e", e=D0),
                                          s.acc[:, blocks(g + 3), 0:D].rearrange("p j (h e) -> p j h e", e=D0),
                                          over(inv[:, :, :], D0), ALU.mult).then_inc(agg_done, 1)
                        dve.wait_ge(agg_done, g + 4)
                        dve.tensor_scalar(s.acc[:, blocks(g + 3), :], over(zeros[:, :], ACC1), 1.0, None,
                                          ALU.mult).then_inc(cleared, 1)
                group_slots(dve, NG, -3, 1, slot)
                dve.wait_ge(cleared, NG)


def last_phase(nc, z, d, s):
    with ExitStack() as ctx:
        sb = lambda n, sh, dt=F32: ctx.enter_context(nc.sbuf_tensor(f"end_{n}", sh, dt))
        sem = lambda n: ctx.enter_context(nc.semaphore(f"end_{n}"))
        den = sb("den", [P, GRP, H1])
        inv = sb("inv", [P, GRP, H1])
        out1 = sb("out1", [P, GRP, D])
        v = sb("v", [P, PAR, GRP, D])
        stats = sb("stats", [P, GRP, 6])
        mean_var = sb("mean_var", [P, PAR, GRP, 2])
        dev = sb("dev", [P, GRP])
        inv_dev = sb("inv_dev", [P, GRP])
        bias = sb("bias", [P, GRP])
        step, stats_done, asked, root, nobody = sem("step"), sem("stats_done"), sem("asked"), sem("root"), sem("nobody")
        inv_done, scaled, y_done, stored = sem("inv_done"), sem("scaled"), sem("y_done"), sem("stored")
        blocks = lambda g: bass.ds(g * GRP, GRP) if not isinstance(g, int) else slice(g * GRP, (g + 1) * GRP)
        with nc.Block(no_gpsimd_drain=True) as block:

            @block.scalar
            def _(act):
                for g in range(z.NG):
                    act.wait_ge(asked, g + 1)
                    act.activation(dev[:, :], dev[:, :], ACT.Sqrt).then_inc(root, 1)
                    act.wait_ge(scaled, g + 1)
                    normalize(act, s.x_sb[:, blocks(g), :], v[:, g % PAR, :, :], inv_dev, bias, y_done)

            @block.vector
            def _(dve):
                for g in range(-1, z.NG):
                    if g + 1 < z.NG:
                        n = g + 1
                        dve.tensor_scalar(den[:, :, :], s.acc[:, blocks(n), D:ACC1], 1e-6, None, ALU.add).then_inc(step, 1)
                        dve.wait_ge(step, 4 * n + 1)
                        dve.reciprocal(inv[:, :, :], den[:, :, :]).then_inc(step, 1)
                        dve.wait_ge(step, 4 * n + 2)
                        dve.tensor_tensor(out1[:, :, :].rearrange("p j (h e) -> p j h e", e=D1),
                                          s.acc[:, blocks(n), 0:D].rearrange("p j (h e) -> p j h e", e=D1),
                                          over(inv[:, :, :], D1), ALU.mult).then_inc(step, 1)
                        dve.wait_ge(step, 4 * n + 3)
                        if n >= PAR:
                            dve.wait_ge(y_done, n - 1)
                        dve.tensor_tensor(v[:, n % PAR, :, :], s.x1[:, blocks(n), :], out1[:, :, :], ALU.add).then_inc(step, 1)
                        dve.wait_ge(step, 4 * n + 4)
                    if g >= 0:
                        dve.wait_ge(y_done, g) if g else None
                        scale_and_bias(dve, mean_var[:, g % PAR, :, :], dev[:, :], inv_dev[:, :], bias[:, :], root,
                                       inv_done, scaled, g)
                    if g + 1 < z.NG:
                        n = g + 1
                        statistics(dve, v[:, n % PAR, :, :], stats, mean_var[:, n % PAR, :, :], stats_done, nobody, n,
                                   dev[:, :], asked)

            @block.sync
            def _(sp):
                n_stores = 0
                for g in range(z.NG):
                    a, b = g * GRP, min((g + 1) * GRP, z.FULL)
                    sp.wait_ge(y_done, g + 1)
                    if b > a:
                        sp.dma_start(d.out[a * P:b * P, :].rearrange("(b p) e -> p b e", p=P),
                                     s.x_sb[:, a:b, :]).then_inc(stored, 16)
                        n_stores += 1
                    if z.REST and g * GRP <= z.FULL < (g + 1) * GRP:
                        sp.dma_start(d.out[z.FULL * P:z.N, :], s.x_sb[0:z.REST, z.FULL, :]).then_inc(stored, 16)
                        n_stores += 1
                sp.wait_ge(stored, 16 * n_stores)


def build(nc, z, d, where):
    d.T0 = nc.dram_tensor("T0", [z.NB * P, GAT0], F32).ap()
    d.T1 = nc.dram_tensor("T1", [z.NB * P, 2 * D], F32).ap()
    with ExitStack() as ctx:
        def sb(name, shape, dt=F32):
            return ctx.enter_context(nc.sbuf_tensor(name, shape, dt))

        s = Bag()
        s.cst = sb("cst", [P, where[-1][1]])
        s.ident, s.iota, s.tile_no, s.not_first, s.heads, s.node_no = (s.cst[:, a:b] for a, b in where)
        s.x_sb = sb("x_sb", [P, z.NB, D])
        s.acc = sb("acc", [P, z.BROWS, ACC1])
        s.q_tab = sb("q_tab", [P, z.BROWS, 3, D], BF16)
        s.d_tab = sb("d_tab", [P, z.BROWS, 3, 2 * H0], BF16)
        s.w_kvq = sb("w_kvq", [D + 1, 3 * D])
        s.w_e = sb("w_e", [D + 1, D])
        s.w_proj = sb("w_proj", [D + 1, D])
        s.ln_g = sb("ln_g", [P, D])
        s.ln_b = sb("ln_b", [P, D])
        s.x_t1 = sb("x_t1", [D + 1, 1, GRP * P])
        s.attr_t1 = sb("attr_t1", [D + 1, PAR, QUAD * P])
        s.x_t = s.x_t1[:, 0, :]
        s.src_idx = sb("src_idx", [P, z.STEPS], I32)
        s.rel0 = sb("rel0", [P, z.STEPS])
        s.rel = sb("rel", [P, z.STEPS])
        s.block_f = sb("block_f", [1, z.STEPS])
        s.block_row0 = sb("block_row0", [1, z.STEPS], I32)
        s.block_row = sb("block_row", [1, z.STEPS], I32)
        s.edge_row = sb("edge_row", [1, z.STEPS], I32)
        s.viol = sb("viol", [P, 1])
        s.is_sorted = sb("is_sorted", [P, 1])
        s.passes = sb("passes", [P, 1], I32)
        s.is_wide = sb("is_wide", [P, 1], I32)
        with nc.sbuf_tensor("tab0", [P, z.NB, ROW0], F32) as s.tab0, nc.sbuf_tensor("bound", [P, z.NB, H0], F32) as s.bound:
            with ExitStack() as early:
                eb = lambda n, sh: early.enter_context(nc.sbuf_tensor(n, sh, F32))
                s.steps = eb("steps", [P, z.STEPS])
                s.w_x = eb("w_x", [D, ROW0])
                s.dst_f = eb("dst_f", [P, z.KC, P])
                s.src_f = eb("src_f", [P, z.KC, P])
                s.lo = eb("lo", [P, z.KC])
                s.hi = eb("hi", [P, z.KC])
                load_phase(nc, z, d, s, where)
                table_phase(nc, z, d, s)
            exact_max_phase(nc, z, d, s)
            shift_phase(nc, z, d, s)
        edge_phase(nc, z, d, s, 0)
        s.x1 = sb("x1", [P, z.NB, D])
        middle_phase(nc, z, d, s)
        edge_phase(nc, z, d, s, 1)
        last_phase(nc, z, d, s)


_INS = ['x', 'src', 'dst', 'edge_attr_96', 'L0_gnn_W', 'L0_gnn_att_src', 'L0_gnn_att_dst', 'L0_gnn_gat_bias',
        'L0_gnn_proj_W', 'L0_gnn_proj_b', 'L0_gnn_ln_g', 'L0_gnn_ln_b', 'L1_gnn_Wq', 'L1_gnn_bq', 'L1_gnn_Wk',
        'L1_gnn_bk', 'L1_gnn_We', 'L1_gnn_be', 'L1_gnn_Wv', 'L1_gnn_bv']


def program(nc, inputs):
    z = sizes(inputs['x'].shape[0], inputs['src'].shape[0])
    table, where, steps, tail = constants(z)
    arrays = {name: np.ascontiguousarray(inputs[name]) for name in _INS}
    arrays |= {'cst': table, 'steps': steps, 'tail': tail}

    def given(name):
        a = arrays[name]
        return nc.dram_tensor(f"in_{name}_dram", a.shape, mybir.dt.from_np(a.dtype), kind="ExternalInput").ap()

    d = Bag()
    d.x, d.src, d.dst, d.attr = (given(n) for n in _INS[:4])
    d.W, d.att_src, d.att_dst, d.gat_bias, d.proj_W, d.proj_b, d.ln_g, d.ln_b = (given(n) for n in _INS[4:12])
    d.Wq, d.bq, d.Wk, d.bk, d.We, d.be, d.Wv, d.bv = (given(n) for n in _INS[12:])
    d.cst, d.steps, d.tail = given('cst'), given('steps'), given('tail')
    d.out = nc.dram_tensor("out_0_dram", (z.N, D), F32, kind="ExternalOutput").ap()
    build(nc, z, d, where)
    return {f"in_{name}_dram": a for name, a in arrays.items()}


def kernel(**inputs):
    import concourse.bacc as _bacc
    from concourse.bass_utils import run_bass_kernel_spmd as _run

    nc = _bacc.Bacc("TRN2", target_bir_lowering=False, num_devices=1)
    arrays = program(nc, inputs)
    r = _run(nc, [arrays], core_ids=[0])
    return r.results[0]["out_0_dram"]
```

```python
from contextlib import ExitStack

import concourse.bass as bass
import numpy as np
from concourse import mybir


class Bag:
    pass


F32 = mybir.dt.float32
BF16 = mybir.dt.bfloat16
I32 = mybir.dt.int32
ALU = mybir.AluOpType
ACT = mybir.ActivationFunctionType
AX_X = mybir.AxisListType.X
RMAX = bass.bass_isa.ReduceOp.max

P = 128
D = 96
H0, D0 = 4, 24
H1, D1 = 8, 12
SLOPE, EPS = 0.2, 1e-5
ROW0 = D + 2 * H0
GAT0 = D + H0
ACC0 = D + H0
ACC1 = D + H1
QUAD = 4
RING = 4
PAR = 2
GRP = 7
SHIFT = 8192.0
BIG = 3e38
SPREAD_MAX = 60.0
LAST_DST = 1 << 20


def sizes(n_nodes, n_edges):
    z = Bag()
    z.N, z.E = n_nodes, n_edges
    z.NB = -(-n_nodes // (P * GRP)) * GRP
    z.FULL = n_nodes // P
    z.REST = n_nodes - z.FULL * P
    z.NG = z.NB // GRP
    z.T = -(-n_edges // P)
    z.TAIL = n_edges - (z.T - 1) * P
    z.KC = -(-z.T // P)
    body = QUAD * RING
    z.NIT = -(-(z.T + z.NB - 1) // body)
    z.NQ = z.NIT * RING
    z.STEPS = z.NIT * body
    z.BROWS = z.STEPS - z.T + 2
    assert z.BROWS >= z.NB and z.NIT >= 3 and z.STEPS <= 1024
    return z


def constants(z):
    part = np.arange(P, dtype=np.float32)[:, None]
    tile = part + P * np.arange(z.KC, dtype=np.float32)[None, :]
    heads = (np.arange(P)[:, None] // D0 == np.arange(H0)[None, :]).astype(np.float32)
    cols = [
        np.eye(P, dtype=np.float32),
        np.tile(np.arange(P, dtype=np.float32)[None, :], (P, 1)),
        tile,
        (tile > 0).astype(np.float32),
        heads,
        part + P * np.arange(z.NB, dtype=np.float32)[None, :],
    ]
    at, where = 0, []
    for c in cols:
        where.append((at, at + c.shape[1]))
        at += c.shape[1]
    steps = np.tile(np.arange(z.STEPS, dtype=np.float32)[None, :], (P, 1))
    tail = np.full((1, P + 1), -1, np.int32)
    tail[0, P] = LAST_DST
    return np.ascontiguousarray(np.concatenate(cols, 1)), where, steps, tail


def over(ap, n):
    return ap.unsqueeze(len(ap.shape)).to_broadcast([*ap.shape, n])


def across(ap, n):
    return ap.unsqueeze(1).to_broadcast([ap.shape[0], n, ap.shape[1]])


def held(eng, nobody):
    eng.sem_inc(nobody, 1)


def first_phase(nc, z, d, s):
    with ExitStack() as ctx:
        sb = lambda n, sh, dt=F32: ctx.enter_context(nc.sbuf_tensor(n, sh, dt))
        sem = lambda n: ctx.enter_context(nc.semaphore(n))
        steps = sb("steps", [P, z.STEPS])
        w_raw = sb("w_raw", [D, D])
        pw_raw = sb("pw_raw", [D, D])
        att = sb("att", [D, 2])
        attm = sb("attm", [D, 2, H0])
        gbias = sb("gbias", [D, 1])
        pbias = sb("pbias", [1, D])
        bias2 = sb("bias2", [1, D])
        w_t = sb("w_t", [D, D])
        w_x = sb("w_x", [D, ROW0])
        x_g = sb("x_g", [P, GRP, D])
        dst_i = sb("dst_i", [P, z.KC, P + 1], I32)
        src_i = sb("src_i", [P, z.KC, P], I32)
        first_i = sb("first_i", [P, z.KC], I32)
        later_i = sb("later_i", [P, z.KC], I32)
        dst_f = sb("dst_f", [P, z.KC, P])
        src_f = sb("src_f", [P, z.KC, P])
        down = sb("down", [P, z.KC, P])
        down_max = sb("down_max", [P, 1])
        lo = sb("lo", [P, z.KC])
        hi = sb("hi", [P, z.KC])
        windows = [(k * P, min(z.STEPS, (k + 1) * P + z.NB)) for k in range(z.KC - 1)] + [((z.KC - 1) * P, z.STEPS)]
        WIN = max(b - a for a, b in windows)
        pick = sb("pick", [P, z.KC, WIN])
        row_t = sb("row_t", [1, z.STEPS])
        row_b = s.block_f
        row_e = sb("row_e", [1, z.STEPS])
        neg_p = sb("neg_p", [1, P])
        ext = sb("ext", [P, 2 * H0])
        ext_all = sb("ext_all", [P, 2 * H0])
        spread = sb("spread", [P, H0])
        wide = sb("wide", [P, 2])
        ps = lambda n: ctx.enter_context(nc.psum_tensor(n, [P, 1024], F32))
        ps_x, ps_h, ps_s, ps_r = ps("ps_x"), ps("ps_h"), ps("ps_s"), ps("ps_r")
        ps_w, ps_a, ps_p, ps_b = ps_r[:, 0:512], ps_r[:, 512:1024], ps_s[:, 0:512], ps_s[:, 512:1024]

        w_loaded = sem("w_loaded")
        EARLY = z.NG // 2
        x_cuts = [(0, EARLY * GRP), (EARLY * GRP, z.FULL)]
        x_loaded, x_cleared = [sem(f"x_loaded_{n}") for n in range(2)], sem("x_cleared")
        par_loaded = sem("par_loaded")
        par_more = sem("par_more")
        cleared = sem("cleared")
        edges_loaded = sem("edges_loaded")
        tail_loaded = sem("tail_loaded")
        w_turned, w_copied = sem("w_turned"), sem("w_copied")
        p_turned, p_copied = sem("p_turned"), sem("p_copied")
        att_made, comp_done, w_x_made = sem("att_made"), sem("comp_done"), sem("w_x_made")
        bias_done, bias_made = sem("bias_done"), sem("bias_made")
        dve_step = sem("dve_step")
        viol_in, viol_out = sem("viol_in"), sem("viol_out")
        parts = [(0, 4), (4, GRP)]
        both = lambda n: [sem(f"{n}_{i}") for i in range(2)]
        x_copied, x_turned, xt_copied = both("x_copied"), both("x_turned"), both("xt_copied")
        h_done, h_copied = both("h_done"), both("h_copied")
        t0_stored, nobody = sem("t0_stored"), sem("nobody0")
        pick_step, pick_done = sem("pick_step"), sem("pick_done")
        row_done, row_copied, row_step, rel_done, src_done = sem("row_done"), sem("row_copied"), sem("row_step"), sem("rel_done"), sem("src_done")
        srcs_copied, rels_copied = sem("srcs_copied"), sem("rels_copied")
        neg_set, ext_step, ext_in, ext_out = sem("neg_set"), sem("ext_step"), sem("ext_in"), sem("ext_out")
        t0_rows = d.T0.rearrange("(b p) c -> p b c", p=P)

        ra = z.T - 1
        lp, lk = ra % P, ra // P
        spans = [(k0, k1, n) for k0, k1, n in ((0, lk, P), (lk, lk + 1, lp)) if k1 > k0 and n > 0]
        N_EDGE = 4 * len(spans) + 3
        banks = [(0, min(512, z.STEPS))] + ([(512, z.STEPS - 512)] if z.STEPS > 512 else [])
        KL = z.T - (z.KC - 1) * P

        def staircase(pe, out, value, bank, stop, done):
            at, w = bank
            jobs = [(k, a, min(a + P, at + w, windows[k][1]))
                    for m, a in enumerate(range(0, z.STEPS, P)) if at <= a < at + w
                    for k in range(min(m, z.KC - 1), -1, -1) if windows[k][1] > a]
            for n, (k, a, end) in enumerate(jobs):
                rows = KL if k == z.KC - 1 else P
                pe.wait_ge(pick_done, k + 1)
                last = pe.matmul(out[:, a:end], value(rows, k), pick[0:rows, k, a - k * P:end - k * P],
                                 start=(n == 0), stop=(stop and n == len(jobs) - 1))
            if done:
                last.then_inc(done, 1)

        with nc.Block(no_gpsimd_drain=True) as block:

            @block.sync
            def _(sp):
                row = lambda v: v.rearrange("(o e) -> o e", o=1)
                sp.dma_start(w_raw[:, :], d.W).then_inc(w_loaded, 16)
                sp.dma_start(s.cst[:, :], d.cst).then_inc(w_loaded, 16)
                sp.dma_start(att[:, 0:1], d.att_src.rearrange("h (e o) -> (h e) o", o=1)).then_inc(w_loaded, 16)
                sp.dma_start(att[:, 1:2], d.att_dst.rearrange("h (e o) -> (h e) o", o=1)).then_inc(w_loaded, 16)
                for n, (a, b) in enumerate(x_cuts):
                    sp.dma_start(s.x_sb[:, a:b, :],
                                 d.x[a * P:b * P, :].rearrange("(b p) e -> p b e", p=P)).then_inc(x_loaded[n], 16)
                sp.wait_ge(x_cleared, 1)
                if z.REST:
                    sp.dma_start(s.x_sb[0:z.REST, z.FULL, :], d.x[z.FULL * P:z.N, :]).then_inc(x_loaded[-1], 16)
                sp.dma_start(pw_raw[:, :], d.proj_W).then_inc(par_loaded, 16)
                sp.dma_start(gbias[:, :], d.gat_bias.rearrange("(e o) -> e o", o=1)).then_inc(par_loaded, 16)
                sp.dma_start(pbias[:, :], row(d.proj_b)).then_inc(par_loaded, 16)
                sp.dma_start(steps[:, :], d.steps).then_inc(par_loaded, 16)
                for n, (w, b) in enumerate(((d.Wk, d.bk), (d.Wv, d.bv), (d.Wq, d.bq))):
                    sp.dma_start(s.w_kvq[0:D, n * D:(n + 1) * D], w).then_inc(par_more, 16)
                    sp.dma_start(s.w_kvq[D:D + 1, n * D:(n + 1) * D], row(b)).then_inc(par_more, 16)
                sp.dma_start(s.w_e[0:D, :], d.We).then_inc(par_more, 16)
                sp.dma_start(s.w_e[D:D + 1, :], row(d.be)).then_inc(par_more, 16)
                sp.dma_start(s.ln_g[:, :], row(d.ln_g).to_broadcast([P, D])).then_inc(par_more, 16)
                sp.dma_start(s.ln_b[:, :], row(d.ln_b).to_broadcast([P, D])).then_inc(par_more, 16)
                sp.wait_ge(tail_loaded, 16)
                sp.dma_start(dst_i[lp:lp + 1, lk, P - z.TAIL:P],
                             d.dst[z.E - z.TAIL:z.E].rearrange("(o e) -> o e", o=1)).then_inc(edges_loaded, 16)
                with sp.Fori(0, z.NG) as g:
                    for n in range(2):
                        sp.wait_ge(h_copied[n], g + 2)
                    sp.dma_start(t0_rows[:, bass.ds(g * GRP, GRP), :],
                                 s.tab0[:, bass.ds(g * GRP, GRP), 0:GAT0]).then_inc(t0_stored, 16)
                sp.wait_ge(bias_made, 1)
                sp.dma_start(s.w_proj[D:D + 1, :], bias2[:, :]).then_inc(par_more, 16)
                sp.wait_ge(par_more, 16 * 11)
                sp.wait_ge(t0_stored, 16 * z.NG)

            @block.scalar
            def _(act):
                act.wait_ge(cleared, 3)
                for k0, k1, n in spans:
                    at, to = k0 * P * P, (k0 * P + (k1 - k0 - 1) * P + n) * P
                    tiles = lambda v: v.rearrange("(k t e) -> t k e", k=k1 - k0, t=n)
                    act.dma_start(dst_i[0:n, k0:k1, 0:P], tiles(d.dst[at:to])).then_inc(edges_loaded, 16)
                    act.dma_start(dst_i[0:n, k0:k1, P:P + 1], tiles(d.dst[at + P:to + 1:P]),
                                  allow_slow_non_contiguous=True).then_inc(edges_loaded, 16)
                    act.dma_start(src_i[0:n, k0:k1, :], tiles(d.src[at:to])).then_inc(edges_loaded, 16)
                    act.dma_start(first_i[0:n, k0:k1].unsqueeze(2), tiles(d.dst[at:to - P + 1:P]),
                                  allow_slow_non_contiguous=True).then_inc(edges_loaded, 16)
                act.dma_start(src_i[lp:lp + 1, lk, :],
                              d.src[z.E - P:z.E].rearrange("(o e) -> o e", o=1)).then_inc(edges_loaded, 16)
                act.dma_start(first_i[lp:lp + 1, lk:lk + 1],
                              d.dst[z.E - z.TAIL:z.E - z.TAIL + 1].rearrange("(o e) -> o e", o=1)).then_inc(edges_loaded, 16)
                act.dma_start(dst_i[lp:lp + 1, lk, :], d.tail).then_inc(tail_loaded, 16)
                act.wait_ge(w_turned, 1)
                act.activation(w_t[:, :], ps_w[0:D, 0:D], ACT.Copy).then_inc(w_copied, 1)
                for n in range(2):
                    act.sem_inc(xt_copied[n], 1)
                    act.sem_inc(h_copied[n], 1)

                def turned(g, n):
                    a, b = parts[n]
                    act.wait_ge(x_turned[n], g + 2)
                    act.wait_ge(h_done[n], g + 1)
                    act.activation(s.x_t[0:D, a * P:b * P], ps_x[0:D, a * P:b * P], ACT.Copy).then_inc(xt_copied[n], 1)

                def product(g, n):
                    a, b = parts[n]
                    act.wait_ge(h_done[n], g + 2)
                    held(act, nobody)
                    act.activation(s.tab0[:, bass.ds(g * GRP + a, b - a), :],
                                   ps_h[:, a * P:b * P].rearrange("p (j c) -> p j c", c=P)[:, :, 0:ROW0],
                                   ACT.Copy).then_inc(h_copied[n], 1)

                turned(0, 0)
                turned(0, 1)
                with act.Fori(0, z.NG - 2) as g:
                    for n in range(2):
                        product(g, n)
                        turned(g + 1, n)
                act.wait_ge(p_turned, 1)
                act.activation(s.w_proj[0:D, :], ps_p[0:D, 0:D], ACT.Copy).then_inc(p_copied, 1)
                for n in range(2):
                    product(z.NG - 2, n)
                    turned(z.NG - 1, n)
                for n in range(2):
                    product(z.NG - 1, n)
                act.wait_ge(row_step, 3)
                act.activation(s.edge_row[:, :], row_e[:, :], ACT.Copy).then_inc(srcs_copied, 1)
                act.activation(s.block_row0[:, :], row_b[:, :], ACT.Copy).then_inc(srcs_copied, 1)
                act.activation(s.block_row[:, :], row_b[:, :], ACT.Copy).then_inc(srcs_copied, 1)
                for n, (at, w) in enumerate(banks):
                    act.wait_ge(src_done, n + 1)
                    act.activation(s.src_idx[:, at:at + w], ps_s[:, at:at + w], ACT.Copy).then_inc(srcs_copied, 1)
                for n, (at, w) in enumerate(banks):
                    act.wait_ge(rels_copied, n + 1)
                    act.activation(s.rel[:, at:at + w], s.rel0[:, at:at + w], ACT.Copy).then_inc(srcs_copied, 1)
                act.wait_ge(srcs_copied, 3 + 2 * len(banks))

            @block.tensor
            def _(pe):
                pe.wait_ge(w_loaded, 16 * 4)
                pe.transpose(ps_w[0:D, 0:D], w_raw[:, :], s.ident[0:D, 0:D]).then_inc(w_turned, 1)
                pe.wait_ge(w_copied, 1)
                pe.wait_ge(att_made, 2)
                pe.matmul(ps_a[0:D, 0:2 * H0], w_t[:, :], attm[:, :, :].rearrange("p a h -> p (a h)"),
                          start=True, stop=True).then_inc(comp_done, 1)

                def turn(g, n):
                    a, b = parts[n]
                    pe.wait_ge(x_copied[n], g + 1)
                    pe.wait_ge(xt_copied[n], g + 1)
                    for j in range(a, b):
                        last = pe.transpose(ps_x[0:D, j * P:(j + 1) * P], x_g[:, j, :], s.ident[:, :])
                    last.then_inc(x_turned[n], 1)

                def multiply(g, n):
                    a, b = parts[n]
                    pe.wait_ge(xt_copied[n], g + 2)
                    pe.wait_ge(h_copied[n], g + 1)
                    for j in range(a, b):
                        last = pe.matmul(ps_h[:, j * P:j * P + ROW0], s.x_t[0:D, j * P:(j + 1) * P], w_x[:, :],
                                         start=True, stop=True)
                    last.then_inc(h_done[n], 1)

                for n in range(2):
                    pe.sem_inc(x_turned[n], 1)
                    pe.sem_inc(h_done[n], 1)
                turn(0, 0)
                turn(0, 1)
                pe.wait_ge(w_x_made, 2)
                with pe.Fori(0, z.NG - 2) as g:
                    for n in range(2):
                        multiply(g, n)
                        turn(g + 1, n)
                pe.wait_ge(par_loaded, 16 * 4)
                pe.transpose(ps_p[0:D, 0:D], pw_raw[:, :], s.ident[0:D, 0:D]).then_inc(p_turned, 1)
                pe.wait_ge(p_copied, 1)
                pe.matmul(ps_b[0:1, 0:D], gbias[:, :], s.w_proj[0:D, :], start=True, stop=True).then_inc(bias_done, 1)
                for bank in banks:
                    staircase(pe, ps_r[0:1, :], lambda rows, k: s.tile_no[0:rows, k:k + 1], bank, True, row_done)
                for n in range(2):
                    multiply(z.NG - 2, n)
                    turn(z.NG - 1, n)
                for n in range(2):
                    multiply(z.NG - 1, n)
                pe.wait_ge(bias_made, 1)
                for bank in banks:
                    staircase(pe, ps_s, lambda rows, k: src_f[0:rows, k, :], bank, True, src_done)
                for n in range(2):
                    pe.wait_ge(h_copied[n], z.NG + 1)
                pe.wait_ge(neg_set, 1)
                for at, w in banks:
                    staircase(pe, ps_h, lambda rows, k: dst_f[0:rows, k, :], (at, w), False, None)
                    pe.wait_ge(row_step, 2)
                    pe.matmul(ps_h[:, at:at + w], neg_p[:, :], row_b[:, at:at + w],
                              start=False, stop=True).then_inc(rel_done, 1)

            @block.gpsimd
            def _(pool):
                pool.memset(dst_i[:, :, :], 0).then_inc(cleared, 1)
                pool.memset(src_i[:, :, :], 0).then_inc(cleared, 1)
                pool.memset(first_i[:, :], 0).then_inc(cleared, 1)
                pool.memset(s.x_sb[:, z.FULL:z.NB, :], 0.0).then_inc(x_cleared, 1)

                def rows(first, last):
                    with pool.Fori(first, last) as g:
                        for n, (a, b) in enumerate(parts):
                            pool.wait_ge(x_turned[n], g + 1)
                            held(pool, nobody)
                            pool.tensor_copy(x_g[:, a:b, :], s.x_sb[:, bass.ds(g * GRP + a, b - a), :]).then_inc(x_copied[n], 1)

                pool.wait_ge(x_loaded[0], 16)
                rows(0, EARLY)
                pool.wait_ge(x_loaded[1], 16 * (1 + bool(z.REST)))
                pool.wait_ge(x_cleared, 1)
                rows(EARLY, EARLY + 1)
                pool.wait_ge(viol_in, 1)
                pool.partition_all_reduce(s.viol[:, :], down_max[:, :], P, RMAX).then_inc(viol_out, 1)
                rows(EARLY + 1, z.NG)
                pool.wait_ge(ext_in, 1)
                pool.partition_all_reduce(ext_all[:, :], ext[:, :], P, RMAX).then_inc(ext_out, 1)

            @block.vector
            def _(dve):
                dve.memset(neg_p[:, :], -float(P)).then_inc(neg_set, 1)
                dve.memset(s.x_t1[D:D + 1, :, :], 1.0).then_inc(dve_step, 1)
                dve.memset(s.attr_t1[:, :, :], 1.0).then_inc(dve_step, 1)
                dve.memset(s.acc[:, z.NB:z.BROWS, :], 0.0).then_inc(dve_step, 1)
                dve.memset(s.q_tab[:, z.NB:z.BROWS, :, :], 0.0).then_inc(dve_step, 1)
                dve.memset(s.d_tab[:, z.NB:z.BROWS, :, :], 0.0).then_inc(dve_step, 1)
                dve.wait_ge(w_loaded, 16 * 4)
                for a in range(2):
                    dve.tensor_scalar(attm[:, a, :], s.heads[0:D, :], att[:, a:a + 1], None, ALU.mult).then_inc(att_made, 1)
                dve.tensor_copy(w_x[:, 0:D], w_raw[:, :]).then_inc(w_x_made, 1)
                dve.wait_ge(comp_done, 1)
                dve.tensor_copy(w_x[:, D:ROW0], ps_a[0:D, 0:2 * H0]).then_inc(w_x_made, 1)
                dve.wait_ge(edges_loaded, 16 * N_EDGE)
                dve.tensor_tensor(down[:, :, :], dst_i[:, :, 0:P], dst_i[:, :, 1:P + 1], ALU.is_gt).then_inc(dve_step, 1)
                dve.tensor_copy(later_i[:, :], dst_i[:, :, P]).then_inc(dve_step, 1)
                dve.tensor_scalar(first_i[:, :], first_i[:, :], 7, None, ALU.arith_shift_right).then_inc(dve_step, 1)
                dve.wait_ge(dve_step, 6)
                dve.tensor_reduce(down_max[:, :], down[:, :, :].rearrange("p k e -> p (k e)"), AX_X, ALU.max).then_inc(viol_in, 1)
                dve.wait_ge(dve_step, 8)
                dve.tensor_scalar(later_i[:, :], later_i[:, :], 7, None, ALU.arith_shift_right).then_inc(dve_step, 1)
                dve.tensor_copy(lo[:, :], first_i[:, :]).then_inc(dve_step, 1)
                dve.wait_ge(dve_step, 9)
                dve.tensor_copy(hi[:, :], later_i[:, :]).then_inc(dve_step, 1)
                dve.tensor_copy(src_f[:, :, :], src_i[:, :, :]).then_inc(dve_step, 1)
                dve.tensor_scalar(dst_f[:, :, :], dst_i[:, :, 0:P], SHIFT, None, ALU.add).then_inc(dve_step, 1)
                dve.wait_ge(viol_out, 1)
                dve.tensor_scalar(s.is_sorted[:, :], s.viol[:, :], -1.0, 1.0, ALU.mult, ALU.add).then_inc(dve_step, 1)
                dve.tensor_scalar(s.passes[:, :], s.viol[:, :], float(z.NB - 1), 1.0, ALU.mult, ALU.add).then_inc(dve_step, 1)
                dve.wait_ge(dve_step, 15)
                dve.tensor_scalar(lo[:, :], lo[:, :], s.is_sorted[:, 0:1], None, ALU.mult).then_inc(dve_step, 1)
                dve.tensor_scalar(hi[:, :], hi[:, :], s.is_sorted[:, 0:1], 1.0, ALU.mult, ALU.add).then_inc(dve_step, 1)
                dve.wait_ge(dve_step, 17)
                dve.tensor_tensor(lo[:, :], lo[:, :], s.tile_no[:, :], ALU.add).then_inc(dve_step, 1)
                dve.tensor_tensor(hi[:, :], hi[:, :], s.tile_no[:, :], ALU.add).then_inc(dve_step, 1)
                dve.wait_ge(dve_step, 19)
                dve.tensor_tensor(lo[:, :], lo[:, :], s.not_first[:, :], ALU.mult).then_inc(dve_step, 1)
                dve.wait_ge(dve_step, 20)
                dve.wait_ge(par_loaded, 16 * 4)
                for k, (a, b) in enumerate(windows):
                    dve.tensor_scalar(pick[:, k, 0:b - a], steps[:, a:b], hi[:, k:k + 1], None, ALU.is_lt).then_inc(pick_step, 1)
                for k, (a, b) in enumerate(windows):
                    dve.wait_ge(pick_step, k + 1)
                    dve.scalar_tensor_tensor(out=pick[:, k, 0:b - a], in0=steps[:, a:b], scalar=lo[:, k:k + 1],
                                             in1=pick[:, k, 0:b - a], op0=ALU.is_ge, op1=ALU.mult).then_inc(pick_done, 1)
                dve.wait_ge(bias_done, 1)
                dve.tensor_tensor(bias2[:, :], ps_b[0:1, 0:D], pbias[:, :], ALU.add).then_inc(bias_made, 1)
                for n, (at, w) in enumerate(banks):
                    dve.wait_ge(row_done, n + 1)
                    dve.tensor_copy(row_t[:, at:at + w], ps_r[0:1, at:at + w]).then_inc(row_copied, 1)
                dve.wait_ge(row_copied, len(banks))
                dve.tensor_tensor(row_b[:, :], steps[0:1, :], row_t[:, :], ALU.subtract).then_inc(row_step, 1)
                dve.wait_ge(row_step, 1)
                dve.tensor_scalar(row_b[:, :], row_b[:, :], s.is_sorted[0:1, 0:1], None, ALU.mult).then_inc(row_step, 1)
                dve.tensor_scalar(row_e[:, :], row_t[:, :], float(P), float(z.E - P), ALU.mult, ALU.min).then_inc(row_step, 1)
                for n in range(2):
                    dve.wait_ge(h_copied[n], z.NG + 1)
                a_src = s.tab0[:, :, D:D + H0].rearrange("p b h -> p h b")
                dve.tensor_reduce(ext[:, 0:H0], a_src, AX_X, ALU.max).then_inc(ext_step, 1)
                dve.tensor_reduce(spread[:, :], a_src, AX_X, ALU.min).then_inc(ext_step, 1)
                dve.wait_ge(ext_step, 2)
                dve.tensor_scalar(ext[:, H0:2 * H0], spread[:, :], -1.0, None, ALU.mult).then_inc(ext_in, 1)
                dve.wait_ge(ext_out, 1)
                dve.tensor_tensor(spread[:, :], ext_all[:, 0:H0], ext_all[:, H0:2 * H0], ALU.add).then_inc(row_step, 1)
                dve.tensor_scalar(s.bound[:, :, :], across(ext_all[:, 0:H0], z.NB), 1.0, None, ALU.mult).then_inc(row_step, 1)
                dve.wait_ge(row_step, 5)
                dve.tensor_reduce(wide[:, 0:1], spread[:, :], AX_X, ALU.max).then_inc(row_step, 1)
                dve.wait_ge(row_step, 6)
                dve.tensor_scalar(wide[:, 1:2], wide[:, 0:1], SPREAD_MAX, None, ALU.is_le).then_inc(row_step, 1)
                dve.wait_ge(row_step, 7)
                dve.tensor_scalar(s.is_wide[:, :], wide[:, 1:2], -1.0, 1.0, ALU.mult, ALU.add).then_inc(row_step, 1)
                for n, (at, w) in enumerate(banks):
                    dve.wait_ge(rel_done, n + 1)
                    dve.tensor_scalar(s.rel0[:, at:at + w], ps_h[:, at:at + w], -SHIFT, None, ALU.add).then_inc(rels_copied, 1)
                dve.wait_ge(rels_copied, len(banks))
                dve.wait_ge(row_step, 8)


def shift_phase(nc, z, d, s):
    with ExitStack() as ctx:
        sb = lambda n, sh, dt=F32: ctx.enter_context(nc.sbuf_tensor(n, sh, dt))
        sem = lambda n: ctx.enter_context(nc.semaphore(n))
        ad_c = sb("ad_c", [P, z.NB, 2 * H0])
        rest = sb("rest", [P, z.NB, 2 * H0])
        part = sb("part", [P, z.NB, 2 * H0])
        own = sb("own", [P, z.NB, H0])
        sum_b = sb("sum_b", [P, z.NB, H0])
        sc, own_exp = sem("shift_step"), sem("own_exp")
        own_sum = sem("own_sum")
        a_src, a_dst = s.tab0[:, :, D:D + H0], s.tab0[:, :, D + H0:ROW0]

        def own_message(eng, h):
            return eng.tensor_tensor(s.acc[:, 0:z.NB, h * D0:(h + 1) * D0], s.tab0[:, :, h * D0:(h + 1) * D0],
                                     s.acc[:, 0:z.NB, D + h:D + h + 1].to_broadcast([P, z.NB, D0]), ALU.mult)

        with nc.Block(no_gpsimd_drain=True) as block:

            @block.gpsimd
            def _(pool):
                pool.wait_ge(own_exp, 1)
                for h in range(H0 // 2, H0):
                    own_message(pool, h).then_inc(own_sum, 1)
                pool.wait_ge(own_sum, H0)

            @block.scalar
            def _(act):
                act.wait_ge(sc, 7)
                act.activation(s.acc[:, 0:z.NB, D:D + H0], own[:, :, :], ACT.Exp).then_inc(own_exp, 1)

            @block.vector
            def _(dve):
                dve.tensor_copy(ad_c[:, :, 0:H0], a_dst).then_inc(sc, 1)
                dve.tensor_tensor(sum_b[:, :, :], s.bound[:, :, :], a_dst, ALU.add).then_inc(sc, 1)
                dve.tensor_tensor(own[:, :, :], a_src, a_dst, ALU.add).then_inc(sc, 1)
                dve.wait_ge(sc, 2)
                dve.scalar_tensor_tensor(out=ad_c[:, :, H0:2 * H0], in0=sum_b[:, :, :], scalar=SLOPE,
                                         in1=sum_b[:, :, :], op0=ALU.mult, op1=ALU.max).then_inc(sc, 1)
                dve.wait_ge(sc, 3)
                dve.scalar_tensor_tensor(out=part[:, :, 0:H0], in0=own[:, :, :], scalar=SLOPE,
                                         in1=own[:, :, :], op0=ALU.mult, op1=ALU.max).then_inc(sc, 1)
                dve.wait_ge(sc, 5)
                dve.tensor_tensor(own[:, :, :], part[:, :, 0:H0], ad_c[:, :, H0:2 * H0], ALU.subtract).then_inc(sc, 1)
                dve.tensor_copy(s.d_tab[:, 0:z.NB, 0, :], ad_c[:, :, :]).then_inc(sc, 1)
                dve.wait_ge(sc, 7)
                dve.tensor_tensor(rest[:, :, :], ad_c[:, :, :], s.d_tab[:, 0:z.NB, 0, :], ALU.subtract).then_inc(sc, 1)
                dve.wait_ge(sc, 8)
                dve.tensor_copy(s.d_tab[:, 0:z.NB, 1, :], rest[:, :, :]).then_inc(sc, 1)
                dve.wait_ge(sc, 9)
                dve.tensor_tensor(part[:, :, :], rest[:, :, :], s.d_tab[:, 0:z.NB, 1, :], ALU.subtract).then_inc(sc, 1)
                dve.wait_ge(sc, 10)
                dve.tensor_copy(s.d_tab[:, 0:z.NB, 2, :], part[:, :, :]).then_inc(sc, 1)
                dve.wait_ge(own_exp, 1)
                for h in range(H0 // 2):
                    own_message(dve, h).then_inc(own_sum, 1)
                dve.wait_ge(own_sum, H0)


def exact_max_phase(nc, z, d, s):
    with ExitStack() as ctx:
        sb = lambda n, sh, dt=F32: ctx.enter_context(nc.sbuf_tensor(n, sh, dt))
        sem = lambda n: ctx.enter_context(nc.semaphore(n))
        idx = sb("mx_idx", [P, 1], I32)
        dst_col = sb("mx_dst", [P, 1])
        rows = sb("mx_rows", [P, GAT0])
        wide_s = sb("mx_wide_s", [P, H0 + 1, P])
        cand = sb("mx_cand", [P, H0, P])
        limit = sb("mx_limit", [P, P])
        a_all = sb("mx_a_all", [P, H0, P])
        dst_all = sb("mx_dst_all", [P, P])
        best = sb("mx_best", [P, H0])
        nb_col = sb("mx_nb", [P, 1])
        dst_abs = sb("mx_dst_abs", [P, z.STEPS])
        pos_p = sb("mx_pos_p", [1, P])
        ps_a = ctx.enter_context(nc.psum_tensor("mx_ps_a", [P, 512], F32))
        ps_d = ctx.enter_context(nc.psum_tensor("mx_ps_d", [P, 512], F32))
        idx_set, landed, spread_set, turned = sem("mx_idx_set"), sem("mx_landed"), sem("mx_spread"), sem("mx_turned")
        step, tile_in = sem("mx_step"), sem("mx_tile_in")
        pos_set, block_out, abs_done = sem("mx_pos_set"), sem("mx_block_out"), sem("mx_abs_done")
        HALF = -(-z.STEPS // 2)
        halves = [(0, HALF), (HALF, z.STEPS - HALF)]
        with nc.Block(no_gpsimd_drain=True) as block:

            @block.gpsimd
            def _(pool):
                wide = pool.value_load(s.is_wide[0:1, 0:1], min_val=0, max_val=1)
                with pool.If(wide != 0):
                    with pool.Fori(0, z.STEPS) as t:
                        pool.wait_ge(idx_set, t + 1)
                        pool.sem_inc(tile_in, 1)
                        pool.indirect_dma_start(rows[:, :], None, d.T0,
                                                bass.IndirectOffsetOnAxis(ap=idx[:, 0:1], axis=0)).then_inc(landed, 16)
                with pool.Else():
                    pool.sem_inc(tile_in, 1)

            @block.tensor
            def _(pe):
                wide = pe.value_load(s.is_wide[0:1, 0:1], min_val=0, max_val=1)
                with pe.If(wide != 0):
                    pe.wait_ge(pos_set, 1)
                    pe.matmul(ps_a[:, 0:HALF], pos_p[:, :], s.block_f[:, 0:HALF], start=True, stop=True)
                    pe.matmul(ps_d[:, 0:z.STEPS - HALF], pos_p[:, :], s.block_f[:, HALF:z.STEPS],
                              start=True, stop=True).then_inc(block_out, 1)
                    with pe.Fori(0, z.STEPS) as t:
                        pe.wait_ge(spread_set, t + 1)
                        for h in range(H0):
                            pe.matmul(ps_a[:, h * P:(h + 1) * P], wide_s[:, h, :], s.ident[:, :], start=True, stop=True)
                        pe.matmul(ps_d[:, 0:P], wide_s[:, H0, :], s.ident[:, :], start=True, stop=True).then_inc(turned, 1)
                with pe.Else():
                    pe.sem_inc(turned, 1)

            @block.vector
            def _(dve):
                wide = dve.value_load(s.is_wide[0:1, 0:1], min_val=0, max_val=1)
                with dve.If(wide != 0):
                    dve.memset(pos_p[:, :], float(P)).then_inc(pos_set, 1)
                    dve.wait_ge(block_out, 1)
                    for (at, w), ps in zip(halves, (ps_a, ps_d)):
                        dve.tensor_tensor(dst_abs[:, at:at + w], s.rel0[:, at:at + w], ps[:, 0:w], ALU.add).then_inc(abs_done, 1)
                    dve.wait_ge(abs_done, 2)
                    dve.tensor_copy(s.bound[:, :, :], s.tab0[:, :, D:D + H0]).then_inc(step, 1)
                    dve.wait_ge(step, 1)
                    PER = 6 + 5 * z.NB
                    with dve.Fori(0, z.STEPS) as t:
                        base = dve.snap(t * PER + 1)
                        dve.tensor_copy(dst_col[:, :], dst_abs[:, bass.ds(t, 1)]).then_inc(step, 1)
                        dve.tensor_copy(idx[:, :], s.src_idx[:, bass.ds(t, 1)]).then_inc(idx_set, 1)
                        dve.wait_ge(landed, t * 16 + 16)
                        for h in range(H0):
                            dve.tensor_scalar(wide_s[:, h, :], rows[:, D + h:D + h + 1].to_broadcast([P, P]), 1.0, None,
                                              ALU.mult).then_inc(step, 1)
                        dve.wait_ge(step, base + 5)
                        dve.tensor_scalar(wide_s[:, H0, :], dst_col[:, 0:1].to_broadcast([P, P]), 1.0, None,
                                          ALU.mult).then_inc(spread_set, 1)
                        dve.wait_ge(turned, t + 1)
                        dve.tensor_copy(a_all[:, :, :].rearrange("p h e -> p (h e)"), ps_a[:, :])
                        dve.tensor_copy(dst_all[:, :], ps_d[:, 0:P]).then_inc(step, 1)
                        with dve.Fori(0, z.NB) as b:
                            at = dve.snap(base + 6 + b * 5)
                            dve.wait_ge(step, at)
                            dve.tensor_copy(nb_col[:, :], s.node_no[:, bass.ds(b, 1)]).then_inc(step, 1)
                            dve.wait_ge(step, at + 1)
                            dve.tensor_scalar(limit[:, :], dst_all[:, :], nb_col[:, 0:1], BIG,
                                              ALU.is_equal, ALU.mult).then_inc(step, 1)
                            dve.wait_ge(step, at + 2)
                            dve.scalar_tensor_tensor(out=cand[:, :, :], in0=across(limit[:, :], H0), scalar=BIG / 2,
                                                     in1=a_all[:, :, :], op0=ALU.subtract, op1=ALU.min).then_inc(step, 1)
                            dve.wait_ge(step, at + 3)
                            dve.tensor_reduce(best[:, :], cand[:, :, :], AX_X, ALU.max).then_inc(step, 1)
                            dve.wait_ge(step, at + 4)
                            dve.tensor_tensor(s.bound[:, bass.ds(b, 1), :].rearrange("p o h -> p (o h)"),
                                              s.bound[:, bass.ds(b, 1), :].rearrange("p o h -> p (o h)"),
                                              best[:, :], ALU.max).then_inc(step, 1)
                        dve.wait_ge(step, base + PER)
                with dve.Else():
                    dve.sem_inc(step, 1)


def edge_phase(nc, z, d, s, layer):
    second = layer == 1
    heads, hd, wide = (H1, D1, ACC1) if second else (H0, D0, ACC0)
    row_w = 2 * D if second else GAT0
    dst_w = D if second else 2 * H0
    table, dst_tab = (d.T1, s.q_tab) if second else (d.T0, s.d_tab)
    acc = s.acc
    with ExitStack() as ctx:
        sb = lambda n, sh, dt=F32: ctx.enter_context(nc.sbuf_tensor(f"{n}{layer}", sh, dt))
        ps = lambda n, sh: ctx.enter_context(nc.psum_tensor(f"{n}{layer}", sh, F32))
        sem = lambda n: ctx.enter_context(nc.semaphore(f"{n}{layer}"))
        idx = sb("idx", [P, RING, QUAD], I32)
        got = sb("got", [P, RING, QUAD, row_w])
        hot = sb("hot", [P, RING, QUAD, P])
        hot_t = sb("hot_t", [P, PAR, QUAD, P], BF16)
        msg = sb("msg", [P, PAR, QUAD, wide])
        sc_a = sb("sc_a", [P, PAR, QUAD, heads])
        sc_b = sb("sc_b", [P, PAR, QUAD, heads])
        sc_c = sb("sc_c", [P, PAR, QUAD, heads])
        sc_d = sb("sc_d", [P, PAR, QUAD, heads])
        ps_hot = ps("ps_hot", [P, PAR, QUAD, P])
        ps_acc = ps("ps_acc", [P, PAR, 512])
        if second:
            prod = sb("prod", [P, PAR, QUAD, D])
            prod_e = sb("prod_e", [P, PAR, QUAD, D])
            attr = sb("attr", [P, RING, QUAD, D])
            attr_t = s.attr_t1[:, :, :].rearrange("p a (j e) -> p a j e", e=P)
            ps_attr = ps("ps_attr", [P, PAR, QUAD, P])
            ps_e = ps("ps_e", [P, 512])
            ps_dst = ps("ps_dst", [P, 1, 512])
        else:
            ps_dst = ps("ps_dst", [P, PAR, 512])
        DST_PAR = 1 if second else PAR
        SCORE0 = 0 if second else PAR

        rows_ready = sem("rows_ready")
        idx_ready = sem("idx_ready")
        gathered = [sem(f"gathered{k}") for k in range(RING)]
        hot_done = sem("hot_done")
        hot_turned = sem("hot_turned")
        hot_t_done = sem("hot_t_done")
        dst_done = sem("dst_done")
        score_done = sem("score_done")
        dst_used = sem("dst_used") if second else score_done
        exp_done = sem("exp_done")
        msg_done = sem("msg_done")
        sum_done = sem("sum_done")
        acc_done = sem("acc_done")
        mid_a, mid_b, mid_c = sem("mid_a"), sem("mid_b"), sem("mid_c")
        pool_go, pass_begun = sem("pool_go"), sem("pass_begun")
        if second:
            attr_in = [sem(f"attr_in{k}") for k in range(RING)]
            attr_turned = sem("attr_turned")
            attr_t_done = sem("attr_t_done")
            e_done = sem("e_done")
            e_used = sem("e_used")

        def in_slots(eng, first, last, slot):
            n_pass = eng.value_load(s.passes[0:1, 0:1], min_val=1, max_val=z.NB)
            with eng.Fori(0, n_pass) as p:
                eng.wait_ge(rows_ready, p * 2 + 2)
                eng.sem_inc(pass_begun, 1)
                base = eng.snap(p * z.NQ)
                rounds = eng.snap(p * z.NIT)
                for q in range(first, RING):
                    slot(q, base, 0, rounds, lambda c, q=q: 0 <= q + c < z.NQ)
                with eng.Fori(1, z.NIT - 1) as it:
                    at = eng.snap(base + it * RING)
                    rd = eng.snap(rounds + it)
                    for k in range(RING):
                        slot(k, at, it, rd, lambda c: True)
                end = z.NIT - 1
                at = eng.snap(base + end * RING)
                rd = eng.snap(rounds + end)
                for k in range(RING + last):
                    slot(k, at, end, rd, lambda c, k=k: 0 <= end * RING + k + c < z.NQ)
                if eng is nc.vector:
                    dve = eng
                    dve.wait_ge(acc_done, (base + z.NQ + PAR) * QUAD)
                    dve.tensor_scalar(s.rel[:, :], s.rel[:, :], -float(P), None, ALU.add).then_inc(rows_ready, 1)
                    dve.tensor_scalar(s.block_row[:, :], s.block_row[:, :], 1, None, ALU.add).then_inc(rows_ready, 1)

        def steps_of(it, n):
            return bass.ds(it * (RING * QUAD) + n * QUAD, QUAD)

        with nc.Block(no_gpsimd_drain=True) as block:

            @block.gpsimd
            def _(pool):
                def slot(k, base, it, rounds, has):
                    pool.wait_ge(idx_ready, base + (k + 1))
                    pool.wait_ge(msg_done, base + (k + 1))
                    pool.sem_inc(pool_go, 1)
                    for j in range(QUAD):
                        pool.indirect_dma_start(got[:, k % RING, j, :], None, table,
                                                bass.IndirectOffsetOnAxis(ap=idx[:, k % RING, j:j + 1], axis=0)
                                                ).then_inc(gathered[k % RING], 16)
                in_slots(pool, 0, 0, slot)

            @block.sync
            def _(sp):
                if not second:
                    return
                regs = [sp.alloc_register(f"edge_at{j}") for j in range(QUAD)]

                def slot(k, base, it, rounds, has):
                    sp.reg_load(regs, s.edge_row[0:1, steps_of(it, k)])
                    sp.wait_ge(attr_turned, base + (k + 1))
                    for j in range(QUAD):
                        at = sp.snap(regs[j], min_val=0, max_val=z.E - P)
                        sp.dma_start(attr[:, k % RING, j, :], d.attr[bass.ds(at, P), :]).then_inc(attr_in[k % RING], 16)
                in_slots(sp, 0, 0, slot)

            @block.scalar
            def _(act):
                act.sem_inc(hot_t_done, PAR)
                if second:
                    act.sem_inc(attr_t_done, PAR)

                def slot(k, base, it, rounds, has):
                    if has(0):
                        n = k
                        act.wait_ge(score_done, base + (n + 1 + SCORE0))
                        act.wait_ge(sum_done, base + (n - PAR + RING + 1))
                        act.activation(msg[:, n % PAR, :, D:wide], sc_c[:, n % PAR, :, :], ACT.Exp).then_inc(exp_done, 1)
                    if has(2):
                        n = k + 2
                        act.wait_ge(hot_turned, base + (n + 1))
                        act.wait_ge(dst_done, base + (n + 1))
                        act.activation(hot_t[:, n % PAR, :, :], ps_hot[:, n % PAR, :, :], ACT.Copy).then_inc(hot_t_done, 1)
                        if second:
                            act.wait_ge(attr_turned, base + (n + RING + 1))
                            act.wait_ge(e_done, base + (n + 1))
                            act.activation(attr_t[0:D, n % PAR, :, :], ps_attr[0:D, n % PAR, :, :],
                                           ACT.Copy).then_inc(attr_t_done, 1)
                in_slots(act, -2, 0, slot)

            @block.tensor
            def _(pe):
                pe.sem_inc(dst_done, PAR)
                pe.sem_inc(sum_done, RING)
                if second:
                    pe.sem_inc(attr_turned, RING)
                    pe.sem_inc(e_done, PAR)
                regs = [pe.alloc_register(f"block_at{layer}_{j}") for j in range(QUAD)]

                def slot(k, base, it, rounds, has):
                    if has(-1):
                        n = k - 1
                        pe.wait_ge(msg_done, base + (n + RING + 1))
                        pe.wait_ge(acc_done, (base + (n + 1)) * QUAD)
                        for j in range(QUAD):
                            last = pe.matmul(ps_acc[:, n % PAR, j * wide:(j + 1) * wide], hot[:, n % RING, j, :],
                                             msg[:, n % PAR, j, :], start=True, stop=True)
                        last.then_inc(sum_done, 1)
                    if has(1):
                        n = k + 1
                        pe.reg_load(regs, s.block_row[0:1, steps_of(it, n)])
                        pe.wait_ge(hot_t_done, base + (n + PAR + 1))
                        pe.wait_ge(dst_used, base + (n + 1))
                        for j in range(QUAD):
                            b = pe.snap(regs[j], min_val=0, max_val=z.BROWS - 1)
                            for c in range(3):
                                last = pe.matmul(ps_dst[:, n % DST_PAR, j * dst_w:(j + 1) * dst_w],
                                                 hot_t[:, n % PAR, j, :],
                                                 dst_tab[:, bass.ds(b, 1), c, :].rearrange("p o e -> p (o e)"),
                                                 start=(c == 0), stop=(c == 2))
                        last.then_inc(dst_done, 1)
                        if second:
                            pe.wait_ge(attr_t_done, base + (n + PAR + 1))
                            pe.wait_ge(e_used, base + (n + 1))
                            for j in range(QUAD):
                                last = pe.matmul(ps_e[:, j * D:(j + 1) * D], attr_t[:, n % PAR, j, :], s.w_e[:, :],
                                                 start=True, stop=True)
                            last.then_inc(e_done, 1)
                    if has(2):
                        n = k + 2
                        pe.wait_ge(hot_done, base + (n + 1))
                        pe.wait_ge(hot_t_done, base + (n + 1))
                        for j in range(QUAD):
                            last = pe.transpose(ps_hot[:, n % PAR, j, :], hot[:, n % RING, j, :], s.ident[:, :])
                        last.then_inc(hot_turned, 1)
                        if second:
                            pe.wait_ge(attr_in[n % RING], (rounds + (n // RING + 1)) * (16 * QUAD))
                            pe.wait_ge(attr_t_done, base + (n + 1))
                            for j in range(QUAD):
                                last = pe.transpose(ps_attr[0:D, n % PAR, j, :], attr[:, n % RING, j, :], s.ident[:, :])
                            last.then_inc(attr_turned, 1)
                in_slots(pe, -2, 1, slot)

            @block.vector
            def _(dve):
                dve.sem_inc(rows_ready, 2)
                dve.sem_inc(msg_done, RING)
                dve.sem_inc(dst_used, DST_PAR)
                dve.sem_inc(acc_done, QUAD * PAR)
                if second:
                    dve.sem_inc(e_used, 1)
                regs = [[dve.alloc_register(f"sum_at{layer}_{n}_{j}") for j in range(QUAD)] for n in range(PAR)]

                def slot(k, base, it, rounds, has):
                    def add(j):
                        if not has(-2):
                            return
                        n = k - 2
                        if j == 0:
                            dve.wait_ge(sum_done, base + (n + RING + 1))
                        b = dve.snap(regs[n % PAR][j], min_val=0, max_val=z.BROWS - 1)
                        to = acc[:, bass.ds(b, 1), 0:wide].rearrange("p o e -> p (o e)")
                        dve.wait_ge(acc_done, (base + (n + PAR)) * QUAD + j)
                        dve.tensor_tensor(to, to, ps_acc[:, n % PAR, j * wide:(j + 1) * wide], ALU.add).then_inc(acc_done, 1)

                    add(0)
                    add(1)
                    if has(-1):
                        n = k - 1
                        dve.wait_ge(exp_done, base + (n + 1))
                        val = got[:, n % RING, :, D:2 * D] if second else got[:, n % RING, :, 0:D]
                        dve.tensor_tensor(msg[:, n % PAR, :, 0:D].rearrange("p j (h e) -> p j h e", e=hd),
                                          val.rearrange("p j (h e) -> p j h e", e=hd),
                                          over(msg[:, n % PAR, :, D:wide], hd), ALU.mult).then_inc(msg_done, 1)
                    if has(3):
                        n = k + 3
                        dve.tensor_copy(idx[:, n % RING, :], s.src_idx[:, steps_of(it, n)]).then_inc(idx_ready, 1)
                    if has(0):
                        dve.wait_ge(gathered[k % RING], (rounds + (k // RING + 1)) * (16 * QUAD))
                        dve.wait_ge(dst_done, base + (k + PAR + 1))
                        at = ps_dst[:, k % DST_PAR, 0:QUAD * dst_w].rearrange("p (j e) -> p j e", j=QUAD)
                        rows = got[:, k % RING, :, :]
                        par = k % PAR
                        if second:
                            dve.tensor_tensor(prod[:, par, :, :], rows[:, :, 0:D], at, ALU.mult).then_inc(dst_used, 1)
                        else:
                            dve.tensor_tensor(sc_a[:, par, :, :], rows[:, :, D:D + H0], at[:, :, 0:H0], ALU.add).then_inc(mid_a, 1)
                    add(2)
                    if has(0):
                        if second:
                            dve.wait_ge(e_done, base + (k + PAR + 1))
                            dve.wait_ge(dst_used, base + (k + 2))
                            dve.tensor_tensor(prod_e[:, par, :, :], prod[:, par, :, :],
                                              ps_e[:, 0:QUAD * D].rearrange("p (j e) -> p j e", j=QUAD),
                                              ALU.mult).then_inc(e_used, 1)
                        else:
                            dve.wait_ge(mid_a, base + (k + 1))
                            dve.scalar_tensor_tensor(out=sc_b[:, par, :, :], in0=sc_a[:, par, :, :], scalar=SLOPE,
                                                     in1=sc_a[:, par, :, :], op0=ALU.mult, op1=ALU.max).then_inc(mid_b, 1)
                    if has(2):
                        n = k + 2
                        dve.wait_ge(sum_done, base + (n + 1))
                        dve.tensor_tensor(hot[:, n % RING, :, :], across(s.iota[:, :], QUAD),
                                          over(s.rel[:, steps_of(it, n)], P), ALU.is_equal).then_inc(hot_done, 1)
                    if has(-1):
                        dve.reg_load(regs[(k - 1) % PAR], s.block_row[0:1, steps_of(it, k - 1)])
                    if has(0):
                        if second:
                            dve.wait_ge(e_used, base + (k + 2))
                            dve.tensor_reduce(sc_a[:, par, :, :].rearrange("p j h -> p (j h)"),
                                              prod_e[:, par, :, :].rearrange("p j (h e) -> p (j h) e", e=D1),
                                              AX_X, ALU.add).then_inc(mid_a, 1)
                        else:
                            dve.wait_ge(mid_b, base + (k + 1))
                            dve.tensor_tensor(sc_d[:, par, :, :], sc_b[:, par, :, :], at[:, :, H0:2 * H0],
                                              ALU.subtract).then_inc(mid_c, 1)
                    add(3)
                    if has(0):
                        if second:
                            dve.wait_ge(mid_a, base + (k + 1))
                            dve.tensor_scalar(sc_c[:, par, :, :], sc_a[:, par, :, :], 5.0, -5.0,
                                              ALU.min, ALU.max).then_inc(score_done, 1)
                        else:
                            dve.wait_ge(mid_c, base + (k + 1))
                            dve.tensor_scalar(sc_c[:, par, :, :], sc_d[:, par, :, :], 0.0, None,
                                              ALU.min).then_inc(score_done, 1)
                in_slots(dve, -3, 2, slot)


def group_slots(eng, n, first, last, slot):
    for g in range(first, 1):
        slot(g, lambda c, g=g: 0 <= g + c < n)
    with eng.Fori(1, n + first) as g:
        slot(g, lambda c: True)
    for g in range(n + first, n + last):
        slot(g, lambda c, g=g: 0 <= g + c < n)


def statistics(dve, v, stats, mean_var, stats_done, nobody, at, var_out, asked):
    for j in range(GRP):
        ins = dve.bn_stats(stats[:, j, :], v[:, j, :])
    ins.then_inc(stats_done, 1)
    dve.wait_ge(stats_done, at * 2 + 1)
    held(dve, nobody)
    for j in range(GRP):
        ins = dve.bn_aggr(mean_var[:, j, :], stats[:, j, :])
    ins.then_inc(stats_done, 1)
    dve.wait_ge(stats_done, at * 2 + 2)
    dve.tensor_scalar(var_out, mean_var[:, :, 1], EPS, None, ALU.add).then_inc(asked, 1)


def scale_and_bias(dve, mean_var, dev, inv, bias, root, inv_done, scaled, at):
    dve.wait_ge(root, at + 1)
    dve.reciprocal(inv, dev).then_inc(inv_done, 1)
    dve.wait_ge(inv_done, at + 1)
    dve.scalar_tensor_tensor(out=bias, in0=mean_var[:, :, 0], scalar=-1.0, in1=inv,
                             op0=ALU.mult, op1=ALU.mult).then_inc(scaled, 1)


def normalize(act, out, v, inv, bias, done):
    for j in range(GRP):
        ins = act.activation(out[:, j, :], v[:, j, :], ACT.Identity, scale=inv[:, j:j + 1], bias=bias[:, j:j + 1])
    ins.then_inc(done, 1)


def middle_phase(nc, z, d, s):
    with ExitStack() as ctx:
        sb = lambda n, sh, dt=F32: ctx.enter_context(nc.sbuf_tensor(f"mid_{n}", sh, dt))
        sem = lambda n: ctx.enter_context(nc.semaphore(f"mid_{n}"))
        inv = sb("inv", [P, z.NB, H0])
        agg = sb("agg", [P, GRP, D])
        agg_t = sb("agg_t", [D + 1, GRP * P])
        v1 = sb("v1", [P, GRP, D])
        n1g = sb("n1g", [P, GRP, D])
        xb = sb("xb", [P, GRP, D])
        v2 = sb("v2", [P, GRP, D])
        x1g = sb("x1g", [P, GRP, D])
        stats = [sb(f"stats{n}", [P, GRP, 6]) for n in range(2)]
        mean_var = [sb(f"mean_var{n}", [P, GRP, 2]) for n in range(2)]
        dev = [sb(f"dev{n}", [P, GRP]) for n in range(2)]
        inv_dev = [sb(f"inv_dev{n}", [P, GRP]) for n in range(2)]
        bias = sb("bias", [P, GRP])
        zeros = sb("zeros", [P, GRP])
        kv = sb("kv", [P, GRP, 2 * D])
        q = sb("q", [P, GRP, D])
        q_r = sb("q_r", [P, GRP, D])
        ps_t = ctx.enter_context(nc.psum_tensor("mid_ps_t", [P, 1024], F32))
        ps_z = ctx.enter_context(nc.psum_tensor("mid_ps_z", [P, 1024], F32))
        ps_k = ctx.enter_context(nc.psum_tensor("mid_ps_k", [P, 4, 512], F32))
        ones_set, nobody = sem("ones_set"), sem("nobody")
        inv_set = sem("inv_set")
        agg_done = sem("agg_done")
        agg_turned, agg_copied = sem("agg_turned"), sem("agg_copied")
        z_done, z_read = sem("z_done"), sem("z_read")
        stats_done = [sem(f"stats_done{n}") for n in range(2)]
        asked = [sem(f"asked{n}") for n in range(2)]
        root = [sem(f"root{n}") for n in range(2)]
        inv_done = [sem(f"inv_done{n}") for n in range(2)]
        scaled = sem("scaled")
        normed = sem("normed")
        xb_done, g_done, v2_done = sem("xb_done"), sem("g_done"), sem("v2_done")
        x1_turned, x1_copied, x1_kept = sem("x1_turned"), sem("x1_copied"), sem("x1_kept")
        k_done, kv_copied, q_copied, t1_stored = sem("k_done"), sem("kv_copied"), sem("q_copied"), sem("t1_stored")
        split_step, split_done, cleared = sem("split_step"), sem("split_done"), sem("cleared")
        t1_rows = d.T1.rearrange("(b p) c -> p b c", p=P)
        parts = [(0, 4), (4, GRP)]
        NG = z.NG

        def blocks(g, a=0, b=GRP):
            return bass.ds(g * GRP + a, b - a)

        with nc.Block(no_gpsimd_drain=True) as block:

            @block.sync
            def _(sp):
                with sp.Fori(0, NG) as g:
                    sp.wait_ge(kv_copied, g * 2 + 2)
                    sp.dma_start(t1_rows[:, blocks(g), :], kv[:, :, :]).then_inc(t1_stored, 16)
                sp.wait_ge(t1_stored, 16 * (NG + 1))

            @block.scalar
            def _(act):
                act.sem_inc(t1_stored, 16)
                act.sem_inc(normed, 1)
                act.sem_inc(x1_kept, 1)

                def project(g, n):
                    a, b = parts[n]
                    act.wait_ge(k_done, g * 2 + (n - 1))
                    if n == 0:
                        act.wait_ge(t1_stored, g * 16)
                        act.wait_ge(split_done, g)
                    held(act, nobody)
                    act.activation(kv[:, a:b, :], ps_k[:, 0:b - a, 0:2 * D], ACT.Copy).then_inc(kv_copied, 1)
                    for to in (s.q_tab[:, blocks(g - 1, a, b), 0, :], q[:, a:b, :]):
                        ins = act.activation(to, ps_k[:, 0:b - a, 2 * D:3 * D], ACT.Copy,
                                             scale=1.0 / float(np.sqrt(D1)))
                    ins.then_inc(q_copied, 1)

                def slot(g, has):
                    if has(0):
                        act.wait_ge(scaled, g + 1)
                        act.wait_ge(x1_kept, g + 1)
                        held(act, nobody)
                        normalize(act, x1g, v2, inv_dev[1], bias, normed)
                    if has(1):
                        act.wait_ge(asked[0], g + 2)
                        act.activation(dev[0][:, :], dev[0][:, :], ACT.Sqrt).then_inc(root[0], 1)
                    if has(-1):
                        project(g, 0)
                    if has(0):
                        act.wait_ge(normed, g + 2)
                        held(act, nobody)
                        act.activation(s.x1[:, blocks(g), :], x1g[:, :, :], ACT.Copy).then_inc(x1_kept, 1)
                    if has(2):
                        act.wait_ge(agg_turned, g + 4)
                        act.activation(agg_t[0:D, 0:4 * P], ps_t[0:D, 0:4 * P], ACT.Copy)
                        act.activation(agg_t[0:D, 4 * P:GRP * P], ps_t[0:D, 4 * P:GRP * P], ACT.Copy).then_inc(agg_copied, 1)
                    if has(-1):
                        project(g, 1)
                    if has(0):
                        act.wait_ge(x1_turned, g + 1)
                        act.activation(s.x_t1[0:D, 0, 0:4 * P], ps_t[0:D, 0:4 * P], ACT.Copy)
                        act.activation(s.x_t1[0:D, 0, 4 * P:GRP * P], ps_t[0:D, 4 * P:GRP * P], ACT.Copy).then_inc(x1_copied, 1)
                    if has(1):
                        act.wait_ge(asked[1], g + 2)
                        act.activation(dev[1][:, :], dev[1][:, :], ACT.Sqrt).then_inc(root[1], 1)
                    if has(3):
                        act.wait_ge(agg_done, g + 4)
                        held(act, nobody)
                        act.activation(s.acc[:, blocks(g + 3), :], over(zeros[:, :], ACC1), ACT.Copy).then_inc(cleared, 1)
                group_slots(act, NG, -3, 1, slot)
                act.wait_ge(x1_kept, NG + 1)

            @block.tensor
            def _(pe):
                pe.wait_ge(ones_set, 2)
                pe.sem_inc(agg_turned, 1)

                def project(g, n):
                    a, b = parts[n]
                    for j in range(a, b):
                        ins = pe.matmul(ps_k[:, j - a, 0:3 * D], s.x_t1[:, 0, j * P:(j + 1) * P],
                                        s.w_kvq[:, :], start=True, stop=True)
                    ins.then_inc(k_done, 1)

                def slot(g, has):
                    if has(-1):
                        pe.wait_ge(x1_copied, g)
                        project(g, 0)
                    if has(2):
                        pe.wait_ge(agg_done, g + 3)
                        for j in range(GRP):
                            ins = pe.transpose(ps_t[0:D, j * P:(j + 1) * P], agg[:, j, :], s.ident[:, :])
                        ins.then_inc(agg_turned, 1)
                    if has(-1):
                        pe.wait_ge(q_copied, g * 2 - 1)
                        project(g, 1)
                    if has(2):
                        pe.wait_ge(agg_copied, g + 3)
                    if has(0):
                        pe.wait_ge(normed, g + 2)
                        for j in range(GRP):
                            ins = pe.transpose(ps_t[0:D, j * P:(j + 1) * P], x1g[:, j, :], s.ident[:, :])
                        ins.then_inc(x1_turned, 1)
                    if has(2):
                        pe.wait_ge(z_read, g + 3)
                        for j in range(GRP):
                            ins = pe.matmul(ps_z[:, j * P:j * P + D], agg_t[:, j * P:(j + 1) * P], s.w_proj[:, :],
                                            start=True, stop=True)
                        ins.then_inc(z_done, 1)
                group_slots(pe, NG, -3, 1, slot)

            @block.gpsimd
            def _(pool):
                pool.sem_inc(split_done, 1)
                pool.wait_ge(inv_set, 1)

                def slot(g, has):
                    if has(1):
                        pool.wait_ge(v2_done, g + 2)
                        held(pool, nobody)
                        pool.tensor_tensor(xb[:, :, :], s.x_sb[:, blocks(g + 1), :], across(s.ln_b[:, :], GRP),
                                           ALU.add).then_inc(xb_done, 1)
                    if has(3):
                        pool.wait_ge(agg_turned, g + 4)
                        held(pool, nobody)
                        pool.tensor_tensor(agg[:, :, :].rearrange("p j (h e) -> p j h e", e=D0),
                                           s.acc[:, blocks(g + 3), 0:D].rearrange("p j (h e) -> p j h e", e=D0),
                                           over(inv[:, blocks(g + 3), :], D0), ALU.mult).then_inc(agg_done, 1)
                    if has(-1):
                        pool.wait_ge(q_copied, g * 2)
                        held(pool, nobody)
                        to = s.q_tab[:, blocks(g - 1), :, :]
                        pool.tensor_tensor(to[:, :, 1, :], q[:, :, :], to[:, :, 0, :], ALU.subtract)
                        pool.tensor_tensor(q_r[:, :, :], q[:, :, :], to[:, :, 0, :], ALU.subtract).then_inc(split_step, 1)
                        pool.wait_ge(split_step, g)
                        held(pool, nobody)
                        pool.tensor_tensor(to[:, :, 2, :], q_r[:, :, :], to[:, :, 1, :], ALU.subtract).then_inc(split_done, 1)
                group_slots(pool, NG, -3, 1, slot)
                pool.wait_ge(split_done, NG + 1)
                pool.wait_ge(agg_done, NG)

            @block.vector
            def _(dve):
                dve.memset(agg_t[D:D + 1, :], 1.0).then_inc(ones_set, 1)
                dve.memset(zeros[:, :], 0.0).then_inc(ones_set, 1)
                dve.reciprocal(inv[:, :, :], s.acc[:, 0:z.NB, D:ACC0]).then_inc(inv_set, 1)
                dve.tensor_copy(s.rel[:, :], s.rel0[:, :]).then_inc(ones_set, 1)
                dve.tensor_copy(s.block_row[:, :], s.block_row0[:, :]).then_inc(ones_set, 1)
                dve.sem_inc(v2_done, 1)
                dve.sem_inc(z_read, 1)
                dve.wait_ge(ones_set, 2)

                def slot(g, has):
                    if has(0):
                        scale_and_bias(dve, mean_var[1], dev[1][:, :], inv_dev[1][:, :], bias[:, :], root[1],
                                       inv_done[1], scaled, g)
                    if has(1):
                        dve.wait_ge(z_done, g + 2)
                        for a, b in parts:
                            ins = dve.tensor_tensor(v1[:, a:b, :], s.x_sb[:, blocks(g + 1, a, b), :],
                                                    ps_z[:, :].rearrange("p (j c) -> p j c", c=P)[:, a:b, 0:D], ALU.add)
                        ins.then_inc(z_read, 1)
                        dve.wait_ge(z_read, g + 3)
                        statistics(dve, v1, stats[0], mean_var[0], stats_done[0], nobody, g + 1, dev[0][:, :], asked[0])
                        for j in range(GRP):
                            ins = dve.scalar_tensor_tensor(out=n1g[:, j, :], in0=v1[:, j, :], scalar=mean_var[0][:, j, 0:1],
                                                           in1=s.ln_g[:, :], op0=ALU.subtract, op1=ALU.mult)
                        ins.then_inc(g_done, 1)
                    if has(1):
                        dve.wait_ge(root[0], g + 2)
                        dve.reciprocal(inv_dev[0][:, :], dev[0][:, :]).then_inc(inv_done[0], 1)
                    if has(1):
                        dve.wait_ge(inv_done[0], g + 2)
                        dve.wait_ge(g_done, g + 2)
                        dve.wait_ge(xb_done, g + 2)
                        dve.wait_ge(normed, g + 2)
                        held(dve, nobody)
                        for j in range(GRP):
                            ins = dve.scalar_tensor_tensor(out=v2[:, j, :], in0=n1g[:, j, :], scalar=inv_dev[0][:, j:j + 1],
                                                           in1=xb[:, j, :], op0=ALU.mult, op1=ALU.add)
                        ins.then_inc(v2_done, 1)
                        dve.wait_ge(v2_done, g + 3)
                        statistics(dve, v2, stats[1], mean_var[1], stats_done[1], nobody, g + 1, dev[1][:, :], asked[1])
                group_slots(dve, NG, -3, 0, slot)
                dve.wait_ge(cleared, NG)


def last_phase(nc, z, d, s):
    with ExitStack() as ctx:
        sb = lambda n, sh, dt=F32: ctx.enter_context(nc.sbuf_tensor(f"end_{n}", sh, dt))
        sem = lambda n: ctx.enter_context(nc.semaphore(f"end_{n}"))
        den = sb("den", [P, z.NB, H1])
        inv = sb("inv", [P, z.NB, H1])
        out1 = sb("out1", [P, PAR, GRP, D])
        v = sb("v", [P, PAR, GRP, D])
        stats = sb("stats", [P, GRP, 6])
        mean_var = sb("mean_var", [P, GRP, 2])
        dev = sb("dev", [P, PAR, GRP])
        inv_dev = sb("inv_dev", [P, PAR, GRP])
        bias = sb("bias", [P, PAR, GRP])
        den_done, inv_set, out_done, v_done = sem("den_done"), sem("inv_set"), sem("out_done"), sem("v_done")
        stats_done, asked, root, nobody = sem("stats_done"), sem("asked"), sem("root"), sem("nobody")
        inv_done, scaled, y_done, stored = sem("inv_done"), sem("scaled"), sem("y_done"), sem("stored")
        with nc.Block(no_gpsimd_drain=True) as block:

            @block.gpsimd
            def _(pool):
                for g in range(z.NG):
                    at, par = slice(g * GRP, (g + 1) * GRP), g % PAR
                    pool.wait_ge(inv_set, 1 + (g > 0))
                    pool.tensor_tensor(out1[:, par, :, :].rearrange("p j (h e) -> p j h e", e=D1),
                                       s.acc[:, at, 0:D].rearrange("p j (h e) -> p j h e", e=D1),
                                       over(inv[:, at, :], D1), ALU.mult).then_inc(out_done, 1)
                    pool.wait_ge(out_done, g + 1)
                    if g >= PAR:
                        pool.wait_ge(y_done, g - PAR + 1)
                    pool.tensor_tensor(v[:, par, :, :], s.x1[:, at, :], out1[:, par, :, :], ALU.add).then_inc(v_done, 1)

            @block.scalar
            def _(act):
                for g in range(z.NG):
                    par = g % PAR
                    act.wait_ge(asked, g + 1)
                    act.activation(dev[:, par, :], dev[:, par, :], ACT.Sqrt).then_inc(root, 1)
                    act.wait_ge(scaled, g + 1)
                    normalize(act, s.x_sb[:, g * GRP:(g + 1) * GRP, :], v[:, par, :, :], inv_dev[:, par, :],
                              bias[:, par, :], y_done)

            @block.vector
            def _(dve):
                dve.tensor_scalar(den[:, :, :], s.acc[:, 0:z.NB, D:ACC1], 1e-6, None, ALU.add).then_inc(den_done, 1)
                dve.wait_ge(den_done, 1)
                dve.reciprocal(inv[:, 0:GRP, :], den[:, 0:GRP, :]).then_inc(inv_set, 1)
                dve.reciprocal(inv[:, GRP:, :], den[:, GRP:, :]).then_inc(inv_set, 1)
                for g in range(z.NG):
                    par = g % PAR
                    dve.wait_ge(v_done, g + 1)
                    statistics(dve, v[:, par, :, :], stats, mean_var, stats_done, nobody, g, dev[:, par, :], asked)
                    if g >= PAR:
                        dve.wait_ge(y_done, g - PAR + 1)
                    scale_and_bias(dve, mean_var, dev[:, par, :], inv_dev[:, par, :], bias[:, par, :], root,
                                   inv_done, scaled, g)

            @block.sync
            def _(sp):
                n_stores = 0
                for g in range(z.NG):
                    a, b = g * GRP, min((g + 1) * GRP, z.FULL)
                    sp.wait_ge(y_done, g + 1)
                    if b > a:
                        sp.dma_start(d.out[a * P:b * P, :].rearrange("(b p) e -> p b e", p=P),
                                     s.x_sb[:, a:b, :]).then_inc(stored, 16)
                        n_stores += 1
                    if z.REST and g * GRP <= z.FULL < (g + 1) * GRP:
                        sp.dma_start(d.out[z.FULL * P:z.N, :], s.x_sb[0:z.REST, z.FULL, :]).then_inc(stored, 16)
                        n_stores += 1
                sp.wait_ge(stored, 16 * n_stores)


def build(nc, z, d, where):
    d.T0 = nc.dram_tensor("T0", [z.NB * P, GAT0], F32).ap()
    d.T1 = nc.dram_tensor("T1", [z.NB * P, 2 * D], F32).ap()
    with ExitStack() as ctx:
        def sb(name, shape, dt=F32):
            return ctx.enter_context(nc.sbuf_tensor(name, shape, dt))

        s = Bag()
        s.cst = sb("cst", [P, where[-1][1]])
        s.ident, s.iota, s.tile_no, s.not_first, s.heads, s.node_no = (s.cst[:, a:b] for a, b in where)
        s.x_sb = sb("x_sb", [P, z.NB, D])
        s.acc = sb("acc", [P, z.BROWS, ACC1])
        s.q_tab = sb("q_tab", [P, z.BROWS, 3, D], BF16)
        s.d_tab = sb("d_tab", [P, z.BROWS, 3, 2 * H0], BF16)
        s.w_kvq = sb("w_kvq", [D + 1, 3 * D])
        s.w_e = sb("w_e", [D + 1, D])
        s.w_proj = sb("w_proj", [D + 1, D])
        s.ln_g = sb("ln_g", [P, D])
        s.ln_b = sb("ln_b", [P, D])
        s.x_t1 = sb("x_t1", [D + 1, 1, GRP * P])
        s.attr_t1 = sb("attr_t1", [D + 1, PAR, QUAD * P])
        s.x_t = s.x_t1[:, 0, :]
        s.src_idx = sb("src_idx", [P, z.STEPS], I32)
        s.rel0 = sb("rel0", [P, z.STEPS])
        s.rel = sb("rel", [P, z.STEPS])
        s.block_f = sb("block_f", [1, z.STEPS])
        s.block_row0 = sb("block_row0", [1, z.STEPS], I32)
        s.block_row = sb("block_row", [1, z.STEPS], I32)
        s.edge_row = sb("edge_row", [1, z.STEPS], I32)
        s.viol = sb("viol", [P, 1])
        s.is_sorted = sb("is_sorted", [P, 1])
        s.passes = sb("passes", [P, 1], I32)
        s.is_wide = sb("is_wide", [P, 1], I32)
        with nc.sbuf_tensor("tab0", [P, z.NB, ROW0], F32) as s.tab0, nc.sbuf_tensor("bound", [P, z.NB, H0], F32) as s.bound:
            first_phase(nc, z, d, s)
            exact_max_phase(nc, z, d, s)
            shift_phase(nc, z, d, s)
        edge_phase(nc, z, d, s, 0)
        s.x1 = sb("x1", [P, z.NB, D])
        middle_phase(nc, z, d, s)
        edge_phase(nc, z, d, s, 1)
        last_phase(nc, z, d, s)


_INS = ['x', 'src', 'dst', 'edge_attr_96', 'L0_gnn_W', 'L0_gnn_att_src', 'L0_gnn_att_dst', 'L0_gnn_gat_bias',
        'L0_gnn_proj_W', 'L0_gnn_proj_b', 'L0_gnn_ln_g', 'L0_gnn_ln_b', 'L1_gnn_Wq', 'L1_gnn_bq', 'L1_gnn_Wk',
        'L1_gnn_bk', 'L1_gnn_We', 'L1_gnn_be', 'L1_gnn_Wv', 'L1_gnn_bv']


def program(nc, inputs):
    z = sizes(inputs['x'].shape[0], inputs['src'].shape[0])
    table, where, steps, tail = constants(z)
    arrays = {name: np.ascontiguousarray(inputs[name]) for name in _INS}
    arrays |= {'cst': table, 'steps': steps, 'tail': tail}

    def given(name):
        a = arrays[name]
        return nc.dram_tensor(f"in_{name}_dram", a.shape, mybir.dt.from_np(a.dtype), kind="ExternalInput").ap()

    d = Bag()
    d.x, d.src, d.dst, d.attr = (given(n) for n in _INS[:4])
    d.W, d.att_src, d.att_dst, d.gat_bias, d.proj_W, d.proj_b, d.ln_g, d.ln_b = (given(n) for n in _INS[4:12])
    d.Wq, d.bq, d.Wk, d.bk, d.We, d.be, d.Wv, d.bv = (given(n) for n in _INS[12:])
    d.cst, d.steps, d.tail = given('cst'), given('steps'), given('tail')
    d.out = nc.dram_tensor("out_0_dram", (z.N, D), F32, kind="ExternalOutput").ap()
    build(nc, z, d, where)
    return {f"in_{name}_dram": a for name, a in arrays.items()}


def kernel(**inputs):
    import concourse.bacc as _bacc
    from concourse.bass_utils import run_bass_kernel_spmd as _run

    nc = _bacc.Bacc("TRN2", target_bir_lowering=False, num_devices=1)
    arrays = program(nc, inputs)
    r = _run(nc, [arrays], core_ids=[0])
    return r.results[0]["out_0_dram"]
```
